# Optimizing a Trainium2 kernel written in Bass

```python
import numpy as np
import jax
import jax.numpy as jnp

def _softmax(x, axis=-1):
    return jax.nn.softmax(x, axis=axis)

def _gelu(x):
    return jax.nn.gelu(x, approximate=True)

def _silu(x):
    return jax.nn.silu(x)

def _sigmoid(x):
    return jax.nn.sigmoid(x)

def _layernorm(x, axis=-1, eps=1e-05):
    m = jnp.mean(x, axis=axis, keepdims=True)
    v = jnp.var(x, axis=axis, keepdims=True)
    return (x - m) / jnp.sqrt(v + eps)

def _scatter_add(tgt, idx, src, axis=0):
    return tgt.at[idx].add(src)

def _segment_sum(src, seg, n):
    return jax.ops.segment_sum(src, seg, n)
kernel_name = 'mk_prb_d2_jaxref_r8_2f1d19'

def setup_inputs(seed: int=0):
    np.random.seed(seed)
    _w = jnp.asarray

    def _L0_attn_setup():
        import jax, jax.numpy as jnp
        import numpy as np
        B, N, C, H, K = (4, 512, 128, 16, 2)
        D = C // H

        def _kernel(x):
            return jax.nn.silu(x) + 0.5
        key = jax.random.key(seed)
        ks = jax.random.split(key, 8)
        s = 0.02
        x = jax.random.normal(ks[0], (B, N, C), jnp.float32)
        Wq = jax.random.normal(ks[1], (C, C), jnp.float32) * s
        bq = jnp.zeros((C,), jnp.float32)
        Wk = jax.random.normal(ks[2], (K, C, C), jnp.float32) * s
        bk = jnp.zeros((K, C), jnp.float32)
        Wv = jax.random.normal(ks[3], (K, C, C), jnp.float32) * s
        bv = jnp.zeros((K, C), jnp.float32)
        Wo = jax.random.normal(ks[4], (C, C), jnp.float32) * s
        bo = jnp.zeros((C,), jnp.float32)
        ln_g = jnp.ones((C,), jnp.float32)
        ln_b = jnp.zeros((C,), jnp.float32)
        return dict(x=x, Wq=Wq, bq=bq, Wk=Wk, bk=bk, Wv=Wv, bv=bv, Wo=Wo, bo=bo, ln_g=ln_g, ln_b=ln_b)
    _L0_attn_in = _L0_attn_setup()

    def _L0_ffn_setup():
        import jax, jax.numpy as jnp
        import numpy as np
        B, S, D, E = (2, 256, 128, 8)
        key = jax.random.key(seed)
        ks = jax.random.split(key, 5)
        x = jax.random.normal(ks[0], (B, S, D), dtype=jnp.float32)
        router_w = jax.random.normal(ks[1], (E, D), dtype=jnp.float32) * 0.02
        router_b = jnp.zeros((E,), dtype=jnp.float32)
        expert_w = jax.random.normal(ks[2], (E, D, D), dtype=jnp.float32) * 0.02
        expert_b = jnp.zeros((E, D), dtype=jnp.float32)
        return {'x': x, 'router_w': router_w, 'router_b': router_b, 'expert_w': expert_w, 'expert_b': expert_b}
    _L0_ffn_in = _L0_ffn_setup()

    def _L1_attn_setup():
        import jax, jax.numpy as jnp
        import numpy as np
        D_MODEL = 128
        N_HEADS = 16
        LATENT_HEADS = 8
        LATENT_DIM = 64
        N_LATENTS = 64
        WINDOW = 32
        HEAD_DIM = D_MODEL // N_HEADS
        LAT_HD = LATENT_DIM // LATENT_HEADS
        B, S = (2, 512)

        def _pool_to_latents(x):
            Bx, Sx, C = x.shape
            chunk = max(1, Sx // N_LATENTS)
            return x.reshape(Bx, N_LATENTS, chunk, C).mean(axis=2)

        def _local_window_attn(Q, K, V):
            Bx, H, Sx, D = Q.shape
            W = WINDOW
            nb = Sx // W
            Qb = Q.reshape(Bx, H, nb, W, D)
            Kp = jnp.pad(K, ((0, 0), (0, 0), (W, 0), (0, 0))).reshape(Bx, H, nb + 1, W, D)
            Vp = jnp.pad(V, ((0, 0), (0, 0), (W, 0), (0, 0))).reshape(Bx, H, nb + 1, W, D)
            Kw = jnp.concatenate([Kp[:, :, :-1], Kp[:, :, 1:]], axis=3)
            Vw = jnp.concatenate([Vp[:, :, :-1], Vp[:, :, 1:]], axis=3)
            i = jnp.arange(W)[:, None]
            j = jnp.arange(2 * W)[None, :]
            base = (j > i) & (j <= i + W)
            blk0 = (jnp.arange(nb) > 0)[:, None, None] | (j >= W)[None, :, :]
            mask = base[None, :, :] & blk0
            sc = jnp.einsum('bhnid,bhnjd->bhnij', Qb, Kw) / np.sqrt(D).astype(np.float32)
            sc = jnp.where(mask[None, None], sc, -jnp.inf)
            p = jax.nn.softmax(sc, axis=-1)
            out = jnp.einsum('bhnij,bhnjd->bhnid', p, Vw)
            return out.reshape(Bx, H, Sx, D)
        key = jax.random.key(seed)
        ks = jax.random.split(key, 11)
        std = 0.02
        w = lambda k, shp: jax.random.normal(k, shp, jnp.float32) * std
        return {'x': jax.random.normal(ks[0], (B, S, D_MODEL), jnp.float32), 'wq': w(ks[1], (D_MODEL, D_MODEL)), 'wk': w(ks[2], (D_MODEL, D_MODEL)), 'wv': w(ks[3], (D_MODEL, D_MODEL)), 'wgq': w(ks[4], (D_MODEL, LATENT_DIM)), 'wgk': w(ks[5], (D_MODEL, LATENT_DIM)), 'wgv': w(ks[6], (D_MODEL, LATENT_DIM)), 'r_out_w': w(ks[7], (LATENT_DIM, D_MODEL)), 'gate_local_w': w(ks[8], (N_HEADS, HEAD_DIM)), 'gate_remote_w': w(ks[9], (N_HEADS, HEAD_DIM)), 'w_out': w(ks[10], (D_MODEL, D_MODEL))}
    _L1_attn_in = _L1_attn_setup()

    def _L1_ffn_setup():
        import jax, jax.numpy as jnp
        import numpy as np
        TEMPERATURE = 1.0
        TOPK = 2
        key = jax.random.key(seed)
        ks = jax.random.split(key, 6)
        S, B, H, F, E = (256, 4, 128, 512, 8)
        x = jax.random.normal(ks[0], (S, B, H), dtype=jnp.float32)
        gate_w = jax.random.normal(ks[1], (E, H), dtype=jnp.float32) * (1.0 / np.sqrt(H))
        w1 = jax.random.normal(ks[2], (E, H, F), dtype=jnp.float32) * (1.0 / np.sqrt(H))
        b1 = jnp.zeros((E, F), dtype=jnp.float32)
        w2 = jax.random.normal(ks[3], (E, F, H), dtype=jnp.float32) * (1.0 / np.sqrt(F))
        b2 = jnp.zeros((E, H), dtype=jnp.float32)
        return {'x': x, 'gate_w': gate_w, 'w1': w1, 'b1': b1, 'w2': w2, 'b2': b2}
    _L1_ffn_in = _L1_ffn_setup()
    _d = {'L0_attn_x': _L0_attn_in['x'], 'L0_attn_Wq': _L0_attn_in['Wq'], 'L0_attn_bq': _L0_attn_in['bq'], 'L0_attn_Wk': _L0_attn_in['Wk'], 'L0_attn_bk': _L0_attn_in['bk'], 'L0_attn_Wv': _L0_attn_in['Wv'], 'L0_attn_bv': _L0_attn_in['bv'], 'L0_attn_Wo': _L0_attn_in['Wo'], 'L0_attn_bo': _L0_attn_in['bo'], 'L0_attn_ln_g': _L0_attn_in['ln_g'], 'L0_attn_ln_b': _L0_attn_in['ln_b'], 'L0_ffn_router_w': _L0_ffn_in['router_w'], 'L0_ffn_router_b': _L0_ffn_in['router_b'], 'L0_ffn_expert_w': _L0_ffn_in['expert_w'], 'L0_ffn_expert_b': _L0_ffn_in['expert_b'], 'L1_attn_wq': _L1_attn_in['wq'], 'L1_attn_wk': _L1_attn_in['wk'], 'L1_attn_wv': _L1_attn_in['wv'], 'L1_attn_wgq': _L1_attn_in['wgq'], 'L1_attn_wgk': _L1_attn_in['wgk'], 'L1_attn_wgv': _L1_attn_in['wgv'], 'L1_attn_r_out_w': _L1_attn_in['r_out_w'], 'L1_attn_gate_local_w': _L1_attn_in['gate_local_w'], 'L1_attn_gate_remote_w': _L1_attn_in['gate_remote_w'], 'L1_attn_w_out': _L1_attn_in['w_out'], 'L1_ffn_gate_w': _L1_ffn_in['gate_w'], 'L1_ffn_w1': _L1_ffn_in['w1'], 'L1_ffn_b1': _L1_ffn_in['b1'], 'L1_ffn_w2': _L1_ffn_in['w2'], 'L1_ffn_b2': _L1_ffn_in['b2']}
    _x0 = _d['L0_attn_x']
    _d['L0_attn_x'] = jax.random.normal(jax.random.fold_in(jax.random.key(seed), 1), (8, 512, 128), dtype=_x0.dtype)
    del _x0
    return _d

def reference(L0_attn_x, L0_attn_Wq, L0_attn_bq, L0_attn_Wk, L0_attn_bk, L0_attn_Wv, L0_attn_bv, L0_attn_Wo, L0_attn_bo, L0_attn_ln_g, L0_attn_ln_b, L0_ffn_router_w, L0_ffn_router_b, L0_ffn_expert_w, L0_ffn_expert_b, L1_attn_wq, L1_attn_wk, L1_attn_wv, L1_attn_wgq, L1_attn_wgk, L1_attn_wgv, L1_attn_r_out_w, L1_attn_gate_local_w, L1_attn_gate_remote_w, L1_attn_w_out, L1_ffn_gate_w, L1_ffn_w1, L1_ffn_b1, L1_ffn_w2, L1_ffn_b2):

    def _L0_attn_ref(x, Wq, bq, Wk, bk, Wv, bv, Wo, bo, ln_g, ln_b):
        import jax, jax.numpy as jnp
        import numpy as np
        B, N, C, H, K = (4, 512, 128, 16, 2)
        D = C // H

        def _kernel(x):
            return jax.nn.silu(x) + 0.5
        dtype = x.dtype
        Bn, Nn, Cn = x.shape
        q = x + x @ Wq.T + bq
        ks = x[None] + jnp.einsum('bnc,kdc->kbnd', x, Wk) + bk[:, None, None, :]
        vs = x[None] + jnp.einsum('bnc,kdc->kbnd', x, Wv) + bv[:, None, None, :]
        q = q.reshape(Bn, Nn, H, D).transpose(0, 2, 1, 3)
        ks = ks.reshape(K, Bn, Nn, H, D).transpose(0, 1, 3, 2, 4)
        vs = vs.reshape(K, Bn, Nn, H, D).transpose(0, 1, 3, 2, 4)
        q = _kernel(q)
        ks = _kernel(ks)
        q = q / (jnp.linalg.norm(q, axis=-1, keepdims=True) + 1e-06)
        ks = ks / (jnp.linalg.norm(ks, axis=-1, keepdims=True) + 1e-06)
        scale = Nn ** (-0.5)
        ks = ks.astype(jnp.float32) * scale
        vs = vs.astype(jnp.float32) * scale
        states = jnp.einsum('kbhnd,kbhne->kbhde', ks, vs)
        state = jnp.prod(states, axis=0)
        out = jnp.einsum('bhnd,bhde->bhne', q.astype(jnp.float32), state)
        out = out.astype(dtype)
        out = out.transpose(0, 2, 1, 3).reshape(Bn, Nn, Cn)
        mu = out.mean(axis=-1, keepdims=True)
        var = out.var(axis=-1, keepdims=True)
        out = (out - mu) * jax.lax.rsqrt(var + 1e-05) * ln_g + ln_b
        out = out @ Wo.T + bo
        return out

    def _L0_ffn_ref(x, router_w, router_b, expert_w, expert_b):
        import jax, jax.numpy as jnp
        import numpy as np
        B, S, D, E = (2, 256, 128, 8)
        logits = jnp.einsum('bsd,ed->bse', x, router_w) + router_b
        probs = jax.nn.softmax(logits, axis=-1)
        weights = jnp.max(probs, axis=-1)
        top1 = jnp.argmax(probs, axis=-1)
        y_all = jnp.einsum('bsd,eod->bseo', x, expert_w) + expert_b
        y = jnp.take_along_axis(y_all, top1[:, :, None, None], axis=2)[:, :, 0, :]
        out = y * weights[:, :, None]
        return out

    def _L1_attn_ref(x, wq, wk, wv, wgq, wgk, wgv, r_out_w, gate_local_w, gate_remote_w, w_out):
        import jax, jax.numpy as jnp
        import numpy as np
        D_MODEL = 128
        N_HEADS = 16
        LATENT_HEADS = 8
        LATENT_DIM = 64
        N_LATENTS = 64
        WINDOW = 32
        HEAD_DIM = D_MODEL // N_HEADS
        LAT_HD = LATENT_DIM // LATENT_HEADS
        B, S = (2, 512)

        def _pool_to_latents(x):
            Bx, Sx, C = x.shape
            chunk = max(1, Sx // N_LATENTS)
            return x.reshape(Bx, N_LATENTS, chunk, C).mean(axis=2)

        def _local_window_attn(Q, K, V):
            Bx, H, Sx, D = Q.shape
            W = WINDOW
            nb = Sx // W
            Qb = Q.reshape(Bx, H, nb, W, D)
            Kp = jnp.pad(K, ((0, 0), (0, 0), (W, 0), (0, 0))).reshape(Bx, H, nb + 1, W, D)
            Vp = jnp.pad(V, ((0, 0), (0, 0), (W, 0), (0, 0))).reshape(Bx, H, nb + 1, W, D)
            Kw = jnp.concatenate([Kp[:, :, :-1], Kp[:, :, 1:]], axis=3)
            Vw = jnp.concatenate([Vp[:, :, :-1], Vp[:, :, 1:]], axis=3)
            i = jnp.arange(W)[:, None]
            j = jnp.arange(2 * W)[None, :]
            base = (j > i) & (j <= i + W)
            blk0 = (jnp.arange(nb) > 0)[:, None, None] | (j >= W)[None, :, :]
            mask = base[None, :, :] & blk0
            sc = jnp.einsum('bhnid,bhnjd->bhnij', Qb, Kw) / np.sqrt(D).astype(np.float32)
            sc = jnp.where(mask[None, None], sc, -jnp.inf)
            p = jax.nn.softmax(sc, axis=-1)
            out = jnp.einsum('bhnij,bhnjd->bhnid', p, Vw)
            return out.reshape(Bx, H, Sx, D)
        Bx, Sx, _ = x.shape
        chunk = max(1, Sx // N_LATENTS)
        Q = (x @ wq).reshape(Bx, Sx, N_HEADS, HEAD_DIM).transpose(0, 2, 1, 3)
        K = (x @ wk).reshape(Bx, Sx, N_HEADS, HEAD_DIM).transpose(0, 2, 1, 3)
        V = (x @ wv).reshape(Bx, Sx, N_HEADS, HEAD_DIM).transpose(0, 2, 1, 3)
        local = _local_window_attn(Q, K, V)
        GQ = (x @ wgq).reshape(Bx, Sx, LATENT_HEADS, LAT_HD).transpose(0, 2, 1, 3)
        GK = _pool_to_latents(x @ wgk).reshape(Bx, N_LATENTS, LATENT_HEADS, LAT_HD).transpose(0, 2, 1, 3)
        GV = _pool_to_latents(x @ wgv).reshape(Bx, N_LATENTS, LATENT_HEADS, LAT_HD).transpose(0, 2, 1, 3)
        lsc = jnp.einsum('bhsd,bhnd->bhsn', GQ, GK) / np.sqrt(LAT_HD).astype(np.float32)
        lmask = jnp.arange(N_LATENTS)[None, :] <= (jnp.arange(Sx) // chunk)[:, None]
        lsc = jnp.where(lmask[None, None], lsc, -jnp.inf)
        lp = jax.nn.softmax(lsc, axis=-1)
        rem = jnp.einsum('bhsn,bhnd->bhsd', lp, GV)
        rem = rem.transpose(0, 2, 1, 3).reshape(Bx, Sx, LATENT_DIM) @ r_out_w
        rem = rem.reshape(Bx, Sx, N_HEADS, HEAD_DIM).transpose(0, 2, 1, 3)
        gl = jax.nn.sigmoid(jnp.einsum('bhsd,hd->bhs', Q, gate_local_w))[..., None]
        gr = jax.nn.sigmoid(jnp.einsum('bhsd,hd->bhs', Q, gate_remote_w))[..., None]
        out = gl * local + gr * rem
        out = out.transpose(0, 2, 1, 3).reshape(Bx, Sx, D_MODEL)
        return out @ w_out

    def _L1_ffn_ref(x, gate_w, w1, b1, w2, b2):
        import jax, jax.numpy as jnp
        import numpy as np
        TEMPERATURE = 1.0
        TOPK = 2
        s, b, h = x.shape
        x_flat = x.reshape(s * b, h)
        logits = x_flat @ gate_w.T
        probs = jax.nn.softmax(logits / TEMPERATURE, axis=-1)
        topk_probs, topk_idx = jax.lax.top_k(probs, TOPK)
        hidden = jax.nn.relu(jnp.einsum('th,ehf->tef', x_flat, w1) + b1[None])
        all_out = jnp.einsum('tef,efh->teh', hidden, w2) + b2[None]
        gathered = jnp.take_along_axis(all_out, topk_idx[:, :, None], axis=1)
        y_flat = jnp.sum(gathered * topk_probs[:, :, None], axis=1)
        return y_flat.reshape(s, b, h)
    x = L0_attn_x
    xn = _layernorm(x, axis=-1)
    x = x + _L0_attn_ref(xn, L0_attn_Wq, L0_attn_bq, L0_attn_Wk, L0_attn_bk, L0_attn_Wv, L0_attn_bv, L0_attn_Wo, L0_attn_bo, L0_attn_ln_g, L0_attn_ln_b) + _L0_ffn_ref(xn, L0_ffn_router_w, L0_ffn_router_b, L0_ffn_expert_w, L0_ffn_expert_b)
    xn = _layernorm(x, axis=-1)
    x = x + _L1_attn_ref(xn, L1_attn_wq, L1_attn_wk, L1_attn_wv, L1_attn_wgq, L1_attn_wgk, L1_attn_wgv, L1_attn_r_out_w, L1_attn_gate_local_w, L1_attn_gate_remote_w, L1_attn_w_out) + _L1_ffn_ref(xn, L1_ffn_gate_w, L1_ffn_w1, L1_ffn_b1, L1_ffn_w2, L1_ffn_b2)
    return x

_drawn_inputs = setup_inputs


def setup_inputs(seed=0):
    import zlib

    import numpy as np

    out = dict(_drawn_inputs(seed))
    spreads = {'L0_attn_bq': (0.0, 0.1),
     'L0_attn_bk': (0.0, 0.1),
     'L0_attn_bv': (0.0, 0.1),
     'L0_attn_bo': (0.0, 0.1),
     'L0_attn_ln_g': (1.0, 0.2),
     'L0_attn_ln_b': (0.0, 0.1),
     'L0_ffn_router_b': (0.0, 0.1),
     'L0_ffn_expert_b': (0.0, 0.1),
     'L1_ffn_b1': (0.0, 0.269),
     'L1_ffn_b2': (0.0, 0.286)}
    factors = {'L0_attn_Wk': 2.975,
     'L1_attn_wq': 8.0,
     'L1_attn_wk': 8.0,
     'L1_attn_wv': 8.0,
     'L1_attn_wgq': 8.0,
     'L1_attn_wgk': 8.0,
     'L1_attn_wgv': 8.0,
     'L1_attn_r_out_w': 8.0,
     'L1_attn_gate_local_w': 8.0,
     'L1_attn_gate_remote_w': 8.0,
     'L1_attn_w_out': 8.0}
    for name, (base, spread) in spreads.items():
        noise = np.random.default_rng([zlib.crc32(name.encode()), seed]).standard_normal(out[name].shape)
        drawn = base * np.exp(spread * noise) if base else spread * noise
        out[name] = jnp.asarray(drawn.astype(out[name].dtype))
    for name, factor in factors.items():
        out[name] = (out[name] * factor).astype(out[name].dtype)
    return out
```

```python
from contextlib import ExitStack

import concourse.bass as bass
from concourse import mybir

F32 = mybir.dt.float32
BF16 = mybir.dt.bfloat16
I32 = mybir.dt.int32
ALU = mybir.AluOpType
ACT = mybir.ActivationFunctionType
AX = mybir.AxisListType.X

P = 128
EPS = 1e-5
NEG = -1e30
BAD_ROW = 1 << 20


class Chain:

    def __init__(self, eng, sem):
        self.eng, self.sem, self.n = eng, sem, 0

    def after(self, ins):
        ins.then_inc(self.sem, 1)
        self.n += 1

    def sync(self):
        self.eng.wait_ge(self.sem, self.n)

    def link(self, ins):
        self.after(ins)
        self.sync()

    def restart(self):
        self.sync()
        self.eng.sem_clear(self.sem)
        self.n = 0


def build(nc, d, out, sorted0, sorted1, ydram):
    B, S, C = d["L0_attn_x"].shape
    E = d["L0_ffn_router_w"].shape[0]
    F = d["L1_ffn_w1"].shape[2]
    NK = d["L0_attn_Wk"].shape[0]
    LAT = d["L1_attn_wgq"].shape[1]
    H, LH, HD, W, NL = 16, 8, 8, 32, 64
    T = S // P
    NT = B * T
    FC = F // P
    ROW = C + 2
    NT0 = sorted0.shape[0] // P
    NT1 = sorted1.shape[0] // P
    NB = S // W
    G = 4
    HB = NB // 2
    SCORE = float(HD) ** -0.5
    assert C == P and NK == 2 and B % 2 == 0

    x_v = d["L0_attn_x"].rearrange("b (t p) c -> p (b t) c", p=P)
    out_v = out.rearrange("b (t p) c -> p (b t) c", p=P)
    y_v = ydram.rearrange("(k n p) c -> p k n c", p=P, k=2)

    ctx = ExitStack()
    with ctx:
        def sb(name, shape, dt=F32):
            return ctx.enter_context(nc.sbuf_tensor(name, shape, dt))

        def sem(name):
            return ctx.enter_context(nc.semaphore(name))

        x_all = sb("x_all", [P, NT, C])
        xr_all = sb("xr_all", [P, NT, ROW])
        xnT_all = sb("xnT_all", [C, NT * P])
        w1 = sb("w1", [C, E, F])
        w2 = sb("w2", [P, E * FC, C])
        b1_bc = sb("b1_bc", [P, E, F])
        b2_bc = sb("b2_bc", [P, E, C])
        mix0 = sb("mix0", [P, 2 * E * C])
        eb_bc = mix0[:, 0:E * C].rearrange("p (e c) -> p e c", e=E)
        weT = mix0[:, E * C:2 * E * C].rearrange("p (e c) -> p e c", e=E)
        pre_row = sb("pre_row", [P, ROW])[:, :]
        ident = sb("ident", [P, P])
        onesb = sb("onesb", [P, 512], BF16)
        lower = sb("lower", [P, P], BF16)
        block1 = sb("block1", [P, H])
        bmask = sb("bmask", [P, H, HD])
        head_m = sb("head_m", [P, G])
        gk_m = sb("gk_m", [64, H])
        row_m = sb("row_m", [P, G])
        pick = sb("pick", [P, W])
        selq = sb("selq", [P, G, W], BF16)
        selr = sb("selr", [P, P], BF16)
        lmask = sb("lmask", [P, 2, 2, 2 * W], BF16)
        gmask = sb("gmask", [P, T, NL], BF16)
        wqT = sb("wqT", [C, C])
        wkT = sb("wkT", [C, NK * C])
        wvT = sb("wvT", [C, NK, C])
        wog = sb("wog", [C, C])
        woT = sb("woT", [C, C])
        rwT = sb("rwT", [C, 2, E])
        bo_bc = sb("bo_bc", [P, C])
        bv_bc = sb("bv_bc", [P, NK, C])
        rb_bc = sb("rb_bc", [P, E])
        lng = sb("lng", [C, 1])
        lnb = sb("lnb", [C, 1])
        bo_row = sb("bo_row", [1, C])
        brow = sb("brow", [1, 3 * C])
        bres = sb("bres", [1, 3 * C])
        bparts = sb("bparts", [1, 3, 3 * C], BF16)
        b3 = sb("b3", [3, 3 * C], BF16)
        wq1 = sb("wq1", [C, C])
        wk1 = sb("wk1", [C, C])
        wv1 = sb("wv1", [C, C])
        wgq = sb("wgq", [C, LAT])
        wgk = sb("wgk", [C, LAT])
        wgv = sb("wgv", [C, LAT])
        rout = sb("rout", [LAT, C])
        wout = sb("wout", [C, C])
        glr = sb("glr", [P, 2, C])
        wgate = sb("wgate", [C, 2, H, HD])
        wg16 = sb("wg16", [C, 2, H])
        lg = sb("lg", [P, NT, E])
        ex = sb("ex", [P, NT, E])
        ra = sb("ra", [P, NT, E])
        rc = sb("rc", [P, NT, E])
        rd = sb("rd", [P, NT, E])
        m1 = sb("m1", [P, NT, E])
        m2 = sb("m2", [P, NT, E])
        mb = sb("mb", [P, NT, E], BF16)
        top = sb("top", [P, NT])
        tie = sb("tie", [P, NT])
        den = sb("den", [P, NT])
        gate = sb("gate", [P, 2, NT])
        slotf = sb("slotf", [P, NT])
        slot = sb("slot", [P, 2, NT], I32)
        desc = sb("desc", [P, E])
        big_t = sb("big_t", [P, NT])
        kidx = sb("kidx", [P, NT1])
        cmp_ = sb("cmp_", [P, NT1 * E])
        cnt = sb("cnt", [P, E])
        ends = sb("ends", [P, E])
        endb = sb("endb", [P, E])
        kexp = sb("kexp", [P, NT1])
        expert = sb("expert", [P, 2, NT1], I32)
        st_all = sb("st_all", [P, NT, 6])
        mean = sb("mean", [P, NT])
        nq = sb("nq", [P, NT])
        st4 = sb("st4", [P, T, 6])
        mv4 = sb("mv4", [P, T, 2])
        rstd = sb("rstd", [P, NT])
        arena = sb("arena", [P, 16300])
        at = [0]

        def start_views(n=0):
            at[0] = n

        def view(n, parts=P, dt=F32):
            a = arena[0:parts, at[0]:at[0] + n]
            at[0] += n
            assert at[0] <= 16300, at[0]
            return a if dt == F32 else a.bitcast(dt)

        psum = ctx.enter_context(nc.psum_tensor("psum", [P, 8, 512], F32))

        s_x = sem("s_x")
        s_w = sem("s_w")
        s_w2 = sem("s_w2")
        s_w3 = sem("s_w3")
        s_b3 = sem("s_b3")
        s_const = sem("s_const")
        s_pool = sem("s_pool")
        s_pre = [sem(f"s_pre{n}") for n in range(2)]
        s_chain = sem("s_chain")
        s_achain = sem("s_achain")
        s_tr = sem("s_tr")
        s_trc = sem("s_trc")
        s_split = sem("s_split")
        s_phase = sem("s_phase")
        s_xn = sem("s_xn")
        s_tp = sem("s_tp")
        s_xT = sem("s_xT")
        s_lg = sem("s_lg")
        s_cp = sem("s_cp")
        s_stat = sem("s_stat")
        s_root = sem("s_root")
        s_rt = sem("s_rt")
        s_rex = sem("s_rex")
        s_rps = sem("s_rps")
        s_slot = sem("s_slot")
        s_sc = sem("s_sc")
        s_bo = sem("s_bo")
        s_out = sem("s_out")

        s_alone = {e: sem(f"s_alone_{e}") for e in ("pe", "pool", "sp")}

        def alone(eng, name):
            eng.sem_inc(s_alone[name], 1)

        def phase_end(eng, n):
            eng.drain().then_inc(s_phase, 1)
            eng.wait_ge(s_phase, 3 * n)

        start_views()
        raw = view(6 * C).rearrange("p (n c) -> p n c", n=6)
        raw_e = view(E * C).rearrange("p (n c) -> p n c", n=E)
        raw_r = view(2 * C, parts=E).rearrange("p (n c) -> p n c", n=2)
        N_W = 14

        def load_list(eng, sem_, pairs):
            for dst, src in pairs:
                eng.dma_start(dst, src).then_inc(sem_, 16)

        def setup_loads(sp):
            for b in range(B):
                sp.dma_start(x_all[:, b * T:(b + 1) * T, :], x_v[:, b * T:(b + 1) * T, :]).then_inc(s_x, 16)
            load_list(sp, s_w, [
                (raw[:, 0, :], d["L0_attn_Wq"]),
                (raw[:, 1:3, :], d["L0_attn_Wk"].rearrange("k o c -> o k c")),
                (raw[:, 3:5, :], d["L0_attn_Wv"].rearrange("k o c -> o k c")),
                (raw[:, 5, :], d["L0_attn_Wo"]),
                (raw_r[:, 0, :], d["L0_ffn_router_w"]),
                (raw_r[:, 1, :], d["L1_ffn_gate_w"]),
                (raw_e, d["L0_ffn_expert_w"].rearrange("e o c -> o e c")),
                (lng[:, :], d["L0_attn_ln_g"].rearrange("(c o) -> c o", o=1)),
                (lnb[:, :], d["L0_attn_ln_b"].rearrange("(c o) -> c o", o=1)),
                (bo_row[:, :], d["L0_attn_bo"].rearrange("(o c) -> o c", o=1)),
                (brow[:, 0:C], d["L0_attn_bq"].rearrange("(o c) -> o c", o=1)),
                (brow[:, C:3 * C], d["L0_attn_bk"].rearrange("(o k) c -> o (k c)", o=1)),
                (bv_bc[:, :, :], d["L0_attn_bv"].partition_broadcast(P)),
                (rb_bc[:, :], d["L0_ffn_router_b"].partition_broadcast(P))])

        N_W2 = 11

        def late_loads(sp):
            def prefill(dst, sem_):
                v = dst.rearrange("(n p) c -> p n c", p=P)
                sp.dma_start(v, pre_row.unsqueeze(1).to_broadcast([P, dst.shape[0] // P, ROW])).then_inc(sem_, 16)

            load_list(sp, s_w2, [
                (glr[:, 0, :], d["L1_attn_gate_local_w"].rearrange("h e -> (h e)").partition_broadcast(P)),
                (glr[:, 1, :], d["L1_attn_gate_remote_w"].rearrange("h e -> (h e)").partition_broadcast(P)),
                (wq1[:, :], d["L1_attn_wq"]),
                (wk1[:, :], d["L1_attn_wk"]),
                (wv1[:, :], d["L1_attn_wv"]),
                (wgq[:, :], d["L1_attn_wgq"]),
                (wgk[:, :], d["L1_attn_wgk"]),
                (wgv[:, :], d["L1_attn_wgv"]),
                (rout[:, :], d["L1_attn_r_out_w"]),
                (wout[:, :], d["L1_attn_w_out"]),
                (eb_bc[:, :, :], d["L0_ffn_expert_b"].partition_broadcast(P))])
            sp.wait_ge(s_const, 2)
            prefill(sorted0, s_pre[0])
            load_list(sp, s_w3, [
                (w1[:, :, :], d["L1_ffn_w1"].rearrange("e h f -> h e f")),
                (w2[:, :, :], d["L1_ffn_w2"].rearrange("e (j f) h -> f (e j) h", f=P)),
                (b1_bc[:, :, :], d["L1_ffn_b1"].partition_broadcast(P)),
                (b2_bc[:, :, :], d["L1_ffn_b2"].partition_broadcast(P))])
            prefill(sorted1, s_pre[1])


        def setup_pool(g):
            ch = Chain(g, s_pool)
            ch.after(g.memset(ident[:, :], 0.0))
            ch.after(g.memset(onesb[:, :], 1.0))
            ch.after(g.memset(pre_row, 0.0))
            ch.after(g.memset(block1[:, :], 1.0))
            ch.after(g.memset(bmask[:, :, :], float(S) ** -2))
            ch.after(g.memset(row_m[:, :], 1.0))
            ch.after(g.memset(pick[:, :], 0.0))
            ch.after(g.memset(selq[:, :, :], 0.0))
            ch.after(g.memset(selr[:, :], 1.0))
            ch.after(g.memset(lmask[:, :, :, :], 0.0))
            ch.after(g.memset(gmask[:, :, :], 0.0))
            ch.after(g.memset(xr_all[:, :, C:C + 1], 1.0))
            ch.after(g.iota(xr_all[:, :, C + 1:C + 2].bitcast(I32), pattern=[[P, NT], [0, 1]], base=0,
                            channel_multiplier=1))
            ch.after(g.iota(desc[:, :], pattern=[[-1, E]], base=E, channel_multiplier=0,
                            allow_small_or_imprecise_dtypes=True))
            ch.after(g.iota(big_t[:, :], pattern=[[P, NT]], base=0, channel_multiplier=0,
                            allow_small_or_imprecise_dtypes=True))
            ch.after(g.iota(kidx[:, :], pattern=[[1, NT1]], base=0, channel_multiplier=0,
                            allow_small_or_imprecise_dtypes=True))
            ch.sync()

            def keep(view, pattern, base, mult, fill=0.0, op=ALU.is_ge):
                ch.link(g.affine_select(out=view, in_=view, compare_op=op, fill=fill, base=base, pattern=pattern,
                                        channel_multiplier=mult))

            keep(ident[:, :], [[-1, P]], 0, 1, 1.0, ALU.not_equal)
            ch.link(g.iota(pre_row[:, C + 1:C + 2].bitcast(I32), pattern=[[0, 1]], base=BAD_ROW,
                           channel_multiplier=1))
            g.memset(lower[:, :], 1.0).then_inc(s_const, 2)
            g.wait_ge(s_const, 2)
            keep(lower[:, :], [[1, P]], -1, -1)
            keep(block1[:, :], [[-HD, H]], 0, 1)
            keep(block1[:, :], [[HD, H]], HD - 1, -1)
            keep(bmask[:, :, :], [[-HD, H], [0, HD]], 0, 1)
            keep(bmask[:, :, :], [[HD, H], [0, HD]], HD - 1, -1)
            keep(row_m[:, :], [[-W, G]], 0, 1)
            keep(row_m[:, :], [[W, G]], W - 1, -1)
            for g4 in range(G):
                keep(pick[:, :], [[-1, W]], -W * g4, 1, 1.0, ALU.not_equal)
                keep(selq[:, :, :], [[0, G], [-1, W]], -W * g4, 1, 1.0, ALU.not_equal)
            keep(selr[:, :], [[1, P]], 0, -HD)
            keep(selr[:, :], [[-1, P]], HD - 1, HD)
            for g4 in range(G):
                q = lmask[W * g4:W * g4 + W, :, :, :]
                keep(q, [[0, 2], [0, 2], [1, 2 * W]], -1, -1, NEG)
                keep(q, [[0, 2], [0, 2], [-1, 2 * W]], W, 1, NEG)
                q0 = lmask[W * g4:W * g4 + W, 0, 0, :]
                keep(q0, [[1, 2 * W]], -W, 0, NEG)
            keep(gmask[:, :, :], [[P // HD, T], [-1, NL]], 0, 1, NEG)
            g.engine_nop().then_inc(s_const, 1)

        def setup_pe(pe):
            pe.wait_ge(s_const, 2)
            pe.wait_ge(s_w, 16 * N_W)
            for i in range(4):
                pe.transpose(psum[:, 0, i * C:(i + 1) * C], raw[:, i, :], ident[:, :])
            for i in range(2):
                mm = pe.transpose(psum[:, 1, i * C:(i + 1) * C], raw[:, 4 + i, :], ident[:, :])
            for i in range(2):
                mm = pe.transpose(psum[:, 1, 2 * C + i * E:2 * C + (i + 1) * E], raw_r[:, i, :], ident[0:E, 0:E])
            mm.then_inc(s_tr, 1)
            for e in range(E):
                mm = pe.transpose(psum[:, 2 + e // 4, (e % 4) * C:(e % 4 + 1) * C], raw_e[:, e, :], ident[:, :])
            mm.then_inc(s_tr, 1)
            pe.wait_ge(s_trc, 1)
            pe.matmul(psum[:, 4, 0:C], lnb[:, 0:1].to_broadcast([C, P]), woT[:, :], start=True, stop=False)
            pe.wait_ge(s_split, 1)
            pe.matmul(psum[:, 4, 0:C], ones_row, bo_row[:, :], start=False, stop=True).then_inc(s_tr, 1)

        ones_row = arena[0:1, 8000:8000 + P]

        def setup_dve(v):
            ch = Chain(v, s_chain)
            v.memset(ones_row, 1.0).then_inc(s_split, 1)
            v.wait_ge(s_w, 16 * N_W)
            ch.link(v.tensor_copy(bparts[:, 0, :], brow[:, :]))
            ch.link(v.tensor_tensor(bres[:, :], brow[:, :], bparts[:, 0, :], ALU.subtract))
            ch.link(v.tensor_copy(bparts[:, 1, :], bres[:, :]))
            ch.link(v.tensor_tensor(bres[:, :], bres[:, :], bparts[:, 1, :], ALU.subtract))
            v.tensor_copy(bparts[:, 2, :], bres[:, :]).then_inc(s_split, 1)
            v.wait_ge(s_tr, 1)
            ch.after(v.tensor_tensor(wqT[:, :], psum[:, 0, 0:C], ident[:, :], ALU.add))
            ch.after(v.tensor_tensor(wkT[:, :].rearrange("p (k c) -> p k c", k=NK),
                                     psum[:, 0, C:3 * C].rearrange("p (k c) -> p k c", k=NK),
                                     ident[:, :].unsqueeze(1).to_broadcast([P, NK, C]), ALU.add))
            ch.after(v.tensor_tensor(wvT[:, 0, :], psum[:, 0, 3 * C:4 * C], ident[:, :], ALU.add))
            ch.after(v.tensor_tensor(wvT[:, 1, :], psum[:, 1, 0:C], ident[:, :], ALU.add))
            ch.after(v.tensor_copy(rwT[:, :, :].rearrange("p a e -> p (a e)"), psum[:, 1, 2 * C:2 * C + 2 * E]))
            ch.after(v.tensor_scalar(wog[:, :], psum[:, 1, C:2 * C], lng[:, 0:1], None, ALU.mult))
            v.tensor_copy(woT[:, :], psum[:, 1, C:2 * C]).then_inc(s_trc, 1)
            ch.sync()
            v.wait_ge(s_tr, 2)
            ch.after(v.tensor_copy(weT[:, :, :].rearrange("p e c -> p (e c)"),
                                   psum[:, 2:4, :].rearrange("p a c -> p (a c)")))
            v.wait_ge(s_tr, 3)
            v.tensor_copy(bo_bc[:, :], psum[:, 4, 0:C]).then_inc(s_bo, 1)
            ch.restart()

        def layer1_dve(v):
            ch = Chain(v, s_chain)
            v.wait_ge(s_w2, 16 * N_W2)
            v.wait_ge(s_const, 3)
            ch.link(v.tensor_reduce(head_m[:, :], block1[:, :].rearrange("p (g h) -> p h g", g=G), AX, ALU.add))
            ch.after(v.tensor_scalar(head_m[:, :], head_m[:, :], SCORE, None, ALU.mult))
            ch.after(v.tensor_scalar(gk_m[:, :], block1[0:64, :], SCORE, None, ALU.mult))
            ch.after(v.tensor_scalar(wgk[:, :], wgk[:, :], NL / S, None, ALU.mult))
            ch.after(v.tensor_scalar(wgv[:, :], wgv[:, :], NL / S, None, ALU.mult))
            ch.after(v.tensor_scalar(wout[:, :], wout[:, :], 0.5, None, ALU.mult))
            ch.link(v.tensor_tensor(glr[:, :, :], glr[:, :, :], wq1[:, :].unsqueeze(1).to_broadcast([C, 2, C]),
                                    ALU.mult))
            ch.link(v.tensor_reduce(wg16[:, :, :], glr[:, :, :].rearrange("p a (h e) -> p a h e", e=HD), AX,
                                    ALU.add))
            ch.after(v.tensor_copy(wgate[:, :, :, :], wg16[:, :, :].unsqueeze(3).to_broadcast([C, 2, H, HD])))
            ch.restart()

        start_views(8200)
        xns = [view(T * C).rearrange("p (t c) -> p t c", t=T) for _ in range(2)]
        xns_T = [view(T * P) for _ in range(2)]
        yl = [view(T * C).rearrange("p (t c) -> p t c", t=T) for _ in range(2)]
        s_yl = [sem(f"s_yl{r}") for r in range(2)]
        s_yu = sem("s_yu")

        def norm_dve_stats(v, layer):
            ch = Chain(v, s_chain)
            with v.Fori(0, B // 2) as i:
                for r in range(2):
                    b = i * 2 + r
                    t0 = b * T
                    if layer:
                        v.wait_ge(s_yl[r], 16 * (i + 1))
                        for t in range(T):
                            xt = x_all[:, bass.ds(t0 + t, 1), :].rearrange("p a c -> p (a c)")
                            g1 = gate[:, 0, bass.ds(t0 + t, 1)]
                            ch.after(v.scalar_tensor_tensor(out=xt, in0=yl[r][:, t, :], scalar=g1, in1=xt,
                                                            op0=ALU.mult, op1=ALU.add))
                        ch.sync()
                        v.sem_inc(s_yu, 1)
                    for t in range(T):
                        xt = x_all[:, bass.ds(t0 + t, 1), :].rearrange("p a c -> p (a c)")
                        ch.after(v.bn_stats(st_all[:, bass.ds(t0 + t, 1), :].rearrange("p a c -> p (a c)"), xt))
                    ch.restart()
            me, qe, mo, qo = (st_all[:, :, k] for k in (1, 2, 4, 5))
            ch.after(v.tensor_tensor(mean[:, :], me, mo, ALU.add))
            ch.after(v.tensor_tensor(rstd[:, :], me, mo, ALU.subtract))
            ch.link(v.tensor_tensor(nq[:, :], qe, qo, ALU.add))
            ch.link(v.tensor_tensor(rstd[:, :], rstd[:, :], rstd[:, :], ALU.mult))
            ch.after(v.tensor_scalar(mean[:, :], mean[:, :], 0.5, None, ALU.mult))
            ch.link(v.scalar_tensor_tensor(out=rstd[:, :], in0=rstd[:, :], scalar=C / 4.0, in1=nq[:, :],
                                           op0=ALU.mult, op1=ALU.add))
            v.tensor_scalar(rstd[:, :], rstd[:, :], 1.0 / C, EPS, ALU.mult, ALU.add).then_inc(s_stat, 1)
            ch.restart()
            v.wait_ge(s_root, layer + 1)
            ch.link(v.reciprocal(rstd[:, :], rstd[:, :]))
            ch.restart()

        def norm_dve_rows(v, layer):
            with v.Fori(0, B // 2) as i:
                for r in range(2):
                    b = i * 2 + r
                    k = B * layer + b
                    t0 = b * T
                    v.wait_ge(s_tp, k + 1)
                    v.wait_ge(s_cp, k + 1)
                    for t in range(T):
                        xt = x_all[:, bass.ds(t0 + t, 1), :].rearrange("p a c -> p (a c)")
                        ins = v.tensor_scalar(xns[r][:, t, :], xt, mean[:, bass.ds(t0 + t, 1)],
                                              rstd[:, bass.ds(t0 + t, 1)], ALU.subtract, ALU.mult)
                    ins.then_inc(s_xn, 1)
                for r in range(2):
                    b = i * 2 + r
                    k = B * layer + b
                    v.wait_ge(s_xn, k + 1)
                    v.tensor_copy(xr_all[:, bass.ds(b * T, T), 0:C], xns[r]).then_inc(s_cp, 1)
                for r in range(2):
                    b = i * 2 + r
                    v.wait_ge(s_lg, B * layer + b + 3)
                    o = lg[:, bass.ds(b * T, T), :]
                    src = psum[:, 2 + r, 0:T * E].rearrange("p (t e) -> p t e", t=T)
                    if layer:
                        v.tensor_copy(o, src).then_inc(s_lgu, 1)
                    else:
                        v.tensor_tensor(o, src, rb_bc[:, :].unsqueeze(1).to_broadcast([P, T, E]),
                                        ALU.add).then_inc(s_lgu, 1)

        s_lgu = sem("s_lgu")
        s_xT2 = sem("s_xT2")

        def norm_pe(pe, layer):
            with pe.Fori(0, B // 2) as i:
                for r in range(2):
                    b = i * 2 + r
                    k = B * layer + b
                    pe.wait_ge(s_xn, k + 1)
                    pe.wait_ge(s_xT2, k + 1)
                    for t in range(T):
                        mm = pe.transpose(psum[:, r, t * P:(t + 1) * P], xns[r][:, t, :], ident[:, :])
                    mm.then_inc(s_tp, 1)
                    pe.wait_ge(s_xT, k + 1)
                    pe.wait_ge(s_lgu, k + 1)
                    for t in range(T):
                        mm = pe.matmul(psum[:, 2 + r, t * E:(t + 1) * E], xns_T[r][:, t * P:(t + 1) * P],
                                       rwT[:, layer, :], start=True, stop=True)
                    mm.then_inc(s_lg, 1)

        def norm_act_root(act, layer):
            act.wait_ge(s_stat, layer + 1)
            act.activation(rstd[:, :], rstd[:, :], ACT.Sqrt).then_inc(s_root, 1)

        def norm_act(act, layer):
            with act.Fori(0, B // 2) as i:
                for r in range(2):
                    b = i * 2 + r
                    k = B * layer + b
                    act.wait_ge(s_tp, k + 3)
                    act.wait_ge(s_lg, k + 1)
                    act.activation(xns_T[r], psum[:, r, :], ACT.Copy).then_inc(s_xT, 1)
                    act.activation(xnT_all[:, bass.ds(b * S, S)], psum[:, r, :], ACT.Copy).then_inc(s_xT2, 1)

        def bc_e(a):
            return a.unsqueeze(2).to_broadcast([P, NT, E])

        def routing_dve(v, layer):
            ch = Chain(v, s_chain)
            nt = NT1 if layer else NT0
            for r in range(2):
                v.wait_ge(s_lgu, B * (layer + 1) + 2)
            ch.link(v.tensor_reduce(top[:, :], lg[:, :, :], AX, ALU.max))
            ch.after(v.tensor_tensor(ra[:, :, :], lg[:, :, :], bc_e(top[:, :]), ALU.subtract))
            ch.sync()
            v.engine_nop().then_inc(s_rt, 1)

            def first_of(dst, src, peak):
                ch.link(v.tensor_tensor(rc[:, :, :], src, bc_e(peak), ALU.is_equal))
                ch.link(v.tensor_tensor(rc[:, :, :], rc[:, :, :],
                                        desc[:, :].unsqueeze(1).to_broadcast([P, NT, E]), ALU.mult))
                ch.link(v.tensor_reduce(tie[:, :], rc[:, :, :], AX, ALU.max))
                ch.link(v.tensor_tensor(dst, rc[:, :, :], bc_e(tie[:, :]), ALU.is_equal))

            first_of(m1[:, :, :], lg[:, :, :], top[:, :])
            mask = m1
            if layer:
                ch.link(v.tensor_scalar(rd[:, :, :], m1[:, :, :], NEG, None, ALU.mult))
                ch.link(v.tensor_tensor(rd[:, :, :], rd[:, :, :], lg[:, :, :], ALU.add))
                ch.link(v.tensor_reduce(top[:, :], rd[:, :, :], AX, ALU.max))
                first_of(m2[:, :, :], rd[:, :, :], top[:, :])
                ch.link(v.tensor_tensor(mb[:, :, :], m1[:, :, :], m2[:, :, :], ALU.add))
            else:
                ch.link(v.tensor_copy(mb[:, :, :], mask[:, :, :]))
            v.engine_nop().then_inc(s_rt, 1)
            v.wait_ge(s_rex, layer + 1)
            ch.link(v.tensor_reduce(den[:, :], ex[:, :, :], AX, ALU.add))
            ch.link(v.reciprocal(gate[:, 0, :], den[:, :]))
            if layer:
                ch.link(v.tensor_tensor(rc[:, :, :], ex[:, :, :], m2[:, :, :], ALU.mult))
                ch.link(v.tensor_reduce(tie[:, :], rc[:, :, :], AX, ALU.add))
                ch.link(v.tensor_tensor(gate[:, 1, :], tie[:, :], gate[:, 0, :], ALU.mult))
            v.wait_ge(s_rps, layer + 1)
            tot = psum[:, 5, 0:NT * E].rearrange("p (t e) -> p t e", t=NT)
            before = psum[:, 4, 0:NT * E].rearrange("p (t e) -> p t e", t=NT)
            ch.link(v.tensor_copy(ra[:, :, :], tot))
            src, dst = ra, rc
            step = 1
            while step < NT:
                ch.after(v.tensor_copy(dst[:, 0:step, :], src[:, 0:step, :]))
                ch.link(v.tensor_tensor(dst[:, step:NT, :], src[:, step:NT, :], src[:, 0:NT - step, :], ALU.add))
                src, dst = dst, src
                step *= 2
            ch.link(v.tensor_copy(cnt[:, :], src[:, NT - 1, :]))
            ch.link(v.tensor_tensor(rd[:, :, :], src[:, :, :], tot, ALU.subtract))
            ch.link(v.tensor_tensor(rd[:, :, :], rd[:, :, :], before, ALU.add))
            c3 = cmp_[:, 0:E * NT].rearrange("p (e t) -> p e t", e=E)
            ch.link(v.tensor_tensor(c3, cnt[:, :].unsqueeze(2).to_broadcast([P, E, NT]),
                                    big_t[:, :].unsqueeze(1).to_broadcast([P, E, NT]), ALU.is_gt))
            ch.link(v.tensor_reduce(cnt[:, :], c3, AX, ALU.add))
            src2, dst2 = ends, endb
            ch.link(v.tensor_copy(src2[:, :], cnt[:, :]))
            step = 1
            while step < E:
                ch.after(v.tensor_copy(dst2[:, 0:step], src2[:, 0:step]))
                ch.link(v.tensor_tensor(dst2[:, step:E], src2[:, step:E], src2[:, 0:E - step], ALU.add))
                src2, dst2 = dst2, src2
                step *= 2
            ch.link(v.tensor_tensor(dst2[:, :], src2[:, :], cnt[:, :], ALU.subtract))
            ch.link(v.tensor_scalar(dst2[:, :], dst2[:, :], float(P), None, ALU.mult))
            ch.link(v.tensor_tensor(rd[:, :, :], rd[:, :, :], dst2[:, :].unsqueeze(1).to_broadcast([P, NT, E]),
                                    ALU.add))
            for c, m in ((0, m1), (1, m2))[:layer + 1]:
                ch.link(v.tensor_tensor(rc[:, :, :], rd[:, :, :], m[:, :, :], ALU.mult))
                ch.link(v.tensor_reduce(slotf[:, :], rc[:, :, :], AX, ALU.add))
                ch.link(v.tensor_copy(slot[:, c, :], slotf[:, :]))
            c4 = cmp_[:, 0:nt * E].rearrange("p (k e) -> p k e", e=E)
            ch.link(v.tensor_tensor(c4, kidx[:, 0:nt].unsqueeze(2).to_broadcast([P, nt, E]),
                                    src2[:, :].unsqueeze(1).to_broadcast([P, nt, E]), ALU.is_ge))
            ch.link(v.tensor_reduce(kexp[:, 0:nt], c4, AX, ALU.add))
            ch.link(v.tensor_scalar(expert[:, layer, 0:nt], kexp[:, 0:nt], float(E - 1), None, ALU.min))
            ch.restart()
            v.engine_nop().then_inc(s_slot, 1)

        def routing_act(act, layer):
            act.wait_ge(s_rt, 2 * layer + 1)
            act.activation(ex[:, :, :], ra[:, :, :], ACT.Exp).then_inc(s_rex, 1)

        def routing_pe(pe, layer):
            pe.wait_ge(s_rt, 2 * layer + 2)
            m = mb[:, :, :].rearrange("p t e -> p (t e)")
            pe.matmul(psum[:, 4, 0:NT * E], lower[:, :], m, start=True, stop=True)
            pe.matmul(psum[:, 5, 0:NT * E], onesb[:, 0:P], m, start=True, stop=True).then_inc(s_rps, 1)

        def scatter_pool(g, layer, choice, dst):
            g.wait_ge(s_slot, layer + 1)
            g.wait_ge(s_cp, B * (layer + 1) + 2)
            g.wait_ge(s_pre[layer], 16)
            for t in range(NT):
                g.indirect_dma_start(out=dst, out_offset=bass.IndirectOffsetOnAxis(ap=slot[:, choice, t:t + 1], axis=0),
                                     in_=xr_all[:, t, :], in_offset=None, bounds_check=dst.shape[0] - 1,
                                     oob_is_err=False).then_inc(s_sc, 16)

        start_views()
        a_xT = [view(S) for _ in range(2)]
        a_tq = view(S)
        a_uq = view(S)
        a_zq = [view(S) for _ in range(2)]
        a_sq = [view(S) for _ in range(2)]
        a_tk = view(2 * S)
        a_uk = view(2 * S)
        a_k2 = view(2 * S)
        a_kh = [view(2 * S).rearrange("p (t k c) -> p t k c", t=T, k=NK) for _ in range(2)]
        NG = C + 1
        a_G = view(2 * NG).rearrange("p (k c) -> p k c", k=NK)
        a_GT = view(2 * C).rearrange("p (k c) -> p k c", k=NK)
        a_s = view(2 * C).rearrange("p (k c) -> p k c", k=NK)
        a_bd = [view(C) for _ in range(2)]
        a_o = view(S).rearrange("p (t c) -> p t c", t=T)
        a_on = view(S).rearrange("p (t c) -> p t c", t=T)
        a_oT = view(S)
        NKN = T * NK * H
        NQN = T * H
        NN = NKN + NQN + T
        a_nn = view(NN)
        a_nr = view(NN)
        a_rq = [view(NQN) for _ in range(2)]
        a_rl = view(T)
        a_ld = [sem(f"a_ld{r}") for r in range(2)]
        (a_q, a_tqr, a_qu, a_zqr, a_sqr, a_nsq, a_k, a_tkr, a_ku, a_ukr, a_k2r, a_nnr, a_nrr, a_khr, a_g, a_gs,
         a_gt, a_gts, a_st, a_su, a_bdr, a_out, a_onr, a_oTp, a_oTs, a_wo, a_xu) = (
            sem(n) for n in ("a_q a_tqr a_qu a_zqr a_sqr a_nsq a_k a_tkr a_ku a_ukr a_k2r a_nnr a_nrr a_khr a_g "
                             "a_gs a_gt a_gts a_st a_su a_bdr a_out a_onr a_oTp a_oTs a_wo a_xu").split())

        def attn0_loads(sp):
            sp.wait_ge(s_phase, 6)
            for b in range(B):
                if b >= 2:
                    sp.wait_ge(a_k, b - 1)
                sp.dma_start(a_xT[b % 2], xnT_all[:, b * S:(b + 1) * S]).then_inc(a_ld[b % 2], 16)

        def attn0_pe(pe, cur, nxt):
            if cur:
                i, r = cur
                b = i * 2 + r
                pe.wait_ge(a_khr, b + 1)
                for k in range(NK):
                    for t in range(T):
                        mm = pe.matmul(psum[:, 3, k * NG:(k + 1) * NG], a_kh[r][:, t, k, :],
                                       xr_all[:, bass.ds(b * T + t, 1), 0:NG].rearrange("p a c -> p (a c)"),
                                       start=(t == 0), stop=(t == T - 1))
                mm.then_inc(a_g, 1)
            if nxt:
                ni, nr = nxt
                nb = ni * 2 + nr
                pe.wait_ge(a_ld[nr], 16 * (ni + 1))
                pe.wait_ge(a_qu, nb + 1)
                pe.matmul(psum[:, 0, :], b3[:, 0:C], onesb[0:3, :], start=True, stop=False)
                pe.matmul(psum[:, 0, :], wqT[:, :], a_xT[nr], start=False, stop=True).then_inc(a_q, 1)
            if cur:
                pe.wait_ge(a_gs, b + 1)
                pe.wait_ge(a_su, b + 1)
                for k in range(NK):
                    mm = pe.transpose(psum[:, 4, k * C:(k + 1) * C], a_G[:, k, 0:C], ident[:, :])
                mm.then_inc(a_gt, 1)
            if nxt:
                pe.wait_ge(a_ku, nb + 1)
                for t in range(T):
                    o = psum[:, 1 + t // 2, (t % 2) * 2 * C:(t % 2 + 1) * 2 * C]
                    pe.matmul(o, onesb[0:3, 0:P], b3[:, C:3 * C], start=True, stop=False)
                    mm = pe.matmul(o, a_xT[nr][:, t * P:(t + 1) * P], wkT[:, :], start=False, stop=True)
                mm.then_inc(a_k, 1)
            if cur:
                pe.wait_ge(a_gts, b + 1)
                for k in range(NK):
                    mm = pe.matmul(psum[:, 4, 2 * C + k * C:2 * C + (k + 1) * C], a_GT[:, k, :], wvT[:, k, :],
                                   start=True, stop=True)
                mm.then_inc(a_st, 1)
            if nxt:
                pe.wait_ge(a_sqr, nb + 1)
                for t in range(T):
                    mm = pe.matmul(psum[:, 6, t * H:(t + 1) * H], a_sq[nr][:, t * P:(t + 1) * P], block1[:, :],
                                   start=True, stop=True)
                mm.then_inc(a_nsq, 1)
            if cur:
                pe.wait_ge(a_bdr, b + 1)
                pe.wait_ge(a_xu, b + 1)
                for t in range(T):
                    mm = pe.matmul(psum[:, 5, t * C:(t + 1) * C], a_zq[r][:, t * P:(t + 1) * P], a_bd[r],
                                   start=True, stop=True)
                mm.then_inc(a_out, 1)
                pe.wait_ge(a_onr, b + 1)
                for t in range(T):
                    mm = pe.transpose(psum[:, 7, t * P:(t + 1) * P], a_on[:, t, :], ident[:, :])
                mm.then_inc(a_oTp, 1)
                pe.wait_ge(a_oTs, b + 1)
                for t in range(T):
                    mm = pe.matmul(psum[:, 5, t * C:(t + 1) * C], a_oT[:, t * P:(t + 1) * P], wog[:, :],
                                   start=True, stop=True)
                mm.then_inc(a_wo, 1)

        def attn0_act(act, cur, nxt):
            if cur:
                i, r = cur
                b = i * 2 + r
                act.wait_ge(a_g, b + 1)
                act.activation(a_G.rearrange("p k c -> p (k c)"), psum[:, 3, 0:2 * NG], ACT.Copy).then_inc(a_gs, 1)
            if nxt:
                ni, nr = nxt
                nb = ni * 2 + nr
                act.wait_ge(a_q, nb + 1)
                act.wait_ge(a_qu, nb + 1)
                act.activation(a_tq, psum[:, 0, :], ACT.Tanh, scale=0.5).then_inc(a_tqr, 1)
            if cur:
                act.wait_ge(a_gt, b + 1)
                act.activation(a_GT.rearrange("p k c -> p (k c)"), psum[:, 4, 0:2 * C], ACT.Copy).then_inc(a_gts, 1)
            if nxt:
                act.wait_ge(a_k, nb + 1)
                act.wait_ge(a_ku, nb + 1)
                act.activation(a_tk, psum[:, 1:3, :].rearrange("p a c -> p (a c)"), ACT.Tanh,
                               scale=0.5).then_inc(a_tkr, 1)
                act.wait_ge(a_zqr, nb + 1)
                act.activation(a_sq[nr], a_zq[nr], ACT.Square).then_inc(a_sqr, 1)
                act.wait_ge(a_ukr, nb + 1)
                act.activation(a_k2, a_uk, ACT.Square, bias=1.0).then_inc(a_k2r, 1)
            lo = 0 if nxt else NKN + NQN
            hi = NN if cur else NKN + NQN
            act.wait_ge(a_nnr, nb + 1 if nxt else b + 2)
            act.activation(a_nr[:, lo:hi], a_nn[:, lo:hi], ACT.Sqrt).then_inc(a_nrr, 1)
            if cur:
                act.wait_ge(a_oTp, b + 1)
                act.activation(a_oT, psum[:, 7, :], ACT.Copy).then_inc(a_oTs, 1)

        def attn0_dve(v, cur, nxt):
            ch = Chain(v, s_chain)
            if cur:
                i, r = cur
                b = i * 2 + r
                v.wait_ge(a_st, b + 1)
                for k in range(NK):
                    ins = v.scalar_tensor_tensor(out=a_s[:, k, :], in0=bv_bc[:, k, :], scalar=a_G[:, k, C:C + 1],
                                                 in1=psum[:, 4, 2 * C + k * C:2 * C + (k + 1) * C],
                                                 op0=ALU.mult, op1=ALU.add)
                    ch.after(ins)
                ch.sync()
                ch.link(v.tensor_tensor(a_s[:, 0, :], a_s[:, 0, :], a_s[:, 1, :], ALU.mult))
                v.tensor_tensor(a_bd[r], a_s[:, 0, :], bmask[:, :, :].rearrange("p h e -> p (h e)"),
                                ALU.mult).then_inc(a_bdr, 1)
                v.engine_nop().then_inc(a_su, 1)
            if nxt:
                ni, nr = nxt
                nb = ni * 2 + nr
                v.wait_ge(a_tqr, nb + 1)
                ch.link(v.scalar_tensor_tensor(out=a_uq, in0=a_tq, scalar=1.0, in1=psum[:, 0, :], op0=ALU.add,
                                               op1=ALU.mult))
                v.engine_nop().then_inc(a_qu, 1)
                v.tensor_scalar(a_zq[nr], a_uq, 1.0, None, ALU.add).then_inc(a_zqr, 1)
                v.wait_ge(a_tkr, nb + 1)
                v.scalar_tensor_tensor(out=a_uk, in0=a_tk, scalar=1.0,
                                       in1=psum[:, 1:3, :].rearrange("p a c -> p (a c)"), op0=ALU.add,
                                       op1=ALU.mult).then_inc(a_ukr, 1)
                v.wait_ge(a_ukr, nb + 1)
                v.sem_inc(a_ku, 1)
            if cur:
                v.wait_ge(a_out, b + 1)
                ch.link(v.tensor_tensor(a_o.rearrange("p t (h e) -> p (t h) e", e=HD),
                                        psum[:, 5, :].rearrange("p (h e) -> p h e", e=HD),
                                        a_rq[r].unsqueeze(2).to_broadcast([P, T * H, HD]), ALU.mult))
                for t in range(T):
                    ch.after(v.bn_stats(st4[:, t, :], a_o[:, t, :]))
                ch.sync()
                for t in range(T):
                    ch.after(v.bn_aggr(mv4[:, t, :], st4[:, t, :]))
                ch.sync()
                ch.after(v.tensor_scalar(a_nn[:, NKN + NQN:NN], mv4[:, :, 1], EPS, None, ALU.add))
            if nxt:
                v.wait_ge(a_k2r, nb + 1)
                ch.after(v.tensor_reduce(a_nn[:, 0:NKN], a_k2.rearrange("p (n e) -> p n e", e=HD), AX, ALU.add))
                v.wait_ge(a_nsq, nb + 1)
                ch.after(v.tensor_copy(a_nn[:, NKN:NKN + NQN], psum[:, 6, 0:NQN]))
            ch.sync()
            v.engine_nop().then_inc(a_nnr, 1)
            v.wait_ge(a_nrr, nb + 1 if nxt else b + 2)
            if nxt:
                ch.link(v.tensor_scalar(a_nr[:, 0:NKN + NQN], a_nr[:, 0:NKN + NQN], 2e-6, None, ALU.add))
                ch.after(v.reciprocal(a_nn[:, 0:NKN], a_nr[:, 0:NKN]))
                ch.after(v.reciprocal(a_rq[nr], a_nr[:, NKN:NKN + NQN]))
            if cur:
                ch.link(v.reciprocal(a_rl, a_nr[:, NKN + NQN:NN]))
                for t in range(T):
                    ins = v.tensor_scalar(a_on[:, t, :], a_o[:, t, :], mv4[:, t, 0:1], a_rl[:, t:t + 1],
                                          ALU.subtract, ALU.mult)
                ins.then_inc(a_onr, 1)
            ch.sync()
            if nxt:
                v.scalar_tensor_tensor(out=a_kh[nr].rearrange("p t k (h e) -> p (t k h) e", e=HD),
                                       in0=a_uk.rearrange("p (n e) -> p n e", e=HD), scalar=1.0,
                                       in1=a_nn[:, 0:NKN].unsqueeze(2).to_broadcast([P, NKN, HD]), op0=ALU.add,
                                       op1=ALU.mult).then_inc(a_khr, 1)
            if nxt:
                v.wait_ge(a_khr, nb + 1)
            if cur:
                v.wait_ge(a_wo, b + 1)
                xb = x_all[:, bass.ds(b * T, T), :]
                ch.link(v.tensor_tensor(xb, xb, psum[:, 5, :].rearrange("p (t c) -> p t c", t=T), ALU.add))
                v.engine_nop().then_inc(a_xu, 1)
            ch.restart()

        def attn0(eng, stage):
            stage(eng, None, (0, 0))
            with eng.Fori(0, B // 2 - 1) as i:
                stage(eng, (i, 0), (i, 1))
                stage(eng, (i, 1), (i + 1, 0))
            last = B // 2 - 1
            stage(eng, (last, 0), (last, 1))
            stage(eng, (last, 1), None)

        def bias_pool(g):
            g.wait_ge(s_bo, 1)
            g.wait_ge(s_phase, 6)
            with g.Fori(0, B) as b:
                xb = x_all[:, bass.ds(b * T, T), :]
                g.tensor_tensor(xb, xb, bo_bc[:, :].unsqueeze(1).to_broadcast([P, T, C]), ALU.add).then_inc(s_bo, 1)

        start_views()
        RING = 8
        f_x = [view(ROW) for _ in range(RING)]
        f_y = [view(C) for _ in range(RING)]
        f_xT = [view(P) for _ in range(2)]
        f_h = [view(F) for _ in range(2)]
        f_hT = [view(F) for _ in range(2)]
        ffn_sems = []
        for layer in range(2):
            q = {n: sem(f"f{layer}_{n}") for n in ("xTp", "xT", "hp", "h", "hTp", "hT", "yp", "y")}
            q["ld"] = [sem(f"f{layer}_ld{r}") for r in range(RING)]
            q["sc"] = [sem(f"f{layer}_sc{r}") for r in range(RING)]
            ffn_sems.append(q)

        def steps(eng, layer, lead, lag, step):
            nt = NT1 if layer else NT0
            for k in range(-lead, RING):
                step(k, 0, k)
            with eng.Fori(1, nt // RING - 1) as i:
                for r in range(RING):
                    step(i * RING + r, i, r)
            for k in range(nt - RING, nt + lag):
                step(k, nt // RING - 1, k - (nt - RING))

        def tile(layer, k, i, r, off):
            nt = NT1 if layer else NT0
            if isinstance(k, int) and not 0 <= k + off < nt:
                return None
            r += off
            return k + off, i + r // RING, r % RING

        def expert_of(eng, layer, k):
            return eng.value_load(expert[0:1, layer, bass.ds(k, 1)], min_val=0, max_val=E - 1)

        def ffn_sp(sp, layer, src):
            q = ffn_sems[layer]
            sv = src.rearrange("(n p) c -> p n c", p=P)

            def step(k, i, r):
                t = tile(layer, k, i, r, 0)
                if t:
                    k, n, r = t
                    if not (isinstance(n, int) and n == 0):
                        sp.wait_ge(q["sc"][r], n * 16)
                        alone(sp, "sp")
                        sp.wait_ge(q["xTp"], k - (RING - 1))
                        alone(sp, "sp")
                    sp.dma_start(f_x[r], sv[:, bass.ds(k, 1), :].rearrange("p a c -> p (a c)")).then_inc(
                        q["ld"][r], 16)

            steps(sp, layer, 0, 0, step)

        def ffn_pe(pe, layer):
            q = ffn_sems[layer]

            def step(k, i, r):
                t = tile(layer, k, i, r, 1)
                if t:
                    n, u, rr = t
                    pe.wait_ge(q["ld"][rr], (u + 1) * 16)
                    pe.transpose(psum[:, rr % 2, 0:P], f_x[rr][:, 0:C], ident[:, :]).then_inc(q["xTp"], 1)
                t = tile(layer, k, i, r, 0)
                if t:
                    n, u, rr = t
                    e = expert_of(pe, layer, n)
                    pe.wait_ge(q["xT"], n + 1)
                    if layer:
                        pe.matmul(psum[:, 2 + rr % 2, :], f_xT[rr % 2],
                                  w1[:, bass.ds(e, 1), :].rearrange("p a f -> p (a f)"),
                                  start=True, stop=True).then_inc(q["hp"], 1)
                    else:
                        if not (isinstance(n, int) and n < 2):
                            pe.wait_ge(q["y"], n - 1)
                        pe.matmul(psum[:, 6 + rr % 2, 0:C], f_xT[rr % 2],
                                  weT[:, bass.ds(e, 1), :].rearrange("p a f -> p (a f)"),
                                  start=True, stop=True).then_inc(q["yp"], 1)
                if not layer:
                    return
                t = tile(layer, k, i, r, -1)
                if t:
                    n, u, rr = t
                    pe.wait_ge(q["h"], n + 1)
                    for j in range(FC):
                        mm = pe.transpose(psum[:, 4 + rr % 2, j * P:(j + 1) * P], f_h[rr % 2][:, j * P:(j + 1) * P],
                                          ident[:, :])
                    mm.then_inc(q["hTp"], 1)
                t = tile(layer, k, i, r, -2)
                if t:
                    n, u, rr = t
                    e = expert_of(pe, layer, n)
                    pe.wait_ge(q["hT"], n + 1)
                    if not (isinstance(n, int) and n < 2):
                        pe.wait_ge(q["y"], n - 1)
                    for j in range(FC):
                        mm = pe.matmul(psum[:, 6 + rr % 2, 0:C], f_hT[rr % 2][:, j * P:(j + 1) * P],
                                       w2[:, bass.ds(e * FC + j, 1), :].rearrange("p a f -> p (a f)"),
                                       start=(j == 0), stop=(j == FC - 1))
                    mm.then_inc(q["yp"], 1)

            steps(pe, layer, 1, 2 * layer, step)

        def ffn_act(act, layer):
            q = ffn_sems[layer]

            def step(k, i, r):
                t = tile(layer, k, i, r, 1)
                if t:
                    n, u, rr = t
                    act.wait_ge(q["xTp"], n + 1)
                    act.activation(f_xT[rr % 2], psum[:, rr % 2, 0:P], ACT.Copy).then_inc(q["xT"], 1)
                t = tile(layer, k, i, r, -1) if layer else None
                if t:
                    n, u, rr = t
                    act.wait_ge(q["hTp"], n + 1)
                    act.activation(f_hT[rr % 2], psum[:, 4 + rr % 2, :], ACT.Relu).then_inc(q["hT"], 1)

            steps(act, layer, 1, layer, step)

        def ffn_dve(v, layer):
            q = ffn_sems[layer]
            bias2 = b2_bc if layer else eb_bc

            def step(k, i, r):
                t = tile(layer, k, i, r, 0) if layer else None
                if t:
                    n, u, rr = t
                    e = expert_of(v, layer, n)
                    v.wait_ge(q["hp"], n + 1)
                    v.tensor_tensor(f_h[rr % 2], psum[:, 2 + rr % 2, :],
                                    b1_bc[:, bass.ds(e, 1), :].rearrange("p a f -> p (a f)"),
                                    ALU.add).then_inc(q["h"], 1)
                t = tile(layer, k, i, r, -2 * layer)
                if t:
                    n, u, rr = t
                    e = expert_of(v, layer, n)
                    v.wait_ge(q["yp"], n + 1)
                    if not (isinstance(u, int) and u == 0):
                        v.wait_ge(q["sc"][rr], u * 16)
                    v.tensor_tensor(f_y[rr], psum[:, 6 + rr % 2, 0:C],
                                    bias2[:, bass.ds(e, 1), :].rearrange("p a f -> p (a f)"),
                                    ALU.add).then_inc(q["y"], 1)

            steps(v, layer, 0, 2 * layer, step)

        def ffn_pool(g, layer):
            q = ffn_sems[layer]

            def step(k, i, r):
                t = tile(layer, k, i, r, 0)
                if t:
                    n, u, rr = t
                    g.wait_ge(q["y"], n + 1)
                    alone(g, "pool")
                    g.indirect_dma_start(out=ydram, out_offset=bass.IndirectOffsetOnAxis(
                        ap=f_x[rr][:, C + 1:C + 2].bitcast(I32), axis=0), in_=f_y[rr], in_offset=None,
                        bounds_check=ydram.shape[0] - 1, oob_is_err=False).then_inc(q["sc"][rr], 16)

            steps(g, layer, 0, 0, step)

        def ffn_scattered(eng, layer):
            for r in range(RING):
                eng.wait_ge(ffn_sems[layer]["sc"][r], 16 * ((NT1 if layer else NT0) // RING))

        def y0_loads(sp):
            ffn_scattered(sp, 0)
            for b in range(B):
                if b >= 2:
                    sp.wait_ge(s_yu, b - 1)
                sp.dma_start(yl[b % 2], y_v[:, 0, b * T:(b + 1) * T, :]).then_inc(s_yl[b % 2], 16)

        start_views()
        W2 = 2 * W
        XP = W + S
        NP_ = NB // 2
        c_xT = [view(XP) for _ in range(2)]
        c_kz = view(G * XP).rearrange("p (g n) -> p g n", g=G)
        c_q = mix0[:, 0:NB * P].rearrange("p (n h q) -> p n h q", n=NB, h=G)
        c_gq = view(S)
        c_gk = view(LH * NL).rearrange("p (h n) -> p h n", h=LH)
        c_v = view(NP_ * G * 2 * (W + 1)).rearrange("p (j g b e) -> p j g b e", j=NP_, g=G, b=2)
        c_gv = view(LH * (HD + 1)).rearrange("p (j b e) -> p j b e", j=LH // 2, b=2)
        c_tl = view(S)
        c_tr = view(S)
        c_lg = view(S)
        c_sx = [view(512) for _ in range(2)]
        c_p = [view(512) for _ in range(3)]
        c_pT = [view(512) for _ in range(2)]
        c_z = [view(HB * P).rearrange("p (n g c) -> p n g c", n=HB, g=G) for _ in range(2)]
        c_rem = view(T * LAT).rearrange("p (t c) -> p t c", t=T)
        c_rT = view(S, parts=LAT)
        c_cb = view(S)
        c_xp = view(2 * NL).rearrange("p (b n) -> p b n", b=2)
        c_mx = view(8)
        c_rs = view(8)
        c_rm = view(8 * G).rearrange("p (n h) -> p n h", n=8)
        order = [n // 4 * 4 + (0, 2, 1, 3)[n % 4] for n in range(HB)]
        U = 12

        def pair(u):
            return [u // 4 * HB + order[u % 4 * 2 + k] for k in range(2)]

        ACC = 24
        slots = dict(Q=0, K=1, GQ=2, gl=3, gr=4, V0=5, V1=6, GV=7, loc0=17, loc1=21, remo=22, out=23)
        for u in range(U):
            slots[f"S{u}"] = 8 + u + (u > 8)
        c_rdy = [sem(f"c_rdy{n}") for n in range(4)]
        c_free = [sem(f"c_free{n}") for n in range(4)]
        c_prdy = [sem(f"c_prdy{n}") for n in range(2)]
        c_pfree = [sem(f"c_pfree{n}") for n in range(2)]
        c_ordy = [sem(f"c_ordy{n}") for n in range(2)]
        c_ofree = [sem(f"c_ofree{n}") for n in range(2)]
        c_ld = [sem(f"c_ld{n}") for n in range(2)]
        (c_init, c_xpr, c_qr, c_gqr, c_vr, c_gvr, c_gkr, c_tr_, c_sxr, c_pr, c_pTr, c_zr, c_remr, c_rTr, c_cbr,
         c_rmr) = (
            sem(n) for n in ("c_init c_xpr c_qr c_gqr c_vr c_gvr c_gkr c_tanh c_sxr c_pr c_pTr c_zr c_remr c_rTr "
                             "c_cbr c_rmr").split())

        def acc(name, b):
            n = slots[name]
            return psum[:, n % 4, :], c_rdy[n % 4], c_free[n % 4], b * (ACC // 4) + (n // 4 + 1)

        def pt_bank(n, b):
            return psum[:, 4 + n % 2, :], c_prdy[n % 2], c_pfree[n % 2], b * 7 + (n // 2 + 1)

        def o_bank(u, b):
            return psum[:, 6 + u % 2, :], c_ordy[u % 2], c_ofree[u % 2], b * 6 + (u // 2 + 1)

        def attn1_init(g):
            ch = Chain(g, s_pool)
            g.sem_clear(s_pool)
            g.wait_ge(s_phase, 15)
            for a in (c_xT[0], c_xT[1], c_kz[:, 0, :], c_kz[:, 1, :], c_kz[:, 2, :], c_kz[:, 3, :]):
                ch.link(g.memset(a[:, 0:W], 0.0))
            ch.link(g.memset(c_gq[LAT:P, :], 0.0))
            ch.link(g.memset(c_gk[LAT:P, :, :], 0.0))
            ch.link(g.memset(c_v, 0.0))
            ch.link(g.memset(c_v[0:64, :, :, 0, W:W + 1], 1.0))
            ch.link(g.memset(c_v[64:P, :, :, 1, W:W + 1], 1.0))
            ch.link(g.memset(c_gv, 0.0))
            ch.link(g.memset(c_gv[0:64, :, 0, HD:HD + 1], 1.0))
            ch.link(g.memset(c_gv[64:P, :, 1, HD:HD + 1], 1.0))
            g.engine_nop().then_inc(c_init, 1)

        def attn1_loads(sp):
            sp.wait_ge(c_init, 1)
            for b in range(B):
                if b >= 2:
                    _, rdy, _, n = acc("V1", b - 2)
                    sp.wait_ge(rdy, n)
                    _, rdy, _, n = acc("GV", b - 2)
                    sp.wait_ge(rdy, n)
                    sp.wait_ge(c_xpr, b - 1)
                sp.dma_start(c_xT[b % 2][:, W:XP], xnT_all[:, b * S:(b + 1) * S]).then_inc(c_ld[b % 2], 16)

        def attn1_pe(pe, b, i, r):
            xT = c_xT[r][:, W:XP]

            def begin(bank):
                o, rdy, free, n = bank
                pe.wait_ge(free, n)
                return o, rdy

            pe.wait_ge(c_ld[r], (i + 1) * 16)
            for name, w in (("Q", wq1[:, :]), ("K", wk1[:, :]), ("GQ", wgq[:, :]),
                            ("gl", wgate[:, 0, :, :].rearrange("p h e -> p (h e)")),
                            ("gr", wgate[:, 1, :, :].rearrange("p h e -> p (h e)"))):
                o, rdy = begin(acc(name, b))
                pe.matmul(o[0:LAT, :] if name == "GQ" else o, w, xT, start=True, stop=True).then_inc(rdy, 1)
            for hf in range(2):
                o, rdy = begin(acc(f"V{hf}", b))
                for j in range(NP_ // 2):
                    first = W * (hf * HB + order[2 * j])
                    mm = pe.matmul(o[:, j * C:(j + 1) * C], c_xT[r][:, first:first + 2 * W2], wv1[:, :],
                                   start=True, stop=True)
                mm.then_inc(rdy, 1)
            pe.wait_ge(c_xpr, b + 1)
            o, rdy = begin(pt_bank(0, b))
            pe.matmul(o[0:LAT, 0:NL], wgk[:, :], c_xp[:, 0, :], start=True, stop=True).then_inc(rdy, 1)
            o, rdy = begin(acc("GV", b))
            pe.matmul(o[:, 0:LAT], c_xp.rearrange("p b n -> p (b n)"), wgv[:, :], start=True,
                      stop=True).then_inc(rdy, 1)

            def scores(u):
                o, rdy = begin(acc(f"S{u}", b))
                if u < 8:
                    if u == 0:
                        pe.wait_ge(c_qr, b + 1)
                    pe.matmul(o, selq[:, :, :].rearrange("p h q -> p (h q)"),
                              lmask[:, 0 if u == 0 else 1, :, :].rearrange("p k j -> p (k j)").unsqueeze(1)
                              .to_broadcast([P, G, 2 * W2]), start=True, stop=False, skip_group_check=True)
                    ov = o.rearrange("p (g k j) -> p g k j", g=G, k=2)
                    for k in range(2):
                        n = pair(u)[k]
                        mm = pe.matmul(ov[:, :, k, :], c_q[:, n, :, :].rearrange("p h q -> p (h q)"),
                                       c_kz[:, :, n * W:n * W + W2], start=False, stop=(k == 1),
                                       skip_group_check=True)
                else:
                    t = u - 8
                    if t == 0:
                        pe.wait_ge(c_gqr, b + 1)
                        pe.wait_ge(c_gkr, b + 1)
                    pe.matmul(o, selr[:, :], gmask[:, t, :].unsqueeze(1).to_broadcast([P, LH, NL]), start=True,
                              stop=False)
                    mm = pe.matmul(o, c_gq[:, t * P:(t + 1) * P], c_gk.rearrange("p h n -> p (h n)"), start=False,
                                   stop=True)
                mm.then_inc(rdy, 1)

            def transposes(u):
                pe.wait_ge(c_pr, b * U + (u + 1))
                o, rdy = begin(pt_bank(1 + u, b))
                for j in range(4):
                    mm = pe.transpose(o[:, j * P:(j + 1) * P], c_p[u % 3][:, j * P:(j + 1) * P], ident[:, :])
                mm.then_inc(rdy, 1)

            def values(u):
                pe.wait_ge(c_pTr, b * U + (u + 1))
                if u == 0:
                    pe.wait_ge(c_vr, b + 1)
                o, rdy = begin(o_bank(u, b))
                for j in range(4):
                    w = c_pT[u % 2][:, j * P:(j + 1) * P]
                    if u < 8:
                        dst = o[:, 0:8 * (W + 1)].rearrange("p (k g e) -> p k g e", k=2, g=G)[:, :, j, :]
                        rhs = c_v[:, u, j, :, :]
                    else:
                        n = 2 * (HD + 1)
                        dst = o[:, j * n:(j + 1) * n]
                        rhs = c_gv[:, j, :, :].rearrange("p b e -> p (b e)")
                    mm = pe.matmul(dst, w, rhs, start=True, stop=True)
                mm.then_inc(rdy, 1)

            def local_out(hf):
                pe.wait_ge(c_zr, b * 8 + (4 * hf + 4))
                o, rdy = begin(acc(f"loc{hf}", b))
                for j in range(HB):
                    mm = pe.matmul(o[:, order[j] * W:(order[j] + 1) * W], c_z[hf][:, j, :, :].rearrange("p g c -> p (g c)"),
                                   pick[:, :], start=True, stop=True)
                mm.then_inc(rdy, 1)

            for s in range(U + 3):
                if s < U:
                    scores(s)
                if 0 <= s - 2 < U:
                    transposes(s - 2)
                if s >= 3:
                    values(s - 3)
                if s == 8:
                    local_out(0)
                if s == 12:
                    local_out(1)
            pe.wait_ge(c_remr, b + 1)
            o, rdy = begin(pt_bank(13, b))
            alone(pe, "pe")
            for t in range(T):
                mm = pe.transpose(o[0:LAT, t * P:(t + 1) * P], c_rem[:, t, :], ident[:, :])
            mm.then_inc(rdy, 1)
            pe.wait_ge(c_rTr, b + 1)
            o, rdy = begin(acc("remo", b))
            pe.matmul(o, rout[:, :], c_rT, start=True, stop=True).then_inc(rdy, 1)
            pe.wait_ge(c_cbr, b + 1)
            o, rdy = begin(acc("out", b))
            for t in range(T):
                mm = pe.matmul(o[:, t * C:(t + 1) * C], c_cb[:, t * P:(t + 1) * P], wout[:, :], start=True,
                               stop=True)
            mm.then_inc(rdy, 1)

        def attn1_act(act, b, i, r):
            def bank(x):
                o, rdy, free, n = x
                act.wait_ge(rdy, n)
                return o, free

            o, free = bank(acc("Q", b))
            for h in range(G):
                ins = act.activation(c_q[:, :, h, :], o.rearrange("p (n q) -> p n q", n=NB), ACT.Copy,
                                     scale=head_m[:, h:h + 1])
            ins.then_inc(free, 1)
            o, free = bank(acc("K", b))
            for g in range(G):
                ins = act.activation(c_kz[:, g, W:XP], o, ACT.Copy, scale=row_m[:, g:g + 1])
            ins.then_inc(free, 1)
            act.wait_ge(free, acc("K", b)[3] + 1)
            act.sem_inc(c_qr, 1)
            o, free = bank(acc("GQ", b))
            act.activation(c_gq[0:LAT, :], o[0:LAT, :], ACT.Copy).then_inc(free, 1)
            act.wait_ge(free, acc("GQ", b)[3] + 1)
            act.sem_inc(c_gqr, 1)
            for name, dst in (("gl", c_tl), ("gr", c_tr)):
                o, free = bank(acc(name, b))
                act.activation(dst, o, ACT.Tanh, scale=0.5).then_inc(free, 1)
            act.wait_ge(free, acc("gr", b)[3] + 1)
            act.sem_inc(c_tr_, 1)
            for hf in range(2):
                o, free = bank(acc(f"V{hf}", b))
                ov = o.rearrange("p (j g e) -> p j g e", j=4, g=G)
                for bb in range(2):
                    row = slice(64 * bb, 64 * bb + 64)
                    ins = act.activation(c_v[row, 4 * hf:4 * hf + 4, :, bb, 0:W], ov[row, :, :, :], ACT.Copy)
                ins.then_inc(free, 1)
            o, free = bank(acc("GV", b))
            ov = o[:, 0:LAT].rearrange("p (j b e) -> p j b e", j=LH // 2, b=2)
            for bb in range(2):
                row = slice(64 * bb, 64 * bb + 64)
                ins = act.activation(c_gv[row, :, bb, 0:HD], ov[row, :, bb, :], ACT.Copy)
            ins.then_inc(free, 1)
            act.wait_ge(free, acc("GV", b)[3] + 1)
            act.sem_inc(c_vr, 1)
            for s in range(U + 2):
                if s < U:
                    act.wait_ge(c_sxr, b * U + (s + 1))
                    act.activation(c_p[s % 3], c_sx[s % 2], ACT.Exp).then_inc(c_pr, 1)
                if s >= 2:
                    o, free = bank(pt_bank(1 + s - 2, b))
                    act.activation(c_pT[s % 2], o, ACT.Copy).then_inc(free, 1)
                    act.wait_ge(free, pt_bank(1 + s - 2, b)[3] + 1)
                    act.sem_inc(c_pTr, 1)
            o, free = bank(pt_bank(13, b))
            act.activation(c_rT, o[0:LAT, :], ACT.Copy).then_inc(free, 1)
            act.wait_ge(free, pt_bank(13, b)[3] + 1)
            act.sem_inc(c_rTr, 1)

        def attn1_dve(v, b, i, r):
            ch = Chain(v, s_chain)

            def bank(x):
                o, rdy, free, n = x
                v.wait_ge(rdy, n)
                return o, free

            v.wait_ge(c_ld[r], (i + 1) * 16)
            ch.link(v.tensor_reduce(c_xp[:, 0, :], c_xT[r][:, W:XP].rearrange("p (n e) -> p n e", n=NL), AX,
                                    ALU.add))
            v.tensor_copy(c_xp[:, 1, :], c_xp[:, 0, :]).then_inc(c_xpr, 1)
            o, free = bank(pt_bank(0, b))
            v.tensor_tensor(c_gk[0:LAT, :, :], o[0:LAT, 0:NL].unsqueeze(1).to_broadcast([LAT, LH, NL]),
                            gk_m[:, 0:LH].unsqueeze(2).to_broadcast([LAT, LH, NL]), ALU.mult).then_inc(free, 1)
            v.wait_ge(free, pt_bank(0, b)[3] + 1)
            v.sem_inc(c_gkr, 1)
            for s in range(U + 3):
                if s < U:
                    o, free = bank(acc(f"S{s}", b))
                    sv = o.rearrange("p (n j) -> p n j", n=8)
                    ch.after(v.tensor_reduce(c_mx, sv, AX, ALU.max))
                u = s - 3
                if u >= 0:
                    oo, ofree = bank(o_bank(u, b))
                    e = W if u < 8 else HD
                    ov = oo[:, 0:8 * (e + 1)].rearrange("p (n e) -> p n e", n=8)
                    ch.after(v.reciprocal(c_rs, ov[:, :, e]))
                ch.sync()
                if s < U:
                    if s >= 2:
                        v.wait_ge(c_pr, b * U + (s - 1))
                    v.tensor_tensor(c_sx[s % 2].rearrange("p (n j) -> p n j", n=8), sv,
                                    c_mx.unsqueeze(2).to_broadcast([P, 8, W2]), ALU.subtract).then_inc(c_sxr, 1)
                    v.wait_ge(c_sxr, b * U + (s + 1))
                    v.sem_inc(free, 1)
                if 0 <= u < 8:
                    ch.link(v.tensor_tensor(c_rm, c_rs.unsqueeze(2).to_broadcast([P, 8, G]),
                                            row_m[:, :].unsqueeze(1).to_broadcast([P, 8, G]), ALU.mult))
                    v.tensor_tensor(c_z[u // 4][:, u % 4 * 2:u % 4 * 2 + 2, :, :].rearrange("p k g (h e) -> p (k g) h e",
                                                                                            h=G),
                                    ov[:, :, 0:W].rearrange("p n (h e) -> p n h e", h=G),
                                    c_rm.unsqueeze(3).to_broadcast([P, 8, G, HD]), ALU.mult).then_inc(c_zr, 1)
                    v.wait_ge(c_zr, b * 8 + (u + 1))
                    v.sem_inc(ofree, 1)
                elif u >= 8:
                    ins = v.tensor_tensor(c_rem[:, u - 8, :].rearrange("p (h e) -> p h e", h=LH), ov[:, :, 0:HD],
                                          c_rs.unsqueeze(2).to_broadcast([P, LH, HD]), ALU.mult)
                    ins.then_inc(ofree, 1)
                    v.wait_ge(ofree, o_bank(u, b)[3] + 1)
                if s in (9, 13):
                    hf = 0 if s == 9 else 1
                    if hf == 0:
                        v.wait_ge(c_tr_, b + 1)
                    o, free = bank(acc(f"loc{hf}", b))
                    h2 = slice(hf * S // 2, (hf + 1) * S // 2)
                    v.scalar_tensor_tensor(out=c_lg[:, h2], in0=c_tl[:, h2], scalar=1.0, in1=o[:, 0:S // 2],
                                           op0=ALU.add, op1=ALU.mult).then_inc(free, 1)
            v.sem_inc(c_remr, 1)
            o, free = bank(acc("remo", b))
            v.scalar_tensor_tensor(out=c_cb, in0=c_tr, scalar=1.0, in1=o, op0=ALU.add,
                                   op1=ALU.mult).then_inc(free, 1)
            v.wait_ge(free, acc("remo", b)[3] + 1)
            v.wait_ge(c_free[slots["loc1"] % 4], acc("loc1", b)[3] + 1)
            v.tensor_tensor(c_cb, c_cb, c_lg, ALU.add).then_inc(c_cbr, 1)
            o, free = bank(acc("out", b))
            xb = x_all[:, bass.ds(b * T, T), :]
            v.tensor_tensor(xb, xb, o.rearrange("p (t c) -> p t c", t=T), ALU.add).then_inc(free, 1)
            ch.restart()

        def attn1(eng, body):
            with eng.Fori(0, B // 2) as i:
                for r in range(2):
                    body(eng, i * 2 + r, i, r)

        s_ids = sem("s_ids")

        def ids1(g):
            g.wait_ge(s_sc, 16 * NT * 2)
            g.iota(xr_all[:, :, C + 1:C + 2].bitcast(I32), pattern=[[P, NT], [0, 1]], base=NT * P,
                   channel_multiplier=1).then_inc(s_ids, 1)
            g.wait_ge(s_ids, 1)

        start_views()
        z_y = [view(2 * S).rearrange("p (k t c) -> p k t c", k=2, t=T) for _ in range(2)]
        z_ld = [sem(f"z_ld{r}") for r in range(2)]
        z_x = sem("z_x")

        def last_loads(sp):
            sp.wait_ge(s_phase, 18)
            ffn_scattered(sp, 1)
            for b in range(B):
                if b >= 2:
                    sp.wait_ge(z_x, b - 1)
                for k in range(2):
                    sp.dma_start(z_y[b % 2][:, k, :, :], y_v[:, k, b * T:(b + 1) * T, :]).then_inc(z_ld[b % 2], 16)

        def last_dve(v):
            ch = Chain(v, s_chain)
            with v.Fori(0, B // 2) as i:
                for r in range(2):
                    b = i * 2 + r
                    v.wait_ge(z_ld[r], (i + 1) * 32)
                    for k in range(2):
                        for t in range(T):
                            n = b * T + t
                            xt = x_all[:, bass.ds(n, 1), :].rearrange("p a c -> p (a c)")
                            ch.after(v.scalar_tensor_tensor(out=xt, in0=z_y[r][:, k, t, :],
                                                            scalar=gate[:, k, bass.ds(n, 1)], in1=xt,
                                                            op0=ALU.mult, op1=ALU.add))
                        ch.sync()
                    v.sem_inc(z_x, 1)
                    ch.restart()

        def last_stores(act):
            for b in range(B):
                act.wait_ge(z_x, b + 1)
                act.dma_start(out_v[:, b * T:(b + 1) * T, :], x_all[:, b * T:(b + 1) * T, :]).then_inc(s_out, 16)
            act.wait_ge(s_out, 16 * B)

        block = ctx.enter_context(nc.Block())

        @block.sync
        def _(sp):
            setup_loads(sp)
            late_loads(sp)
            sp.wait_ge(s_split, 2)
            for k in range(3):
                sp.dma_start(b3[k:k + 1, :], bparts[:, k, :]).then_inc(s_b3, 16)
            attn0_loads(sp)
            sp.wait_ge(s_phase, 9)
            sp.wait_ge(s_sc, 16 * NT)
            ffn_sp(sp, 0, sorted0)
            y0_loads(sp)
            attn1_loads(sp)
            sp.wait_ge(s_phase, 18)
            sp.wait_ge(s_sc, 16 * NT * 3)
            ffn_sp(sp, 1, sorted1)
            last_loads(sp)

        @block.gpsimd
        def _(g):
            setup_pool(g)
            bias_pool(g)
            scatter_pool(g, 0, 0, sorted0)
            g.wait_ge(s_sc, 16 * NT)
            ffn_pool(g, 0)
            attn1_init(g)
            scatter_pool(g, 1, 0, sorted1)
            ids1(g)
            scatter_pool(g, 1, 1, sorted1)
            ffn_pool(g, 1)

        @block.scalar
        def _(act):
            norm_act_root(act, 0)
            phase_end(act, 1)
            norm_act(act, 0)
            phase_end(act, 2)
            routing_act(act, 0)
            attn0(act, attn0_act)
            phase_end(act, 3)
            ffn_act(act, 0)
            phase_end(act, 4)
            norm_act_root(act, 1)
            norm_act(act, 1)
            phase_end(act, 5)
            routing_act(act, 1)
            act.wait_ge(c_init, 1)
            attn1(act, attn1_act)
            phase_end(act, 6)
            ffn_act(act, 1)
            last_stores(act)

        @block.vector
        def _(v):
            for s, n in [(s_lgu, 2), (s_tp, 2), (s_lg, 2), (s_xT2, 2), (s_cp, 2), (a_qu, 1), (a_ku, 1), (a_su, 1), (a_xu, 1)] + [
                    (q, 1) for q in c_free + c_pfree + c_ofree]:
                v.sem_inc(s, n)
            v.wait_ge(s_x, 16 * B)
            norm_dve_stats(v, 0)
            setup_dve(v)
            phase_end(v, 1)
            norm_dve_rows(v, 0)
            phase_end(v, 2)
            routing_dve(v, 0)
            layer1_dve(v)
            v.wait_ge(s_bo, 1 + B)
            attn0(v, attn0_dve)
            phase_end(v, 3)
            ffn_dve(v, 0)
            phase_end(v, 4)
            v.wait_ge(s_sc, 16 * NT)
            norm_dve_stats(v, 1)
            norm_dve_rows(v, 1)
            phase_end(v, 5)
            routing_dve(v, 1)
            v.wait_ge(c_init, 1)
            attn1(v, attn1_dve)
            phase_end(v, 6)
            v.wait_ge(s_w3, 64)
            ffn_dve(v, 1)
            last_dve(v)

        @block.tensor
        def _(pe):
            setup_pe(pe)
            phase_end(pe, 1)
            norm_pe(pe, 0)
            phase_end(pe, 2)
            pe.wait_ge(s_const, 3)
            routing_pe(pe, 0)
            pe.wait_ge(s_b3, 48)
            attn0(pe, attn0_pe)
            phase_end(pe, 3)
            ffn_pe(pe, 0)
            phase_end(pe, 4)
            norm_pe(pe, 1)
            phase_end(pe, 5)
            routing_pe(pe, 1)
            pe.wait_ge(c_init, 1)
            attn1(pe, attn1_pe)
            phase_end(pe, 6)
            pe.wait_ge(s_w3, 64)
            ffn_pe(pe, 1)


_INS = ["L0_attn_x", "L0_attn_Wq", "L0_attn_bq", "L0_attn_Wk", "L0_attn_bk", "L0_attn_Wv", "L0_attn_bv",
        "L0_attn_Wo", "L0_attn_bo", "L0_attn_ln_g", "L0_attn_ln_b", "L0_ffn_router_w", "L0_ffn_router_b",
        "L0_ffn_expert_w", "L0_ffn_expert_b", "L1_attn_wq", "L1_attn_wk", "L1_attn_wv", "L1_attn_wgq",
        "L1_attn_wgk", "L1_attn_wgv", "L1_attn_r_out_w", "L1_attn_gate_local_w", "L1_attn_gate_remote_w",
        "L1_attn_w_out", "L1_ffn_gate_w", "L1_ffn_w1", "L1_ffn_b1", "L1_ffn_w2", "L1_ffn_b2"]


def kernel(**inputs):
    import numpy as np
    import concourse.bacc as bacc
    from concourse.bass_utils import run_bass_kernel_spmd

    nc = bacc.Bacc("TRN2", target_bir_lowering=False, num_devices=1)
    arrays, d = {}, {}
    for name in _INS:
        a = np.ascontiguousarray(inputs[name])
        arrays[f"in_{name}_dram"] = a
        d[name] = nc.dram_tensor(f"in_{name}_dram", a.shape, mybir.dt.from_np(a.dtype), kind="ExternalInput").ap()
    shape = inputs["L0_attn_x"].shape
    rows = shape[0] * shape[1]
    experts = inputs["L0_ffn_router_w"].shape[0]
    out = nc.dram_tensor("out_0_dram", shape, F32, kind="ExternalOutput").ap()
    sorted0 = nc.dram_tensor("sorted0", (rows + experts * P, shape[2] + 2), F32, kind="Internal").ap()
    sorted1 = nc.dram_tensor("sorted1", (2 * rows + experts * P, shape[2] + 2), F32, kind="Internal").ap()
    ydram = nc.dram_tensor("ydram", (2 * rows, shape[2]), F32, kind="Internal").ap()
    build(nc, d, out, sorted0, sorted1, ydram)
    r = run_bass_kernel_spmd(nc, [arrays], core_ids=[0])
    return r.results[0]["out_0_dram"]
```

```python
from contextlib import ExitStack

import concourse.bass as bass
from concourse import mybir

F32 = mybir.dt.float32
BF16 = mybir.dt.bfloat16
I32 = mybir.dt.int32
ALU = mybir.AluOpType
ACT = mybir.ActivationFunctionType
AX = mybir.AxisListType.X

P = 128
EPS = 1e-5
NEG = -1e30
BAD_ROW = 1 << 20


class Chain:

    def __init__(self, eng, sem):
        self.eng, self.sem, self.n = eng, sem, 0

    def after(self, ins):
        ins.then_inc(self.sem, 1)
        self.n += 1

    def sync(self):
        self.eng.wait_ge(self.sem, self.n)

    def link(self, ins):
        self.after(ins)
        self.sync()

    def restart(self):
        self.sync()
        self.eng.sem_clear(self.sem)
        self.n = 0


def build(nc, d, out, sorted0, sorted1, ydram):
    B, S, C = d["L0_attn_x"].shape
    E = d["L0_ffn_router_w"].shape[0]
    F = d["L1_ffn_w1"].shape[2]
    NK = d["L0_attn_Wk"].shape[0]
    LAT = d["L1_attn_wgq"].shape[1]
    H, LH, HD, W, NL = 16, 8, 8, 32, 64
    T = S // P
    NT = B * T
    FC = F // P
    ROW = C + 2
    NT0 = sorted0.shape[0] // P
    NT1 = sorted1.shape[0] // P
    NB = S // W
    G = 4
    HB = NB // 2
    SCORE = float(HD) ** -0.5
    assert C == P and NK == 2 and B % 2 == 0

    x_v = d["L0_attn_x"].rearrange("b (t p) c -> p (b t) c", p=P)
    out_v = out.rearrange("b (t p) c -> p (b t) c", p=P)
    y_v = ydram.rearrange("(k n p) c -> p k n c", p=P, k=2)

    ctx = ExitStack()
    with ctx:
        def sb(name, shape, dt=F32):
            return ctx.enter_context(nc.sbuf_tensor(name, shape, dt))

        def sem(name):
            return ctx.enter_context(nc.semaphore(name))

        x_all = sb("x_all", [P, NT, C])
        xr_all = sb("xr_all", [P, NT, ROW])
        xnT_all = sb("xnT_all", [C, NT * P])
        w1 = sb("w1", [C, E, F])
        w2 = sb("w2", [P, E * FC, C])
        b1T = sb("b1T", [P, E * FC])
        b2_bc = sb("b2_bc", [P, E, C])
        mix0 = sb("mix0", [P, 2 * E * C])
        eb_bc = mix0[:, 0:E * C].rearrange("p (e c) -> p e c", e=E)
        weT = mix0[:, E * C:2 * E * C].rearrange("p (e c) -> p e c", e=E)
        pre_row = sb("pre_row", [P, ROW])[:, :]
        ident = sb("ident", [P, P])
        onesb = sb("onesb", [P, 512], BF16)
        lower = sb("lower", [P, P], BF16)
        block1 = sb("block1", [P, H])
        bmask = sb("bmask", [P, H, HD])
        head_m = sb("head_m", [P, G])
        gk_m = sb("gk_m", [64, H])
        row_m = sb("row_m", [P, G])
        pick = sb("pick", [P, W])
        selq = sb("selq", [P, G, W], BF16)
        selr = sb("selr", [P, P], BF16)
        lmask = sb("lmask", [P, 2, 2, 2 * W], BF16)
        gmask = sb("gmask", [P, T, NL], BF16)
        wqT = sb("wqT", [C, C])
        wkT = sb("wkT", [C, NK * C])
        wvT = sb("wvT", [C, NK, C])
        wog = sb("wog", [C, C])
        woT = sb("woT", [C, C])
        rwT = sb("rwT", [C, 2, E])
        bo_bc = sb("bo_bc", [P, C])
        bv_bc = sb("bv_bc", [P, NK, C])
        rb_bc = sb("rb_bc", [P, E])
        lng = sb("lng", [C, 1])
        lnb = sb("lnb", [C, 1])
        bo_row = sb("bo_row", [1, C])
        bparts = sb("bparts", [1, 3, 3 * C], BF16)
        b3 = sb("b3", [3, 3 * C], BF16)
        wq1 = sb("wq1", [C, C])
        wk1 = sb("wk1", [C, C])
        wv1 = sb("wv1", [C, C])
        wgq = sb("wgq", [C, LAT])
        wgk = sb("wgk", [C, LAT])
        wgv = sb("wgv", [C, LAT])
        rout = sb("rout", [LAT, C])
        wout = sb("wout", [C, C])
        glr = sb("glr", [P, 2, C])
        wgate = sb("wgate", [C, 2, H, HD])
        wg16 = sb("wg16", [C, 2, H])
        lg = sb("lg", [P, NT, E])
        ex = sb("ex", [P, NT, E])
        ra = sb("ra", [P, NT, E])
        rc = sb("rc", [P, NT, E])
        rd = sb("rd", [P, NT, E])
        m1 = sb("m1", [P, NT, E])
        m2 = sb("m2", [P, NT, E])
        mb = sb("mb", [P, NT, E], BF16)
        top = sb("top", [P, NT])
        tie = sb("tie", [P, NT])
        den = sb("den", [P, NT])
        gate = sb("gate", [P, 2, NT])
        slotf = sb("slotf", [P, NT])
        slot = sb("slot", [P, 2, NT], I32)
        desc = sb("desc", [P, E])
        big_t = sb("big_t", [P, NT])
        kidx = sb("kidx", [P, NT1])
        cmp_ = sb("cmp_", [P, NT1 * E])
        cnt = sb("cnt", [P, E])
        ends = sb("ends", [P, E])
        endb = sb("endb", [P, E])
        kexp = sb("kexp", [P, NT1])
        expert = sb("expert", [P, 2, NT1], I32)
        st_all = sb("st_all", [P, NT, 6])
        mean = sb("mean", [P, NT])
        nq = sb("nq", [P, NT])
        st4 = sb("st4", [P, T, 6])
        mv4 = sb("mv4", [P, T, 2])
        rstd = sb("rstd", [P, NT])
        arena = sb("arena", [P, 20620])
        at = [0]

        def start_views(n=0):
            at[0] = n

        def view(n, parts=P, dt=F32):
            a = arena[0:parts, at[0]:at[0] + n]
            at[0] += n
            assert at[0] <= 20620, at[0]
            return a if dt == F32 else a.bitcast(dt)

        psum = ctx.enter_context(nc.psum_tensor("psum", [P, 8, 512], F32))

        s_x = sem("s_x")
        s_w = sem("s_w")
        s_w2 = sem("s_w2")
        s_w3 = sem("s_w3")
        s_b3 = sem("s_b3")
        s_const = sem("s_const")
        s_pool = sem("s_pool")
        s_pre = [sem(f"s_pre{n}") for n in range(2)]
        s_chain = sem("s_chain")
        s_achain = sem("s_achain")
        s_tr = sem("s_tr")
        s_trc = sem("s_trc")
        s_split = sem("s_split")
        s_phase = sem("s_phase")
        s_xn = sem("s_xn")
        s_tp = sem("s_tp")
        s_xT = sem("s_xT")
        s_lg = sem("s_lg")
        s_cp = sem("s_cp")
        s_stat = sem("s_stat")
        s_root = sem("s_root")
        s_rt = sem("s_rt")
        s_rex = sem("s_rex")
        s_rps = sem("s_rps")
        s_slot = sem("s_slot")
        s_sc = sem("s_sc")
        s_bo = sem("s_bo")
        s_out = sem("s_out")

        s_alone = sem("s_alone")

        def alone(eng):
            eng.sem_inc(s_alone, 1)

        def phase_end(eng, n):
            eng.drain().then_inc(s_phase, 1)
            eng.wait_ge(s_phase, 3 * n)

        start_views()
        raw = view(6 * C).rearrange("p (n c) -> p n c", n=6)
        raw_e = view(E * C).rearrange("p (n c) -> p n c", n=E)
        raw_r = view(2 * C, parts=E).rearrange("p (n c) -> p n c", n=2)
        raw_b = view(P, parts=E * FC)
        brow = view(3 * C, parts=1)
        bres = view(3 * C, parts=1)
        N_W = 15

        def load_list(eng, sem_, pairs):
            for dst, src in pairs:
                eng.dma_start(dst, src).then_inc(sem_, 16)

        def setup_loads(sp):
            for b in range(B):
                sp.dma_start(x_all[:, b * T:(b + 1) * T, :], x_v[:, b * T:(b + 1) * T, :]).then_inc(s_x, 16)
            load_list(sp, s_w, [
                (raw[:, 0, :], d["L0_attn_Wq"]),
                (raw[:, 1:3, :], d["L0_attn_Wk"].rearrange("k o c -> o k c")),
                (raw[:, 3:5, :], d["L0_attn_Wv"].rearrange("k o c -> o k c")),
                (raw[:, 5, :], d["L0_attn_Wo"]),
                (raw_r[:, 0, :], d["L0_ffn_router_w"]),
                (raw_r[:, 1, :], d["L1_ffn_gate_w"]),
                (raw_e, d["L0_ffn_expert_w"].rearrange("e o c -> o e c")),
                (raw_b, d["L1_ffn_b1"].rearrange("e (j f) -> (e j) f", f=P)),
                (lng[:, :], d["L0_attn_ln_g"].rearrange("(c o) -> c o", o=1)),
                (lnb[:, :], d["L0_attn_ln_b"].rearrange("(c o) -> c o", o=1)),
                (bo_row[:, :], d["L0_attn_bo"].rearrange("(o c) -> o c", o=1)),
                (brow[:, 0:C], d["L0_attn_bq"].rearrange("(o c) -> o c", o=1)),
                (brow[:, C:3 * C], d["L0_attn_bk"].rearrange("(o k) c -> o (k c)", o=1)),
                (bv_bc[:, :, :], d["L0_attn_bv"].partition_broadcast(P)),
                (rb_bc[:, :], d["L0_ffn_router_b"].partition_broadcast(P))])

        N_W2 = 11

        def late_loads(sp):
            def prefill(dst, sem_):
                v = dst.rearrange("(n p) c -> p n c", p=P)
                sp.dma_start(v, pre_row.unsqueeze(1).to_broadcast([P, dst.shape[0] // P, ROW])).then_inc(sem_, 16)

            load_list(sp, s_w2, [
                (glr[:, 0, :], d["L1_attn_gate_local_w"].rearrange("h e -> (h e)").partition_broadcast(P)),
                (glr[:, 1, :], d["L1_attn_gate_remote_w"].rearrange("h e -> (h e)").partition_broadcast(P)),
                (wq1[:, :], d["L1_attn_wq"]),
                (wk1[:, :], d["L1_attn_wk"]),
                (wv1[:, :], d["L1_attn_wv"]),
                (wgq[:, :], d["L1_attn_wgq"]),
                (wgk[:, :], d["L1_attn_wgk"]),
                (wgv[:, :], d["L1_attn_wgv"]),
                (rout[:, :], d["L1_attn_r_out_w"]),
                (wout[:, :], d["L1_attn_w_out"]),
                (eb_bc[:, :, :], d["L0_ffn_expert_b"].partition_broadcast(P))])
            sp.wait_ge(s_const, 2)
            prefill(sorted0, s_pre[0])
            load_list(sp, s_w3, [
                (w1[:, :, :], d["L1_ffn_w1"].rearrange("e h f -> h e f")),
                (w2[:, :, :], d["L1_ffn_w2"].rearrange("e (j f) h -> f (e j) h", f=P)),
                (b2_bc[:, :, :], d["L1_ffn_b2"].partition_broadcast(P))])
            prefill(sorted1, s_pre[1])


        def setup_pool(g):
            ch = Chain(g, s_pool)
            ch.after(g.memset(ident[:, :], 0.0))
            ch.after(g.memset(onesb[:, :], 1.0))
            ch.after(g.memset(pre_row, 0.0))
            ch.after(g.memset(block1[:, :], 1.0))
            ch.after(g.memset(bmask[:, :, :], float(S) ** -2))
            ch.after(g.memset(row_m[:, :], 1.0))
            ch.after(g.memset(pick[:, :], 0.0))
            ch.after(g.memset(selq[:, :, :], 0.0))
            ch.after(g.memset(selr[:, :], 1.0))
            ch.after(g.memset(lmask[:, :, :, :], 0.0))
            ch.after(g.memset(gmask[:, :, :], 0.0))
            ch.after(g.memset(xr_all[:, :, C:C + 1], 1.0))
            ch.after(g.iota(xr_all[:, :, C + 1:C + 2].bitcast(I32), pattern=[[P, NT], [0, 1]], base=0,
                            channel_multiplier=1))
            ch.after(g.iota(desc[:, :], pattern=[[-1, E]], base=E, channel_multiplier=0,
                            allow_small_or_imprecise_dtypes=True))
            ch.after(g.iota(big_t[:, :], pattern=[[P, NT]], base=0, channel_multiplier=0,
                            allow_small_or_imprecise_dtypes=True))
            ch.after(g.iota(kidx[:, :], pattern=[[1, NT1]], base=0, channel_multiplier=0,
                            allow_small_or_imprecise_dtypes=True))
            ch.sync()

            def keep(view, pattern, base, mult, fill=0.0, op=ALU.is_ge):
                ch.link(g.affine_select(out=view, in_=view, compare_op=op, fill=fill, base=base, pattern=pattern,
                                        channel_multiplier=mult))

            keep(ident[:, :], [[-1, P]], 0, 1, 1.0, ALU.not_equal)
            ch.link(g.iota(pre_row[:, C + 1:C + 2].bitcast(I32), pattern=[[0, 1]], base=BAD_ROW,
                           channel_multiplier=1))
            g.memset(lower[:, :], 1.0).then_inc(s_const, 2)
            g.wait_ge(s_const, 2)
            keep(lower[:, :], [[1, P]], -1, -1)
            keep(block1[:, :], [[-HD, H]], 0, 1)
            keep(block1[:, :], [[HD, H]], HD - 1, -1)
            keep(bmask[:, :, :], [[-HD, H], [0, HD]], 0, 1)
            keep(bmask[:, :, :], [[HD, H], [0, HD]], HD - 1, -1)
            keep(row_m[:, :], [[-W, G]], 0, 1)
            keep(row_m[:, :], [[W, G]], W - 1, -1)
            for g4 in range(G):
                keep(pick[:, :], [[-1, W]], -W * g4, 1, 1.0, ALU.not_equal)
                keep(selq[:, :, :], [[0, G], [-1, W]], -W * g4, 1, 1.0, ALU.not_equal)
            keep(selr[:, :], [[1, P]], 0, -HD)
            keep(selr[:, :], [[-1, P]], HD - 1, HD)
            for g4 in range(G):
                q = lmask[W * g4:W * g4 + W, :, :, :]
                keep(q, [[0, 2], [0, 2], [1, 2 * W]], -1, -1, NEG)
                keep(q, [[0, 2], [0, 2], [-1, 2 * W]], W, 1, NEG)
                q0 = lmask[W * g4:W * g4 + W, 0, 0, :]
                keep(q0, [[1, 2 * W]], -W, 0, NEG)
            keep(gmask[:, :, :], [[P // HD, T], [-1, NL]], 0, 1, NEG)
            g.engine_nop().then_inc(s_const, 1)

        def setup_pe(pe):
            pe.wait_ge(s_const, 2)
            pe.wait_ge(s_w, 16 * N_W)
            for i in range(4):
                pe.transpose(psum[:, 0, i * C:(i + 1) * C], raw[:, i, :], ident[:, :])
            for i in range(2):
                mm = pe.transpose(psum[:, 1, i * C:(i + 1) * C], raw[:, 4 + i, :], ident[:, :])
            for i in range(2):
                pe.transpose(psum[:, 1, 2 * C + i * E:2 * C + (i + 1) * E], raw_r[:, i, :], ident[0:E, 0:E])
            mm = pe.transpose(psum[:, 1, 3 * C:3 * C + E * FC], raw_b, ident[0:E * FC, 0:E * FC])
            mm.then_inc(s_tr, 1)
            for e in range(E):
                mm = pe.transpose(psum[:, 2 + e // 4, (e % 4) * C:(e % 4 + 1) * C], raw_e[:, e, :], ident[:, :])
            mm.then_inc(s_tr, 1)
            pe.wait_ge(s_trc, 1)
            pe.matmul(psum[:, 4, 0:C], lnb[:, 0:1].to_broadcast([C, P]), woT[:, :], start=True, stop=False)
            pe.wait_ge(s_split, 1)
            pe.matmul(psum[:, 4, 0:C], ones_row, bo_row[:, :], start=False, stop=True).then_inc(s_tr, 1)

        ones_row = arena[0:1, 8000:8000 + P]

        def setup_dve(v):
            ch = Chain(v, s_chain)
            v.memset(ones_row, 1.0).then_inc(s_split, 1)
            v.wait_ge(s_w, 16 * N_W)
            ch.link(v.tensor_copy(bparts[:, 0, :], brow[:, :]))
            ch.link(v.tensor_tensor(bres[:, :], brow[:, :], bparts[:, 0, :], ALU.subtract))
            ch.link(v.tensor_copy(bparts[:, 1, :], bres[:, :]))
            ch.link(v.tensor_tensor(bres[:, :], bres[:, :], bparts[:, 1, :], ALU.subtract))
            v.tensor_copy(bparts[:, 2, :], bres[:, :]).then_inc(s_split, 1)
            v.wait_ge(s_tr, 1)
            ch.after(v.tensor_tensor(wqT[:, :], psum[:, 0, 0:C], ident[:, :], ALU.add))
            ch.after(v.tensor_tensor(wkT[:, :].rearrange("p (k c) -> p k c", k=NK),
                                     psum[:, 0, C:3 * C].rearrange("p (k c) -> p k c", k=NK),
                                     ident[:, :].unsqueeze(1).to_broadcast([P, NK, C]), ALU.add))
            ch.after(v.tensor_tensor(wvT[:, 0, :], psum[:, 0, 3 * C:4 * C], ident[:, :], ALU.add))
            ch.after(v.tensor_tensor(wvT[:, 1, :], psum[:, 1, 0:C], ident[:, :], ALU.add))
            ch.after(v.tensor_copy(rwT[:, :, :].rearrange("p a e -> p (a e)"), psum[:, 1, 2 * C:2 * C + 2 * E]))
            ch.after(v.tensor_scalar(wog[:, :], psum[:, 1, C:2 * C], lng[:, 0:1], None, ALU.mult))
            ch.after(v.tensor_copy(b1T[:, :], psum[:, 1, 3 * C:3 * C + E * FC]))
            v.tensor_copy(woT[:, :], psum[:, 1, C:2 * C]).then_inc(s_trc, 1)
            ch.sync()
            v.wait_ge(s_tr, 2)
            ch.after(v.tensor_copy(weT[:, :, :].rearrange("p e c -> p (e c)"),
                                   psum[:, 2:4, :].rearrange("p a c -> p (a c)")))
            v.wait_ge(s_tr, 3)
            v.tensor_copy(bo_bc[:, :], psum[:, 4, 0:C]).then_inc(s_bo, 1)
            ch.restart()

        def layer1_dve(v):
            ch = Chain(v, s_chain)
            v.wait_ge(s_w2, 16 * N_W2)
            v.wait_ge(s_const, 3)
            ch.link(v.tensor_reduce(head_m[:, :], block1[:, :].rearrange("p (g h) -> p h g", g=G), AX, ALU.add))
            ch.after(v.tensor_scalar(head_m[:, :], head_m[:, :], SCORE, None, ALU.mult))
            ch.after(v.tensor_scalar(gk_m[:, :], block1[0:64, :], SCORE, None, ALU.mult))
            ch.after(v.tensor_scalar(wgk[:, :], wgk[:, :], NL / S, None, ALU.mult))
            ch.after(v.tensor_scalar(wgv[:, :], wgv[:, :], NL / S, None, ALU.mult))
            ch.after(v.tensor_scalar(wout[:, :], wout[:, :], 0.5, None, ALU.mult))
            ch.link(v.tensor_tensor(glr[:, :, :], glr[:, :, :], wq1[:, :].unsqueeze(1).to_broadcast([C, 2, C]),
                                    ALU.mult))
            ch.link(v.tensor_reduce(wg16[:, :, :], glr[:, :, :].rearrange("p a (h e) -> p a h e", e=HD), AX,
                                    ALU.add))
            ch.after(v.tensor_copy(wgate[:, :, :, :], wg16[:, :, :].unsqueeze(3).to_broadcast([C, 2, H, HD])))
            ch.restart()

        def batch(bt):
            return bt[0] + bt[1] * 2

        def two_deep(eng, stage):
            stage(eng, None, (0, 0))
            with eng.Fori(0, B // 2 - 1) as i:
                stage(eng, (0, i), (1, i))
                stage(eng, (1, i), (2, i))
            stage(eng, (B - 2, 0), (B - 1, 0))
            stage(eng, (B - 1, 0), None)

        start_views(8200)
        xns = [view(T * C).rearrange("p (t c) -> p t c", t=T) for _ in range(2)]
        xns_T = [view(T * P) for _ in range(2)]
        yl = [view(T * C).rearrange("p (t c) -> p t c", t=T) for _ in range(2)]
        s_yl = [sem(f"s_yl{r}") for r in range(2)]
        s_yu = sem("s_yu")

        def norm_dve_stats(v, layer):
            ch = Chain(v, s_chain)
            with v.Fori(0, B // 2) as i:
                for r in range(2):
                    b = i * 2 + r
                    t0 = b * T
                    if layer:
                        v.wait_ge(s_yl[r], 16 * (i + 1))
                        for t in range(T):
                            xt = x_all[:, bass.ds(t0 + t, 1), :].rearrange("p a c -> p (a c)")
                            g1 = gate[:, 0, bass.ds(t0 + t, 1)]
                            ch.after(v.scalar_tensor_tensor(out=xt, in0=yl[r][:, t, :], scalar=g1, in1=xt,
                                                            op0=ALU.mult, op1=ALU.add))
                        ch.sync()
                        v.sem_inc(s_yu, 1)
                    for t in range(T):
                        xt = x_all[:, bass.ds(t0 + t, 1), :].rearrange("p a c -> p (a c)")
                        ch.after(v.bn_stats(st_all[:, bass.ds(t0 + t, 1), :].rearrange("p a c -> p (a c)"), xt))
                    ch.restart()
            me, qe, mo, qo = (st_all[:, :, k] for k in (1, 2, 4, 5))
            ch.after(v.tensor_tensor(mean[:, :], me, mo, ALU.add))
            ch.after(v.tensor_tensor(rstd[:, :], me, mo, ALU.subtract))
            ch.link(v.tensor_tensor(nq[:, :], qe, qo, ALU.add))
            ch.link(v.tensor_tensor(rstd[:, :], rstd[:, :], rstd[:, :], ALU.mult))
            ch.after(v.tensor_scalar(mean[:, :], mean[:, :], 0.5, None, ALU.mult))
            ch.link(v.scalar_tensor_tensor(out=rstd[:, :], in0=rstd[:, :], scalar=C / 4.0, in1=nq[:, :],
                                           op0=ALU.mult, op1=ALU.add))
            v.tensor_scalar(rstd[:, :], rstd[:, :], 1.0 / C, EPS, ALU.mult, ALU.add).then_inc(s_stat, 1)
            ch.restart()
            v.wait_ge(s_root, layer + 1)
            ch.link(v.reciprocal(rstd[:, :], rstd[:, :]))
            ch.restart()

        def norm_dve_rows(v, layer):
            def rows(i):
                for r in range(2):
                    b = i * 2 + r
                    k = B * layer + b
                    v.wait_ge(s_tp, k + 1)
                    v.wait_ge(s_cp, k + 1)
                    for t in range(T):
                        xt = x_all[:, bass.ds(b * T + t, 1), :].rearrange("p a c -> p (a c)")
                        ins = v.tensor_scalar(xns[r][:, t, :], xt, mean[:, bass.ds(b * T + t, 1)],
                                              rstd[:, bass.ds(b * T + t, 1)], ALU.subtract, ALU.mult)
                    ins.then_inc(s_xn, 1)
                for r in range(2):
                    b = i * 2 + r
                    v.wait_ge(s_xn, B * layer + b + 1)
                    v.tensor_copy(xr_all[:, bass.ds(b * T, T), 0:C], xns[r]).then_inc(s_cp, 1)

            def logits(i):
                for r in range(2):
                    b = i * 2 + r
                    v.wait_ge(s_lg, B * layer + b + 3)
                    o = lg[:, bass.ds(b * T, T), :]
                    src = psum[:, 2 + r, 0:T * E].rearrange("p (t e) -> p t e", t=T)
                    if layer:
                        v.tensor_copy(o, src).then_inc(s_lgu, 1)
                    else:
                        v.tensor_tensor(o, src, rb_bc[:, :].unsqueeze(1).to_broadcast([P, T, E]),
                                        ALU.add).then_inc(s_lgu, 1)

            rows(0)
            with v.Fori(1, B // 2) as i:
                rows(i)
                logits(i - 1)
            logits(B // 2 - 1)

        s_lgu = sem("s_lgu")
        s_xT2 = sem("s_xT2")

        def norm_pe(pe, layer):
            def stage(pe, prev, cur):
                if cur:
                    r = cur[0] % 2
                    k = batch(cur) + B * layer
                    pe.wait_ge(s_xn, k + 1)
                    pe.wait_ge(s_xT2, k + 1)
                    for t in range(T):
                        mm = pe.transpose(psum[:, r, t * P:(t + 1) * P], xns[r][:, t, :], ident[:, :])
                    mm.then_inc(s_tp, 1)
                if prev:
                    r = prev[0] % 2
                    k = batch(prev) + B * layer
                    pe.wait_ge(s_xT, k + 1)
                    pe.wait_ge(s_lgu, k + 1)
                    for t in range(T):
                        mm = pe.matmul(psum[:, 2 + r, t * E:(t + 1) * E], xns_T[r][:, t * P:(t + 1) * P],
                                       rwT[:, layer, :], start=True, stop=True)
                    mm.then_inc(s_lg, 1)

            two_deep(pe, stage)

        def norm_act_root(act, layer):
            act.wait_ge(s_stat, layer + 1)
            act.activation(rstd[:, :], rstd[:, :], ACT.Sqrt).then_inc(s_root, 1)

        def norm_act(act, layer):
            with act.Fori(0, B // 2) as i:
                for r in range(2):
                    b = i * 2 + r
                    k = B * layer + b
                    act.wait_ge(s_tp, k + 3)
                    act.wait_ge(s_lg, k + 1)
                    act.activation(xns_T[r], psum[:, r, :], ACT.Copy).then_inc(s_xT, 1)
                    act.activation(xnT_all[:, bass.ds(b * S, S)], psum[:, r, :], ACT.Copy).then_inc(s_xT2, 1)

        def bc_e(a):
            return a.unsqueeze(2).to_broadcast([P, NT, E])

        def routing_dve(v, layer):
            ch = Chain(v, s_chain)
            nt = NT1 if layer else NT0
            for r in range(2):
                v.wait_ge(s_lgu, B * (layer + 1) + 2)
            ch.link(v.tensor_reduce(top[:, :], lg[:, :, :], AX, ALU.max))
            ch.after(v.tensor_tensor(ra[:, :, :], lg[:, :, :], bc_e(top[:, :]), ALU.subtract))
            ch.sync()
            v.engine_nop().then_inc(s_rt, 1)

            def first_of(dst, src, peak):
                ch.link(v.tensor_tensor(rc[:, :, :], src, bc_e(peak), ALU.is_equal))
                ch.link(v.tensor_tensor(rc[:, :, :], rc[:, :, :],
                                        desc[:, :].unsqueeze(1).to_broadcast([P, NT, E]), ALU.mult))
                ch.link(v.tensor_reduce(tie[:, :], rc[:, :, :], AX, ALU.max))
                ch.link(v.tensor_tensor(dst, rc[:, :, :], bc_e(tie[:, :]), ALU.is_equal))

            first_of(m1[:, :, :], lg[:, :, :], top[:, :])
            mask = m1
            if layer:
                ch.link(v.tensor_scalar(rd[:, :, :], m1[:, :, :], NEG, None, ALU.mult))
                ch.link(v.tensor_tensor(rd[:, :, :], rd[:, :, :], lg[:, :, :], ALU.add))
                ch.link(v.tensor_reduce(top[:, :], rd[:, :, :], AX, ALU.max))
                first_of(m2[:, :, :], rd[:, :, :], top[:, :])
                ch.link(v.tensor_tensor(mb[:, :, :], m1[:, :, :], m2[:, :, :], ALU.add))
            else:
                ch.link(v.tensor_copy(mb[:, :, :], mask[:, :, :]))
            v.engine_nop().then_inc(s_rt, 1)
            v.wait_ge(s_rex, layer + 1)
            ch.link(v.tensor_reduce(den[:, :], ex[:, :, :], AX, ALU.add))
            ch.link(v.reciprocal(gate[:, 0, :], den[:, :]))
            if layer:
                ch.link(v.tensor_tensor(rc[:, :, :], ex[:, :, :], m2[:, :, :], ALU.mult))
                ch.link(v.tensor_reduce(tie[:, :], rc[:, :, :], AX, ALU.add))
                ch.link(v.tensor_tensor(gate[:, 1, :], tie[:, :], gate[:, 0, :], ALU.mult))
            v.wait_ge(s_rps, layer + 1)
            tot = psum[:, 5, 0:NT * E].rearrange("p (t e) -> p t e", t=NT)
            before = psum[:, 4, 0:NT * E].rearrange("p (t e) -> p t e", t=NT)
            ch.link(v.tensor_copy(ra[:, :, :], tot))
            src, dst = ra, rc
            step = 1
            while step < NT:
                ch.after(v.tensor_copy(dst[:, 0:step, :], src[:, 0:step, :]))
                ch.link(v.tensor_tensor(dst[:, step:NT, :], src[:, step:NT, :], src[:, 0:NT - step, :], ALU.add))
                src, dst = dst, src
                step *= 2
            ch.link(v.tensor_copy(cnt[:, :], src[:, NT - 1, :]))
            ch.link(v.tensor_tensor(rd[:, :, :], src[:, :, :], tot, ALU.subtract))
            ch.link(v.tensor_tensor(rd[:, :, :], rd[:, :, :], before, ALU.add))
            v.engine_nop().then_inc(s_rt, 1)
            c3 = cmp_[:, 0:E * NT].rearrange("p (e t) -> p e t", e=E)
            ch.link(v.tensor_tensor(c3, cnt[:, :].unsqueeze(2).to_broadcast([P, E, NT]),
                                    big_t[:, :].unsqueeze(1).to_broadcast([P, E, NT]), ALU.is_gt))
            ch.link(v.tensor_reduce(cnt[:, :], c3, AX, ALU.add))
            src2, dst2 = ends, endb
            ch.link(v.tensor_copy(src2[:, :], cnt[:, :]))
            step = 1
            while step < E:
                ch.after(v.tensor_copy(dst2[:, 0:step], src2[:, 0:step]))
                ch.link(v.tensor_tensor(dst2[:, step:E], src2[:, step:E], src2[:, 0:E - step], ALU.add))
                src2, dst2 = dst2, src2
                step *= 2
            ch.link(v.tensor_tensor(dst2[:, :], src2[:, :], cnt[:, :], ALU.subtract))
            ch.link(v.tensor_scalar(dst2[:, :], dst2[:, :], float(P), None, ALU.mult))
            ch.link(v.tensor_tensor(rd[:, :, :], rd[:, :, :], dst2[:, :].unsqueeze(1).to_broadcast([P, NT, E]),
                                    ALU.add))
            for c, m in ((0, m1), (1, m2))[:layer + 1]:
                ch.link(v.tensor_tensor(rc[:, :, :], rd[:, :, :], m[:, :, :], ALU.mult))
                ch.link(v.tensor_reduce(slotf[:, :], rc[:, :, :], AX, ALU.add))
                ch.link(v.tensor_copy(slot[:, c, :], slotf[:, :]))
            c4 = cmp_[:, 0:nt * E].rearrange("p (k e) -> p k e", e=E)
            ch.link(v.tensor_tensor(c4, kidx[:, 0:nt].unsqueeze(2).to_broadcast([P, nt, E]),
                                    src2[:, :].unsqueeze(1).to_broadcast([P, nt, E]), ALU.is_ge))
            ch.link(v.tensor_reduce(kexp[:, 0:nt], c4, AX, ALU.add))
            ch.link(v.tensor_scalar(expert[:, layer, 0:nt], kexp[:, 0:nt], float(E - 1), None, ALU.min))
            ch.restart()
            v.engine_nop().then_inc(s_slot, 1)

        def routing_act(act, layer):
            act.wait_ge(s_rt, 3 * layer + 1)
            act.activation(ex[:, :, :], ra[:, :, :], ACT.Exp).then_inc(s_rex, 1)

        def routing_pe(pe, layer):
            pe.wait_ge(s_rt, 3 * layer + 2)
            m = mb[:, :, :].rearrange("p t e -> p (t e)")
            pe.matmul(psum[:, 4, 0:NT * E], lower[:, :], m, start=True, stop=True)
            pe.matmul(psum[:, 5, 0:NT * E], onesb[:, 0:P], m, start=True, stop=True).then_inc(s_rps, 1)

        def scatter_pool(g, layer, choice, dst):
            g.wait_ge(s_slot, layer + 1)
            g.wait_ge(s_cp, B * (layer + 1) + 2)
            g.wait_ge(s_pre[layer], 16)
            for t in range(NT):
                g.indirect_dma_start(out=dst, out_offset=bass.IndirectOffsetOnAxis(ap=slot[:, choice, t:t + 1], axis=0),
                                     in_=xr_all[:, t, :], in_offset=None, bounds_check=dst.shape[0] - 1,
                                     oob_is_err=False).then_inc(s_sc, 16)

        NKN = T * NK * H
        NQN = T * H
        NN = NKN + NQN
        NG = C + 1
        start_views()
        a_uk = view(B * 2 * S)
        a_zqs = view(B * S)
        a_nn = view(B * NN)
        both = at[0]
        a_xT = [view(S) for _ in range(2)]
        a_uq = [view(S) for _ in range(2)]
        a_tk = [view(2 * S) for _ in range(2)]
        a_sq = [view(S) for _ in range(2)]
        a_k2 = view(2 * S)
        start_views(both)
        a_kh = [view(2 * S).rearrange("p (t k c) -> p t k c", t=T, k=NK) for _ in range(2)]
        a_zq = [view(S) for _ in range(2)]
        a_G = [view(2 * NG).rearrange("p (k c) -> p k c", k=NK) for _ in range(2)]
        a_GT = view(2 * C).rearrange("p (k c) -> p k c", k=NK)
        a_s = view(2 * C).rearrange("p (k c) -> p k c", k=NK)
        a_bd = view(C)
        a_on = view(S).rearrange("p (t c) -> p t c", t=T)
        a_oT = view(S)
        a_w = view(S)
        a_o = [view(S).rearrange("p (t c) -> p t c", t=T) for _ in range(2)]
        small = [cmp_[:, k:k + n] for k, n in ((0, NKN), (NKN, NQN), (NKN + NQN, NQN), (NKN + 2 * NQN, T),
                                               (NKN + 2 * NQN + T, T), (NKN + 2 * NQN + 2 * T, T))]
        a_kn, a_rq, a_ve, a_rl, a_nb = small[0], small[1:3], small[3], small[4], small[5]
        a_ld = [sem(f"a_ld{r}") for r in range(2)]
        b_ld = [sem(f"b_ld{r}") for r in range(2)]
        (a_q, a_tqr, a_uqr, a_zqr, a_sqr, a_nsq, a_nsu, a_k, a_tkr, a_ukr, a_k2r, a_red, a_root, b_all) = (
            sem(n) for n in ("a_q a_tqr a_uqr a_zqr a_sqr a_nsq a_nsu a_k a_tkr a_ukr a_k2r a_red a_root "
                             "b_all").split())
        (b_kh, b_g, b_gs, b_gt, b_gts, b_st, b_bd, b_out, b_ve, b_sq, b_rl, b_on, b_oTp, b_oTs, b_wo, b_w, b_xu) = (
            sem(n) for n in ("b_kh b_g b_gs b_gt b_gts b_st b_bd b_out b_ve b_sq b_rl b_on b_oTp b_oTs b_wo "
                             "b_w b_xu").split())

        def attn0_loads(sp):
            sp.wait_ge(s_phase, 6)
            for b in range(B):
                if b >= 2:
                    sp.wait_ge(a_k, b - 1)
                sp.dma_start(a_xT[b % 2], xnT_all[:, b * S:(b + 1) * S]).then_inc(a_ld[b % 2], 16)
            sp.wait_ge(b_all, 1)
            for b in range(B):
                if b >= 2:
                    sp.wait_ge(b_out, b - 1)
                sp.dma_start(a_zq[b % 2], a_zqs[:, b * S:(b + 1) * S]).then_inc(b_ld[b % 2], 16)

        def feat_pe(pe, prev, cur):
            if cur:
                b, r = batch(cur), cur[0] % 2
                pe.wait_ge(a_ld[r], (cur[1] + (cur[0] // 2 + 1)) * 16)
                pe.wait_ge(a_uqr, b + 1)
                pe.matmul(psum[:, r, :], b3[:, 0:C], onesb[0:3, :], start=True, stop=False)
                pe.matmul(psum[:, r, :], wqT[:, :], a_xT[r], start=False, stop=True).then_inc(a_q, 1)
                pe.wait_ge(a_ukr, b + 1)
                for t in range(T):
                    o = psum[:, 2 + 2 * r + t // 2, (t % 2) * 2 * C:(t % 2 + 1) * 2 * C]
                    pe.matmul(o, onesb[0:3, 0:P], b3[:, C:3 * C], start=True, stop=False)
                    mm = pe.matmul(o, a_xT[r][:, t * P:(t + 1) * P], wkT[:, :], start=False, stop=True)
                mm.then_inc(a_k, 1)
            if prev:
                b, r = batch(prev), prev[0] % 2
                pe.wait_ge(a_sqr, b + 1)
                pe.wait_ge(a_nsu, b + 1)
                for t in range(T):
                    mm = pe.matmul(psum[:, 6 + r, t * H:(t + 1) * H], a_sq[r][:, t * P:(t + 1) * P],
                                   block1[:, :], start=True, stop=True)
                mm.then_inc(a_nsq, 1)

        def keys_psum(r):
            return psum[:, 2 + 2 * r:4 + 2 * r, :].rearrange("p a c -> p (a c)")

        def feat_act(act, prev, cur):
            if cur:
                b, r = batch(cur), cur[0] % 2
                act.wait_ge(a_q, b + 1)
                act.wait_ge(a_zqr, b + 1)
                act.activation(a_uq[r], psum[:, r, :], ACT.Tanh, scale=0.5).then_inc(a_tqr, 1)
                act.wait_ge(a_k, b + 1)
                act.wait_ge(a_ukr, b + 1)
                act.activation(a_tk[r], keys_psum(r), ACT.Tanh, scale=0.5).then_inc(a_tkr, 1)
            if prev:
                b = batch(prev)
                act.wait_ge(a_ukr, b + 3)
                act.wait_ge(a_red, b + 1)
                act.activation(a_k2, a_uk[:, bass.ds(b * 2 * S, 2 * S)], ACT.Square, bias=1.0).then_inc(a_k2r, 1)
            if cur:
                b, r = batch(cur), cur[0] % 2
                act.wait_ge(a_uqr, b + 3)
                act.wait_ge(a_nsq, b)
                act.activation(a_sq[r], a_uq[r], ACT.Square, bias=1.0).then_inc(a_sqr, 1)

        def feat_dve(v, prev, cur):
            if cur:
                b, r = batch(cur), cur[0] % 2
                v.wait_ge(a_tqr, b + 1)
                v.scalar_tensor_tensor(out=a_uq[r], in0=a_uq[r], scalar=1.0, in1=psum[:, r, :], op0=ALU.add,
                                       op1=ALU.mult).then_inc(a_uqr, 1)
                v.wait_ge(a_uqr, b + 3)
                v.tensor_scalar(a_zqs[:, bass.ds(b * S, S)], a_uq[r], 1.0, None, ALU.add).then_inc(a_zqr, 1)
                v.wait_ge(a_tkr, b + 1)
                v.scalar_tensor_tensor(out=a_uk[:, bass.ds(b * 2 * S, 2 * S)], in0=a_tk[r], scalar=1.0,
                                       in1=keys_psum(r), op0=ALU.add, op1=ALU.mult).then_inc(a_ukr, 1)
            if prev:
                b, r = batch(prev), prev[0] % 2
                v.wait_ge(a_k2r, b + 1)
                v.tensor_reduce(a_nn[:, bass.ds(b * NN, NKN)], a_k2.rearrange("p (n e) -> p n e", e=HD), AX,
                                ALU.add).then_inc(a_red, 1)
                v.wait_ge(a_nsq, b + 2)
                v.tensor_copy(a_nn[:, bass.ds(b * NN + NKN, NQN)], psum[:, 6 + r, 0:NQN]).then_inc(a_nsu, 1)

        def roots_act(act):
            act.wait_ge(a_red, 1 + B)
            act.wait_ge(a_nsu, 2 + B)
            act.activation(a_nn, a_nn, ACT.Sqrt).then_inc(a_root, 1)

        def roots_dve(v):
            v.wait_ge(a_root, 1)
            v.tensor_scalar(a_nn, a_nn, 2e-6, None, ALU.add).then_inc(a_root, 1)
            v.wait_ge(a_root, 2)
            v.wait_ge(a_zqr, 2 + B)
            v.wait_ge(a_sqr, B)
            v.sem_inc(b_all, 1)

        def state_pe(pe, three, two, one):
            if two:
                b, r = batch(two), two[0] % 2
                pe.wait_ge(b_gs, b + 1)
                for k in range(NK):
                    mm = pe.transpose(psum[:, 2 + r, k * C:(k + 1) * C], a_G[r][:, k, 0:C], ident[:, :])
                mm.then_inc(b_gt, 1)
                pe.wait_ge(b_gts, b + 1)
                for k in range(NK):
                    mm = pe.matmul(psum[:, 2 + r, 2 * C + k * C:2 * C + (k + 1) * C], a_GT[:, k, :], wvT[:, k, :],
                                   start=True, stop=True)
                mm.then_inc(b_st, 1)
            if three:
                b = batch(three)
                pe.wait_ge(b_on, b + 1)
                for t in range(T):
                    mm = pe.transpose(psum[:, 6, t * P:(t + 1) * P], a_on[:, t, :], ident[:, :])
                mm.then_inc(b_oTp, 1)
            if two:
                b, r = batch(two), two[0] % 2
                pe.wait_ge(b_bd, b + 1)
                alone(pe)
                pe.wait_ge(b_ld[r], (two[1] + (two[0] // 2 + 1)) * 16)
                for t in range(T):
                    mm = pe.matmul(psum[:, 4 + r, t * C:(t + 1) * C], a_zq[r][:, t * P:(t + 1) * P],
                                   a_bd, start=True, stop=True)
                mm.then_inc(b_out, 1)
            if three:
                b = batch(three)
                pe.wait_ge(b_oTs, b + 1)
                pe.wait_ge(b_w, b + 1)
                for t in range(T):
                    mm = pe.matmul(psum[:, 7, t * C:(t + 1) * C], a_oT[:, t * P:(t + 1) * P], wog[:, :],
                                   start=True, stop=True)
                mm.then_inc(b_wo, 1)
            if one:
                b, r = batch(one), one[0] % 2
                pe.wait_ge(b_kh, b + 1)
                for k in range(NK):
                    for t in range(T):
                        mm = pe.matmul(psum[:, r, k * NG:(k + 1) * NG], a_kh[r][:, t, k, :],
                                       xr_all[:, bass.ds(b * T + t, 1), 0:NG].rearrange("p a c -> p (a c)"),
                                       start=(t == 0), stop=(t == T - 1))
                mm.then_inc(b_g, 1)

        def state_act(act, three, two, one):
            if two:
                b, r = batch(two), two[0] % 2
                act.wait_ge(b_gt, b + 1)
                act.activation(a_GT.rearrange("p k c -> p (k c)"), psum[:, 2 + r, 0:2 * C],
                               ACT.Copy).then_inc(b_gts, 1)
            if three:
                b, r = batch(three), three[0] % 2
                act.wait_ge(b_rl, b + 1)
                for t in range(T):
                    ins = act.activation(a_on[:, t, :], a_o[r][:, t, :], ACT.Identity, bias=a_nb[:, t:t + 1],
                                         scale=a_rl[:, t:t + 1])
                ins.then_inc(b_on, 1)
                act.wait_ge(b_oTp, b + 1)
                act.activation(a_oT, psum[:, 6, :], ACT.Copy).then_inc(b_oTs, 1)
            if one:
                b, r = batch(one), one[0] % 2
                act.wait_ge(b_g, b + 1)
                act.activation(a_G[r].rearrange("p k c -> p (k c)"), psum[:, r, 0:2 * NG],
                               ACT.Copy).then_inc(b_gs, 1)
            if three:
                b = batch(three)
                act.wait_ge(b_wo, b + 1)
                act.wait_ge(b_xu, b + 1)
                act.activation(a_w, psum[:, 7, :], ACT.Copy).then_inc(b_w, 1)
            if two:
                b = batch(two)
                act.wait_ge(b_ve, b + 1)
                act.activation(a_ve[:, :], a_ve[:, :], ACT.Sqrt).then_inc(b_sq, 1)

        def state_dve(v, three, two, one):
            ch = Chain(v, s_chain)
            if three:
                v.wait_ge(b_sq, batch(three) + 1)
                ch.link(v.reciprocal(a_rl[:, :], a_ve[:, :]))
                v.scalar_tensor_tensor(out=a_nb[:, :], in0=mv4[:, :, 0], scalar=-1.0, in1=a_rl[:, :], op0=ALU.mult,
                                       op1=ALU.mult).then_inc(b_rl, 1)
                v.wait_ge(b_rl, batch(three) + 1)
            if one:
                b, r = batch(one), one[0] % 2
                ch.after(v.reciprocal(a_kn[:, :], a_nn[:, bass.ds(b * NN, NKN)]))
                ch.after(v.reciprocal(a_rq[r][:, :], a_nn[:, bass.ds(b * NN + NKN, NQN)]))
            if two:
                b, r = batch(two), two[0] % 2
                v.wait_ge(b_st, b + 1)
                for k in range(NK):
                    ch.after(v.scalar_tensor_tensor(out=a_s[:, k, :], in0=bv_bc[:, k, :],
                                                    scalar=a_G[r][:, k, C:C + 1],
                                                    in1=psum[:, 2 + r, 2 * C + k * C:2 * C + (k + 1) * C],
                                                    op0=ALU.mult, op1=ALU.add))
                ch.sync()
                ch.link(v.tensor_tensor(a_s[:, 0, :], a_s[:, 0, :], a_s[:, 1, :], ALU.mult))
                v.tensor_tensor(a_bd, a_s[:, 0, :], bmask[:, :, :].rearrange("p h e -> p (h e)"),
                                ALU.mult).then_inc(b_bd, 1)
                v.wait_ge(b_bd, b + 1)
            alone(v)
            ch.sync()
            if one:
                b, r = batch(one), one[0] % 2
                v.scalar_tensor_tensor(out=a_kh[r].rearrange("p t k (h e) -> p (t k h) e", e=HD),
                                       in0=a_uk[:, bass.ds(b * 2 * S, 2 * S)].rearrange("p (n e) -> p n e", e=HD),
                                       scalar=1.0, in1=a_kn[:, :].unsqueeze(2).to_broadcast([P, NKN, HD]),
                                       op0=ALU.add, op1=ALU.mult).then_inc(b_kh, 1)
                v.wait_ge(b_kh, b + 1)
            if two:
                b, r = batch(two), two[0] % 2
                v.wait_ge(b_out, b + 1)
                ch.link(v.tensor_tensor(a_o[r].rearrange("p t (h e) -> p (t h) e", e=HD),
                                        psum[:, 4 + r, :].rearrange("p (h e) -> p h e", e=HD),
                                        a_rq[r][:, :].unsqueeze(2).to_broadcast([P, T * H, HD]), ALU.mult))
                for t in range(T):
                    ch.after(v.bn_stats(st4[:, t, :], a_o[r][:, t, :]))
                ch.sync()
                for t in range(T):
                    ch.after(v.bn_aggr(mv4[:, t, :], st4[:, t, :]))
                ch.sync()
                v.tensor_scalar(a_ve[:, :], mv4[:, :, 1], EPS, None, ALU.add).then_inc(b_ve, 1)
            alone(v)
            ch.restart()

        def state_pool(g):
            with g.Fori(0, B) as b:
                g.wait_ge(b_w, b + 2)
                alone(g)
                xb = x_all[:, bass.ds(b * T, T), :]
                g.tensor_tensor(xb, xb, a_w.rearrange("p (t c) -> p t c", t=T), ALU.add).then_inc(b_xu, 1)

        def states(eng, stage):
            stage(eng, None, None, (0, 0))
            stage(eng, None, (0, 0), (1, 0))
            with eng.Fori(0, B // 2 - 1) as i:
                stage(eng, (0, i), (1, i), (2, i))
                stage(eng, (1, i), (2, i), (3, i))
            stage(eng, (B - 2, 0), (B - 1, 0), None)
            stage(eng, (B - 1, 0), None, None)

        def bias_pool(g):
            g.wait_ge(s_bo, 1)
            g.wait_ge(s_phase, 6)
            with g.Fori(0, B) as b:
                xb = x_all[:, bass.ds(b * T, T), :]
                g.tensor_tensor(xb, xb, bo_bc[:, :].unsqueeze(1).to_broadcast([P, T, C]), ALU.add).then_inc(s_bo, 1)

        start_views()
        RING = 8
        f_x = [view(ROW) for _ in range(RING)]
        f_y = [view(C) for _ in range(RING)]
        f_xT = [view(P) for _ in range(2)]
        f_w1 = [view(F) for _ in range(4)]
        f_hT = [view(F) for _ in range(4)]
        ffn_sems = []
        for layer in range(2):
            q = {n: sem(f"f{layer}_{n}") for n in ("xTp", "xT", "yp", "y") + ("hp", "hT") * layer}
            q["ld"] = [sem(f"f{layer}_ld{r}") for r in range(RING)]
            q["sc"] = [sem(f"f{layer}_sc{r}") for r in range(RING)]
            q["w"] = [sem(f"f_w{r}") for r in range(4)] if layer else []
            ffn_sems.append(q)

        def steps(eng, layer, lead, lag, step):
            nt = NT1 if layer else NT0
            for k in range(-lead, RING):
                step(k, 0, k)
            with eng.Fori(1, nt // RING - 1) as i:
                for r in range(RING):
                    step(i * RING + r, i, r)
            for k in range(nt - RING, nt + lag):
                step(k, nt // RING - 1, k - (nt - RING))

        def tile(layer, k, i, r, off):
            nt = NT1 if layer else NT0
            if isinstance(k, int) and not 0 <= k + off < nt:
                return None
            r += off
            return k + off, i + r // RING, r % RING

        def expert_of(eng, layer, k):
            return eng.value_load(expert[0:1, layer, bass.ds(k, 1)], min_val=0, max_val=E - 1)

        def ffn_sp(sp, layer, src):
            q = ffn_sems[layer]
            sv = src.rearrange("(n p) c -> p n c", p=P)

            def step(k, i, r):
                t = tile(layer, k, i, r, -1) if layer else None
                if t:
                    n, u, rr = t
                    e = expert_of(sp, layer, n)
                    if not (isinstance(n, int) and n < 4):
                        sp.wait_ge(q["hp"], n - 3)
                        alone(sp)
                    sp.dma_start(f_w1[rr % 4], w1[:, bass.ds(e, 1), :].rearrange("p a f -> p (a f)")).then_inc(
                        q["w"][rr % 4], 16)
                t = tile(layer, k, i, r, 0)
                if t:
                    k, n, r = t
                    if not (isinstance(n, int) and n == 0):
                        sp.wait_ge(q["sc"][r], n * 16)
                        alone(sp)
                        sp.wait_ge(q["xTp"], k - (RING - 1))
                        alone(sp)
                    sp.dma_start(f_x[r], sv[:, bass.ds(k, 1), :].rearrange("p a c -> p (a c)")).then_inc(
                        q["ld"][r], 16)

            steps(sp, layer, 0, layer, step)

        def ffn_pe(pe, layer):
            q = ffn_sems[layer]

            def step(k, i, r):
                t = tile(layer, k, i, r, 1)
                if t:
                    n, u, rr = t
                    pe.wait_ge(q["ld"][rr], (u + 1) * 16)
                    pe.transpose(psum[:, rr % 2, 0:P], f_x[rr][:, 0:C], ident[:, :]).then_inc(q["xTp"], 1)
                t = tile(layer, k, i, r, 0)
                if t:
                    n, u, rr = t
                    if layer:
                        pe.wait_ge(q["xT"], n + 1)
                        pe.wait_ge(q["w"][rr % 4], (u * 2 + (rr // 4 + 1)) * 16)
                        for j in range(FC):
                            mm = pe.matmul(psum[:, 2 + rr % 2, j * P:(j + 1) * P],
                                           f_w1[rr % 4][:, j * P:(j + 1) * P], f_xT[rr % 2], start=True, stop=True)
                        mm.then_inc(q["hp"], 1)
                    else:
                        e = expert_of(pe, layer, n)
                        pe.wait_ge(q["xT"], n + 1)
                        if not (isinstance(n, int) and n < 2):
                            pe.wait_ge(q["y"], n - 1)
                        pe.matmul(psum[:, 6 + rr % 2, 0:C], f_xT[rr % 2],
                                  weT[:, bass.ds(e, 1), :].rearrange("p a f -> p (a f)"),
                                  start=True, stop=True).then_inc(q["yp"], 1)
                if not layer:
                    return
                t = tile(layer, k, i, r, -2)
                if t:
                    n, u, rr = t
                    e = expert_of(pe, layer, n)
                    pe.wait_ge(q["hT"], n + 1)
                    if not (isinstance(n, int) and n < 2):
                        pe.wait_ge(q["y"], n - 1)
                    for j in range(FC):
                        mm = pe.matmul(psum[:, 6 + rr % 2, 0:C], f_hT[rr % 4][:, j * P:(j + 1) * P],
                                       w2[:, bass.ds(e * FC + j, 1), :].rearrange("p a f -> p (a f)"),
                                       start=(j == 0), stop=(j == FC - 1))
                    mm.then_inc(q["yp"], 1)

            steps(pe, layer, 1, 2 * layer, step)

        def ffn_act(act, layer):
            q = ffn_sems[layer]

            def step(k, i, r):
                t = tile(layer, k, i, r, 1)
                if t:
                    n, u, rr = t
                    act.wait_ge(q["xTp"], n + 1)
                    act.activation(f_xT[rr % 2], psum[:, rr % 2, 0:P], ACT.Copy).then_inc(q["xT"], 1)
                t = tile(layer, k, i, r, 0) if layer else None
                if t:
                    n, u, rr = t
                    e = expert_of(act, layer, n)
                    act.wait_ge(q["hp"], n + 1)
                    for j in range(FC):
                        ins = act.activation(f_hT[rr % 4][:, j * P:(j + 1) * P], psum[:, 2 + rr % 2, j * P:(j + 1) * P],
                                             ACT.Relu, bias=b1T[:, bass.ds(e * FC + j, 1)])
                    ins.then_inc(q["hT"], 1)

            steps(act, layer, 1, 0, step)

        def ffn_dve(v, layer):
            q = ffn_sems[layer]
            bias2 = b2_bc if layer else eb_bc

            def step(k, i, r):
                t = tile(layer, k, i, r, -2 * layer)
                if t:
                    n, u, rr = t
                    e = expert_of(v, layer, n)
                    v.wait_ge(q["yp"], n + 1)
                    if not (isinstance(u, int) and u == 0):
                        v.wait_ge(q["sc"][rr], u * 16)
                    v.tensor_tensor(f_y[rr], psum[:, 6 + rr % 2, 0:C],
                                    bias2[:, bass.ds(e, 1), :].rearrange("p a f -> p (a f)"),
                                    ALU.add).then_inc(q["y"], 1)

            steps(v, layer, 0, 2 * layer, step)

        def ffn_pool(g, layer):
            q = ffn_sems[layer]

            def step(k, i, r):
                t = tile(layer, k, i, r, 0)
                if t:
                    n, u, rr = t
                    g.wait_ge(q["y"], n + 1)
                    alone(g)
                    g.indirect_dma_start(out=ydram, out_offset=bass.IndirectOffsetOnAxis(
                        ap=f_x[rr][:, C + 1:C + 2].bitcast(I32), axis=0), in_=f_y[rr], in_offset=None,
                        bounds_check=ydram.shape[0] - 1, oob_is_err=False).then_inc(q["sc"][rr], 16)

            steps(g, layer, 0, 0, step)

        def ffn_scattered(eng, layer):
            for r in range(RING):
                eng.wait_ge(ffn_sems[layer]["sc"][r], 16 * ((NT1 if layer else NT0) // RING))

        def y0_loads(sp):
            ffn_scattered(sp, 0)
            for b in range(B):
                if b >= 2:
                    sp.wait_ge(s_yu, b - 1)
                sp.dma_start(yl[b % 2], y_v[:, 0, b * T:(b + 1) * T, :]).then_inc(s_yl[b % 2], 16)

        start_views()
        W2 = 2 * W
        XP = W + S
        NP_ = NB // 2
        c_xT = [view(XP) for _ in range(2)]
        c_kz = view(G * XP).rearrange("p (g n) -> p g n", g=G)
        c_q = mix0[:, 0:NB * P].rearrange("p (n h q) -> p n h q", n=NB, h=G)
        c_gq = view(S)
        c_gk = view(LH * NL).rearrange("p (h n) -> p h n", h=LH)
        c_v = view(NP_ * G * 2 * (W + 1)).rearrange("p (j g b e) -> p j g b e", j=NP_, g=G, b=2)
        c_gv = view(LH * (HD + 1)).rearrange("p (j b e) -> p j b e", j=LH // 2, b=2)
        c_tl = view(S)
        c_tr = view(S)
        c_lg = view(S)
        c_sx = [view(512) for _ in range(2)]
        c_p = [view(512) for _ in range(3)]
        c_pT = [view(512) for _ in range(2)]
        c_z = [view(HB * P).rearrange("p (n g c) -> p n g c", n=HB, g=G) for _ in range(2)]
        c_rem = view(T * LAT).rearrange("p (t c) -> p t c", t=T)
        c_rT = view(S, parts=LAT)
        c_cb = view(S)
        c_xp = view(2 * NL).rearrange("p (b n) -> p b n", b=2)
        c_mx = view(8)
        c_rs = view(8)
        c_rm = view(8 * G).rearrange("p (n h) -> p n h", n=8)
        order = [n // 4 * 4 + (0, 2, 1, 3)[n % 4] for n in range(HB)]
        U = 12

        def pair(u):
            return [u // 4 * HB + order[u % 4 * 2 + k] for k in range(2)]

        ACC = ["S0", "V1", "S1", "GQ", "S2", "S3", "GV", "S4", "S5", "remo", "S6", "out", "gl", "S7", "gr", "S8",
               "loc0", "Q", "S9", "K", "S10", "V0", "S11", "loc1"]
        PT = ["T10", "T11", "T0", "GK", "T1", "T2", "remT"] + [f"T{u}" for u in range(3, U - 2)]
        PROJ = ("Q", "K", "V0")
        TAIL = ("T10", "T11", "remT", "remo", "out")

        c_vr = [sem(f"c_vr{n}") for n in range(3)]

        def use_counts(period, banks):
            seq = [(n, 0) for n in period if n in PROJ]
            for b in range(B):
                for n in period:
                    owner = b + (1 if n in PROJ else -1 if n in TAIL else 0)
                    if 0 <= owner < B:
                        seq.append((n, owner))
            seq += [(n, B - 1) for n in period if n in TAIL]
            seen, table = [0] * banks, {}
            for n, owner in seq:
                k = period.index(n) % banks
                seen[k] += 1
                table[n, owner] = seen[k]
            return table

        acc_uses, pt_uses = use_counts(ACC, 4), use_counts(PT, 2)

        c_rdy = [sem(f"c_rdy{n}") for n in range(4)]
        c_free = [sem(f"c_free{n}") for n in range(4)]
        c_prdy = [sem(f"c_prdy{n}") for n in range(2)]
        c_pfree = [sem(f"c_pfree{n}") for n in range(2)]
        c_ordy = [sem(f"c_ordy{n}") for n in range(2)]
        c_ofree = [sem(f"c_ofree{n}") for n in range(2)]
        c_ld = [sem(f"c_ld{n}") for n in range(2)]
        (c_init, c_xpr, c_qr, c_gqr, c_gkr, c_tr_, c_sxr, c_pr, c_pTr, c_zr, c_remr, c_rTr, c_cbr) = (
            sem(n) for n in ("c_init c_xpr c_qr c_gqr c_gkr c_tanh c_sxr c_pr c_pTr c_zr c_remr c_rTr "
                             "c_cbr").split())

        def acc(name, bt):
            k = ACC.index(name) % 4
            return psum[:, k, :], c_rdy[k], c_free[k], acc_uses[name, bt[0]] + bt[1] * (2 * len(ACC) // 4)

        def pt_bank(name, bt):
            k = PT.index(name) % 2
            return psum[:, 4 + k, :], c_prdy[k], c_pfree[k], pt_uses[name, bt[0]] + bt[1] * len(PT)

        def o_bank(u, bt):
            return psum[:, 6 + u % 2, :], c_ordy[u % 2], c_ofree[u % 2], batch(bt) * 6 + (u // 2 + 1)

        def attn1_init(g):
            ch = Chain(g, s_pool)
            g.sem_clear(s_pool)
            g.wait_ge(s_phase, 15)
            for a in (c_xT[0], c_xT[1], c_kz[:, 0, :], c_kz[:, 1, :], c_kz[:, 2, :], c_kz[:, 3, :]):
                ch.link(g.memset(a[:, 0:W], 0.0))
            ch.link(g.memset(c_gq[LAT:P, :], 0.0))
            ch.link(g.memset(c_gk[LAT:P, :, :], 0.0))
            ch.link(g.memset(c_v, 0.0))
            ch.link(g.memset(c_v[0:64, :, :, 0, W:W + 1], 1.0))
            ch.link(g.memset(c_v[64:P, :, :, 1, W:W + 1], 1.0))
            ch.link(g.memset(c_gv, 0.0))
            ch.link(g.memset(c_gv[0:64, :, 0, HD:HD + 1], 1.0))
            ch.link(g.memset(c_gv[64:P, :, 1, HD:HD + 1], 1.0))
            g.engine_nop().then_inc(c_init, 1)

        def attn1_loads(sp):
            sp.wait_ge(c_init, 1)
            for b in range(B):
                if b >= 2:
                    _, rdy, _, n = acc("gr", (b - 2, 0))
                    sp.wait_ge(rdy, n)
                    sp.wait_ge(c_xpr, b - 1)
                sp.dma_start(c_xT[b % 2][:, W:XP], xnT_all[:, b * S:(b + 1) * S]).then_inc(c_ld[b % 2], 16)

        def unit_at(s, lag, prev, cur):
            return (s - lag, cur) if s >= lag else (U + s - lag, prev)

        def attn1_pe(pe, prev, cur, nxt):
            def begin(bank):
                o, rdy, free, n = bank
                pe.wait_ge(free, n)
                return o, rdy

            def project(name, bt):
                if not bt:
                    return
                r = bt[0] % 2
                xT = c_xT[r][:, W:XP]
                if name == "Q":
                    pe.wait_ge(c_ld[r], (bt[1] + (bt[0] // 2 + 1)) * 16)
                if name in ("GV", "GK"):
                    pe.wait_ge(c_xpr, batch(bt) + 1)
                o, rdy = begin(pt_bank(name, bt) if name == "GK" else acc(name, bt))
                if name[0] == "V":
                    for j in range(NP_ // 2):
                        first = W * (int(name[1]) * HB + order[2 * j])
                        mm = pe.matmul(o[:, j * C:(j + 1) * C], c_xT[r][:, first:first + 2 * W2], wv1[:, :],
                                       start=True, stop=True)
                elif name == "GV":
                    mm = pe.matmul(o[:, 0:LAT], c_xp.rearrange("p b n -> p (b n)"), wgv[:, :], start=True,
                                   stop=True)
                elif name == "GK":
                    mm = pe.matmul(o[0:LAT, 0:NL], wgk[:, :], c_xp[:, 0, :], start=True, stop=True)
                elif name == "GQ":
                    mm = pe.matmul(o[0:LAT, :], wgq[:, :], xT, start=True, stop=True)
                else:
                    w = dict(Q=wq1[:, :], K=wk1[:, :], gl=wgate[:, 0, :, :].rearrange("p h e -> p (h e)"),
                             gr=wgate[:, 1, :, :].rearrange("p h e -> p (h e)"))[name]
                    mm = pe.matmul(o, w, xT, start=True, stop=True)
                mm.then_inc(rdy, 1)

            def scores(u):
                o, rdy = begin(acc(f"S{u}", cur))
                if u < 8:
                    if u == 0:
                        pe.wait_ge(c_qr, batch(cur) + 1)
                    pe.matmul(o, selq[:, :, :].rearrange("p h q -> p (h q)"),
                              lmask[:, 0 if u == 0 else 1, :, :].rearrange("p k j -> p (k j)").unsqueeze(1)
                              .to_broadcast([P, G, 2 * W2]), start=True, stop=False, skip_group_check=True)
                    ov = o.rearrange("p (g k j) -> p g k j", g=G, k=2)
                    for k in range(2):
                        n = pair(u)[k]
                        mm = pe.matmul(ov[:, :, k, :], c_q[:, n, :, :].rearrange("p h q -> p (h q)"),
                                       c_kz[:, :, n * W:n * W + W2], start=False, stop=(k == 1),
                                       skip_group_check=True)
                else:
                    t = u - 8
                    if t == 0:
                        pe.wait_ge(c_gqr, batch(cur) + 1)
                        pe.wait_ge(c_gkr, batch(cur) + 1)
                    pe.matmul(o, selr[:, :], gmask[:, t, :].unsqueeze(1).to_broadcast([P, LH, NL]), start=True,
                              stop=False)
                    mm = pe.matmul(o, c_gq[:, t * P:(t + 1) * P], c_gk.rearrange("p h n -> p (h n)"), start=False,
                                   stop=True)
                mm.then_inc(rdy, 1)

            def transposes(u, bt):
                if not bt:
                    return
                pe.wait_ge(c_pr, batch(bt) * U + (u + 1))
                o, rdy = begin(pt_bank(f"T{u}", bt))
                for j in range(4):
                    mm = pe.transpose(o[:, j * P:(j + 1) * P], c_p[u % 3][:, j * P:(j + 1) * P], ident[:, :])
                mm.then_inc(rdy, 1)

            def values(u, bt):
                if not bt:
                    return
                pe.wait_ge(c_pTr, batch(bt) * U + (u + 1))
                if u in (0, 4, 8):
                    pe.wait_ge(c_vr[u // 4], batch(bt) + 1)
                o, rdy = begin(o_bank(u, bt))
                for j in range(4):
                    w = c_pT[u % 2][:, j * P:(j + 1) * P]
                    if u < 8:
                        dst = o[:, 0:8 * (W + 1)].rearrange("p (k g e) -> p k g e", k=2, g=G)[:, :, j, :]
                        rhs = c_v[:, u, j, :, :]
                    else:
                        n = 2 * (HD + 1)
                        dst = o[:, j * n:(j + 1) * n]
                        rhs = c_gv[:, j, :, :].rearrange("p b e -> p (b e)")
                    mm = pe.matmul(dst, w, rhs, start=True, stop=True)
                mm.then_inc(rdy, 1)

            def local_out(hf):
                pe.wait_ge(c_zr, batch(cur) * 8 + (4 * hf + 4))
                o, rdy = begin(acc(f"loc{hf}", cur))
                for j in range(HB):
                    mm = pe.matmul(o[:, order[j] * W:(order[j] + 1) * W], c_z[hf][:, j, :, :].rearrange("p g c -> p (g c)"),
                                   pick[:, :], start=True, stop=True)
                mm.then_inc(rdy, 1)

            def tail(name):
                if not prev:
                    return
                if name == "remT":
                    pe.wait_ge(c_remr, batch(prev) + 1)
                    o, rdy = begin(pt_bank("remT", prev))
                    alone(pe)
                    for t in range(T):
                        mm = pe.transpose(o[0:LAT, t * P:(t + 1) * P], c_rem[:, t, :], ident[:, :])
                elif name == "remo":
                    pe.wait_ge(c_rTr, batch(prev) + 1)
                    o, rdy = begin(acc("remo", prev))
                    mm = pe.matmul(o, rout[:, :], c_rT, start=True, stop=True)
                else:
                    pe.wait_ge(c_cbr, batch(prev) + 1)
                    o, rdy = begin(acc("out", prev))
                    for t in range(T):
                        mm = pe.matmul(o[:, t * C:(t + 1) * C], c_cb[:, t * P:(t + 1) * P], wout[:, :],
                                       start=True, stop=True)
                mm.then_inc(rdy, 1)

            if not cur and not prev:
                for name in PROJ:
                    project(name, nxt)
                return
            for s in range(U):
                if cur:
                    scores(s)
                transposes(*unit_at(s, 2, prev, cur))
                values(*unit_at(s, 3, prev, cur))
                if s in (4, 5, 6):
                    tail({4: "remT", 5: "remo", 6: "out"}[s])
                if s == 8 and cur:
                    local_out(0)
                if s == 11 and cur:
                    local_out(1)
                for at_step, name, bt in ((0, "V1", cur), (1, "GQ", cur), (2, "GK", cur), (3, "GV", cur),
                                          (6, "gl", cur), (7, "gr", cur), (8, "Q", nxt), (9, "K", nxt),
                                          (10, "V0", nxt)):
                    if s == at_step:
                        project(name, bt)

        def attn1_act(act, prev, cur, nxt):
            def bank(x):
                o, rdy, free, n = x
                act.wait_ge(rdy, n)
                return o, free

            def queries(heads):
                o, free = bank(acc("Q", nxt))
                for h in heads:
                    ins = act.activation(c_q[:, :, h, :], o.rearrange("p (n q) -> p n q", n=NB), ACT.Copy,
                                         scale=head_m[:, h:h + 1])
                if G - 1 in heads:
                    ins.then_inc(free, 1)

            def keys(groups):
                o, free = bank(acc("K", nxt))
                for g in groups:
                    ins = act.activation(c_kz[:, g, W:XP], o, ACT.Copy, scale=row_m[:, g:g + 1])
                if G - 1 in groups:
                    ins.then_inc(free, 1)
                    act.wait_ge(free, acc("K", nxt)[3] + 1)
                    act.sem_inc(c_qr, 1)

            def gates(name, dst):
                o, free = bank(acc(name, cur))
                act.activation(dst, o, ACT.Tanh, scale=0.5).then_inc(free, 1)
                if name == "gr":
                    act.wait_ge(free, acc("gr", cur)[3] + 1)
                    act.sem_inc(c_tr_, 1)

            def window_values(hf, bt):
                o, free = bank(acc(f"V{hf}", bt))
                ov = o.rearrange("p (j g e) -> p j g e", j=4, g=G)
                for bb in range(2):
                    row = slice(64 * bb, 64 * bb + 64)
                    ins = act.activation(c_v[row, 4 * hf:4 * hf + 4, :, bb, 0:W], ov[row, :, :, :], ACT.Copy)
                ins.then_inc(free, 1)
                act.wait_ge(free, acc(f"V{hf}", bt)[3] + 1)
                act.sem_inc(c_vr[hf], 1)

            def latent_queries():
                o, free = bank(acc("GQ", cur))
                act.activation(c_gq[0:LAT, :], o[0:LAT, :], ACT.Copy).then_inc(free, 1)
                act.wait_ge(free, acc("GQ", cur)[3] + 1)
                act.sem_inc(c_gqr, 1)

            def latent_values():
                o, free = bank(acc("GV", cur))
                ov = o[:, 0:LAT].rearrange("p (j b e) -> p j b e", j=LH // 2, b=2)
                for bb in range(2):
                    row = slice(64 * bb, 64 * bb + 64)
                    ins = act.activation(c_gv[row, :, bb, 0:HD], ov[row, :, bb, :], ACT.Copy)
                ins.then_inc(free, 1)
                act.wait_ge(free, acc("GV", cur)[3] + 1)
                act.sem_inc(c_vr[2], 1)

            def tail():
                o, free = bank(pt_bank("remT", prev))
                act.activation(c_rT, o[0:LAT, :], ACT.Copy).then_inc(free, 1)
                act.wait_ge(free, pt_bank("remT", prev)[3] + 1)
                act.sem_inc(c_rTr, 1)

            if not cur and not prev:
                queries(range(G))
                keys(range(G))
                window_values(0, nxt)
                return
            for s in range(U):
                if cur:
                    act.wait_ge(c_sxr, batch(cur) * U + (s + 1))
                    act.activation(c_p[s % 3], c_sx[s % 2], ACT.Exp).then_inc(c_pr, 1)
                u, bt = unit_at(s, 2, prev, cur)
                if bt:
                    o, free = bank(pt_bank(f"T{u}", bt))
                    act.activation(c_pT[u % 2], o, ACT.Copy).then_inc(free, 1)
                    act.wait_ge(free, pt_bank(f"T{u}", bt)[3] + 1)
                    act.sem_inc(c_pTr, 1)
                if s == 4 and prev:
                    tail()
                if cur:
                    if s == 0:
                        window_values(1, cur)
                    if s == 1:
                        latent_queries()
                    if s == 3:
                        latent_values()
                    if s == 6:
                        gates("gl", c_tl)
                    if s == 7:
                        gates("gr", c_tr)
                if nxt:
                    if s == 8:
                        queries((0, 1, 2))
                    if s == 9:
                        queries((3,))
                        keys((0, 1))
                    if s == 10:
                        keys((2, 3))
                    if s == 11:
                        window_values(0, nxt)

        def attn1_dve(v, prev, cur, nxt):
            ch = Chain(v, s_chain)

            def bank(x):
                o, rdy, free, n = x
                v.wait_ge(rdy, n)
                return o, free

            def pooled():
                r = cur[0] % 2
                v.wait_ge(c_ld[r], (cur[1] + (cur[0] // 2 + 1)) * 16)
                ch.link(v.tensor_reduce(c_xp[:, 0, :], c_xT[r][:, W:XP].rearrange("p (n e) -> p n e", n=NL), AX,
                                        ALU.add))
                v.tensor_copy(c_xp[:, 1, :], c_xp[:, 0, :]).then_inc(c_xpr, 1)

            def latent_keys():
                o, free = bank(pt_bank("GK", cur))
                v.tensor_tensor(c_gk[0:LAT, :, :], o[0:LAT, 0:NL].unsqueeze(1).to_broadcast([LAT, LH, NL]),
                                gk_m[:, 0:LH].unsqueeze(2).to_broadcast([LAT, LH, NL]), ALU.mult).then_inc(free, 1)
                v.wait_ge(free, pt_bank("GK", cur)[3] + 1)
                v.sem_inc(c_gkr, 1)

            def joined():
                o, free = bank(acc("remo", prev))
                v.scalar_tensor_tensor(out=c_cb, in0=c_tr, scalar=1.0, in1=o, op0=ALU.add,
                                       op1=ALU.mult).then_inc(free, 1)
                v.wait_ge(free, acc("remo", prev)[3] + 1)
                v.tensor_tensor(c_cb, c_cb, c_lg, ALU.add).then_inc(c_cbr, 1)

            def onto_stream():
                o, free = bank(acc("out", prev))
                xb = x_all[:, bass.ds(batch(prev) * T, T), :]
                v.tensor_tensor(xb, xb, o.rearrange("p (t c) -> p t c", t=T), ALU.add).then_inc(free, 1)

            def normalise(u, bt):
                if not bt:
                    return
                oo, ofree = bank(o_bank(u, bt))
                e = W if u < 8 else HD
                ov = oo[:, 0:8 * (e + 1)].rearrange("p (n e) -> p n e", n=8)
                ch.link(v.reciprocal(c_rs, ov[:, :, e]))
                if u < 8:
                    ch.link(v.tensor_tensor(c_rm, c_rs.unsqueeze(2).to_broadcast([P, 8, G]),
                                            row_m[:, :].unsqueeze(1).to_broadcast([P, 8, G]), ALU.mult))
                    v.tensor_tensor(c_z[u // 4][:, u % 4 * 2:u % 4 * 2 + 2, :, :]
                                    .rearrange("p k g (h e) -> p (k g) h e", h=G),
                                    ov[:, :, 0:W].rearrange("p n (h e) -> p n h e", h=G),
                                    c_rm.unsqueeze(3).to_broadcast([P, 8, G, HD]), ALU.mult).then_inc(c_zr, 1)
                    v.wait_ge(c_zr, batch(bt) * 8 + (u + 1))
                    v.sem_inc(ofree, 1)
                else:
                    v.tensor_tensor(c_rem[:, u - 8, :].rearrange("p (h e) -> p h e", h=LH), ov[:, :, 0:HD],
                                    c_rs.unsqueeze(2).to_broadcast([P, LH, HD]), ALU.mult).then_inc(ofree, 1)
                    v.wait_ge(ofree, o_bank(u, bt)[3] + 1)

            def gated(hf, bt):
                if hf == 0:
                    v.wait_ge(c_tr_, batch(bt) + 1)
                o, free = bank(acc(f"loc{hf}", bt))
                h2 = slice(hf * S // 2, (hf + 1) * S // 2)
                v.scalar_tensor_tensor(out=c_lg[:, h2], in0=c_tl[:, h2], scalar=1.0,
                                       in1=o[:, 0:S // 2], op0=ALU.add, op1=ALU.mult).then_inc(free, 1)
                v.wait_ge(free, acc(f"loc{hf}", bt)[3] + 1)

            if not cur and not prev:
                return
            for s in range(U):
                if cur:
                    o, free = bank(acc(f"S{s}", cur))
                    sv = o.rearrange("p (n j) -> p n j", n=8)
                    ch.link(v.tensor_reduce(c_mx, sv, AX, ALU.max))
                    if s >= 2:
                        v.wait_ge(c_pr, batch(cur) * U + (s - 1))
                    v.tensor_tensor(c_sx[s % 2].rearrange("p (n j) -> p n j", n=8), sv,
                                    c_mx.unsqueeze(2).to_broadcast([P, 8, W2]), ALU.subtract).then_inc(c_sxr, 1)
                    v.wait_ge(c_sxr, batch(cur) * U + (s + 1))
                    v.sem_inc(free, 1)
                if prev:
                    if s == 0:
                        gated(1, prev)
                    if s == 5:
                        joined()
                    if s == 7:
                        onto_stream()
                if s == 9 and cur:
                    gated(0, cur)
                normalise(*unit_at(s, 3, prev, cur))
                if s == 2 and prev:
                    v.sem_inc(c_remr, 1)
                if cur:
                    if s == 1:
                        pooled()
                    if s == 3:
                        latent_keys()
            alone(v)
            ch.restart()

        def attn1(eng, stage):
            stage(eng, None, None, (0, 0))
            stage(eng, None, (0, 0), (1, 0))
            with eng.Fori(0, B // 2 - 1) as i:
                stage(eng, (0, i), (1, i), (2, i))
                stage(eng, (1, i), (2, i), (3, i))
            stage(eng, (B - 2, 0), (B - 1, 0), None)
            stage(eng, (B - 1, 0), None, None)

        s_ids = sem("s_ids")

        def ids1(g):
            g.wait_ge(s_sc, 16 * NT * 2)
            g.iota(xr_all[:, :, C + 1:C + 2].bitcast(I32), pattern=[[P, NT], [0, 1]], base=NT * P,
                   channel_multiplier=1).then_inc(s_ids, 1)
            g.wait_ge(s_ids, 1)

        start_views()
        Z = 4
        z_y = [view(2 * S).rearrange("p (k t c) -> p k t c", k=2, t=T) for _ in range(Z)]
        z_ld = [sem(f"z_ld{r}") for r in range(Z)]
        z_s = sem("z_s")
        z_x = sem("z_x")

        def last_sp(sp):
            sp.wait_ge(s_phase, 18)
            ffn_scattered(sp, 1)

            def load(b):
                for k in range(2):
                    sp.dma_start(z_y[b % Z][:, k, :, :], y_v[:, k, b * T:(b + 1) * T, :]).then_inc(z_ld[b % Z], 16)

            for b in range(Z):
                load(b)
            for b in range(B):
                sp.wait_ge(z_x, b + 1)
                if b + Z < B:
                    load(b + Z)
                sp.dma_start(out_v[:, b * T:(b + 1) * T, :], x_all[:, b * T:(b + 1) * T, :]).then_inc(s_out, 16)
            sp.wait_ge(s_out, 16 * B)

        def last_act(act):
            with act.Fori(0, B // Z) as i:
                for r in range(Z):
                    b = i * Z + r
                    act.wait_ge(z_ld[r], (i + 1) * 32)
                    for t in range(T):
                        ins = act.activation(z_y[r][:, 0, t, :], z_y[r][:, 0, t, :], ACT.Copy,
                                             scale=gate[:, 0, bass.ds(b * T + t, 1)])
                    ins.then_inc(z_s, 1)

        def last_dve(v):
            ch = Chain(v, s_chain)
            with v.Fori(0, B // Z) as i:
                for r in range(Z):
                    b = i * Z + r
                    v.wait_ge(z_ld[r], (i + 1) * 32)
                    for t in range(T):
                        n = b * T + t
                        xt = x_all[:, bass.ds(n, 1), :].rearrange("p a c -> p (a c)")
                        ch.after(v.scalar_tensor_tensor(out=xt, in0=z_y[r][:, 1, t, :],
                                                        scalar=gate[:, 1, bass.ds(n, 1)], in1=xt,
                                                        op0=ALU.mult, op1=ALU.add))
                    v.wait_ge(z_s, b + 1)
                    alone(v)
                    ch.sync()
                    xb = x_all[:, bass.ds(b * T, T), :]
                    v.tensor_tensor(xb, xb, z_y[r][:, 0, :, :], ALU.add).then_inc(z_x, 1)
                    ch.restart()

        block = ctx.enter_context(nc.Block())

        @block.sync
        def _(sp):
            setup_loads(sp)
            late_loads(sp)
            sp.wait_ge(s_split, 2)
            for k in range(3):
                sp.dma_start(b3[k:k + 1, :], bparts[:, k, :]).then_inc(s_b3, 16)
            attn0_loads(sp)
            sp.wait_ge(s_phase, 9)
            sp.wait_ge(s_sc, 16 * NT)
            sp.wait_ge(b_xu, 1 + B)
            ffn_sp(sp, 0, sorted0)
            y0_loads(sp)
            attn1_loads(sp)
            sp.wait_ge(s_phase, 18)
            sp.wait_ge(s_sc, 16 * NT * 3)
            ffn_sp(sp, 1, sorted1)
            last_sp(sp)

        @block.gpsimd
        def _(g):
            setup_pool(g)
            bias_pool(g)
            scatter_pool(g, 0, 0, sorted0)
            state_pool(g)
            g.wait_ge(s_sc, 16 * NT)
            ffn_pool(g, 0)
            attn1_init(g)
            scatter_pool(g, 1, 0, sorted1)
            ids1(g)
            scatter_pool(g, 1, 1, sorted1)
            ffn_pool(g, 1)

        @block.scalar
        def _(act):
            norm_act_root(act, 0)
            phase_end(act, 1)
            norm_act(act, 0)
            phase_end(act, 2)
            routing_act(act, 0)
            two_deep(act, feat_act)
            roots_act(act)
            states(act, state_act)
            phase_end(act, 3)
            ffn_act(act, 0)
            phase_end(act, 4)
            norm_act_root(act, 1)
            norm_act(act, 1)
            phase_end(act, 5)
            routing_act(act, 1)
            act.wait_ge(c_init, 1)
            attn1(act, attn1_act)
            phase_end(act, 6)
            ffn_act(act, 1)
            last_act(act)

        @block.vector
        def _(v):
            for s, n in [(s_lgu, 2), (s_tp, 2), (s_lg, 2), (s_xT2, 2), (s_cp, 2), (a_uqr, 2), (a_zqr, 2), (a_ukr, 2),
                         (a_nsu, 2), (a_nsq, 1), (a_red, 1), (b_w, 1), (b_xu, 1)] + [
                    (q, 1) for q in c_free + c_pfree + c_ofree]:
                v.sem_inc(s, n)
            v.wait_ge(s_x, 16 * B)
            norm_dve_stats(v, 0)
            setup_dve(v)
            phase_end(v, 1)
            norm_dve_rows(v, 0)
            phase_end(v, 2)
            routing_dve(v, 0)
            layer1_dve(v)
            v.wait_ge(s_bo, 1 + B)
            two_deep(v, feat_dve)
            roots_dve(v)
            states(v, state_dve)
            phase_end(v, 3)
            ffn_dve(v, 0)
            phase_end(v, 4)
            v.wait_ge(s_sc, 16 * NT)
            v.wait_ge(b_xu, 1 + B)
            norm_dve_stats(v, 1)
            norm_dve_rows(v, 1)
            phase_end(v, 5)
            routing_dve(v, 1)
            v.wait_ge(c_init, 1)
            attn1(v, attn1_dve)
            phase_end(v, 6)
            v.wait_ge(s_w3, 48)
            ffn_dve(v, 1)
            last_dve(v)

        @block.tensor
        def _(pe):
            setup_pe(pe)
            phase_end(pe, 1)
            norm_pe(pe, 0)
            phase_end(pe, 2)
            pe.wait_ge(s_const, 3)
            routing_pe(pe, 0)
            pe.wait_ge(s_b3, 48)
            pe.wait_ge(s_rt, 3)
            two_deep(pe, feat_pe)
            states(pe, state_pe)
            phase_end(pe, 3)
            pe.wait_ge(b_w, 1 + B)
            ffn_pe(pe, 0)
            phase_end(pe, 4)
            norm_pe(pe, 1)
            phase_end(pe, 5)
            routing_pe(pe, 1)
            pe.wait_ge(c_init, 1)
            attn1(pe, attn1_pe)
            phase_end(pe, 6)
            pe.wait_ge(s_w3, 48)
            ffn_pe(pe, 1)


_INS = ["L0_attn_x", "L0_attn_Wq", "L0_attn_bq", "L0_attn_Wk", "L0_attn_bk", "L0_attn_Wv", "L0_attn_bv",
        "L0_attn_Wo", "L0_attn_bo", "L0_attn_ln_g", "L0_attn_ln_b", "L0_ffn_router_w", "L0_ffn_router_b",
        "L0_ffn_expert_w", "L0_ffn_expert_b", "L1_attn_wq", "L1_attn_wk", "L1_attn_wv", "L1_attn_wgq",
        "L1_attn_wgk", "L1_attn_wgv", "L1_attn_r_out_w", "L1_attn_gate_local_w", "L1_attn_gate_remote_w",
        "L1_attn_w_out", "L1_ffn_gate_w", "L1_ffn_w1", "L1_ffn_b1", "L1_ffn_w2", "L1_ffn_b2"]


def kernel(**inputs):
    import numpy as np
    import concourse.bacc as bacc
    from concourse.bass_utils import run_bass_kernel_spmd

    nc = bacc.Bacc("TRN2", target_bir_lowering=False, num_devices=1)
    arrays, d = {}, {}
    for name in _INS:
        a = np.ascontiguousarray(inputs[name])
        arrays[f"in_{name}_dram"] = a
        d[name] = nc.dram_tensor(f"in_{name}_dram", a.shape, mybir.dt.from_np(a.dtype), kind="ExternalInput").ap()
    shape = inputs["L0_attn_x"].shape
    rows = shape[0] * shape[1]
    experts = inputs["L0_ffn_router_w"].shape[0]
    out = nc.dram_tensor("out_0_dram", shape, F32, kind="ExternalOutput").ap()
    sorted0 = nc.dram_tensor("sorted0", (rows + experts * P, shape[2] + 2), F32, kind="Internal").ap()
    sorted1 = nc.dram_tensor("sorted1", (2 * rows + experts * P, shape[2] + 2), F32, kind="Internal").ap()
    ydram = nc.dram_tensor("ydram", (2 * rows, shape[2]), F32, kind="Internal").ap()
    build(nc, d, out, sorted0, sorted1, ydram)
    r = run_bass_kernel_spmd(nc, [arrays], core_ids=[0])
    return r.results[0]["out_0_dram"]
```

```python
from contextlib import ExitStack

import concourse.bass as bass
from concourse import mybir

F32 = mybir.dt.float32
BF16 = mybir.dt.bfloat16
I32 = mybir.dt.int32
ALU = mybir.AluOpType
ACT = mybir.ActivationFunctionType
AX = mybir.AxisListType.X

P = 128
EPS = 1e-5
NEG = -1e30
BAD_ROW = 1 << 20


class Chain:

    def __init__(self, eng, sem):
        self.eng, self.sem, self.n = eng, sem, 0

    def after(self, ins):
        ins.then_inc(self.sem, 1)
        self.n += 1

    def sync(self):
        self.eng.wait_ge(self.sem, self.n)

    def link(self, ins):
        self.after(ins)
        self.sync()

    def restart(self):
        self.sync()
        self.eng.sem_clear(self.sem)
        self.n = 0


def build(nc, d, out, sorted0, sorted1, ydram):
    B, S, C = d["L0_attn_x"].shape
    E = d["L0_ffn_router_w"].shape[0]
    F = d["L1_ffn_w1"].shape[2]
    NK = d["L0_attn_Wk"].shape[0]
    LAT = d["L1_attn_wgq"].shape[1]
    H, LH, HD, W, NL = 16, 8, 8, 32, 64
    T = S // P
    NT = B * T
    FC = F // P
    ROW = C + 2
    NT0 = sorted0.shape[0] // P
    NT1 = sorted1.shape[0] // P
    NB = S // W
    G = 4
    HB = NB // 2
    SCORE = float(HD) ** -0.5
    assert C == P and NK == 2 and B % 2 == 0

    x_v = d["L0_attn_x"].rearrange("b (t p) c -> p (b t) c", p=P)
    out_v = out.rearrange("b (t p) c -> p (b t) c", p=P)
    y_v = ydram.rearrange("(k n p) c -> p k n c", p=P, k=2)

    ctx = ExitStack()
    with ctx:
        def sb(name, shape, dt=F32):
            return ctx.enter_context(nc.sbuf_tensor(name, shape, dt))

        def sem(name):
            return ctx.enter_context(nc.semaphore(name))

        x_all = sb("x_all", [P, NT, C])
        xr_all = sb("xr_all", [P, NT, ROW])
        xnT_all = sb("xnT_all", [C, NT * P])
        w2 = sb("w2", [P, E * FC, C])
        b1T = sb("b1T", [P, E * FC])
        b2_bc = sb("b2_bc", [P, E, C])
        mix0 = sb("mix0", [P, 2 * E * C])
        mix0_e = mix0[:, :].rearrange("p (e a c) -> p e a c", e=E, a=2)
        weT, eb_bc = mix0_e[:, :, 0, :], mix0_e[:, :, 1, :]
        pre_row = sb("pre_row", [P, ROW])[:, :]
        ident = sb("ident", [P, P])
        onesb = sb("onesb", [P, 512], BF16)
        lower = sb("lower", [P, P], BF16)
        block1 = sb("block1", [P, H])
        bmask = sb("bmask", [P, H, HD])
        head_m = sb("head_m", [P, G])
        gk_m = sb("gk_m", [64, H])
        row_m = sb("row_m", [P, G])
        pick = sb("pick", [P, W])
        selq = sb("selq", [P, G, W], BF16)
        selr = sb("selr", [P, P], BF16)
        lmask = sb("lmask", [P, 2, 2, 2 * W], BF16)
        gmask = sb("gmask", [P, T, NL], BF16)
        wqT = sb("wqT", [C, C])
        wkT = sb("wkT", [C, NK * C])
        wvT = sb("wvT", [C, NK, C])
        wog = sb("wog", [C, C])
        woT = sb("woT", [C, C])
        rwT = sb("rwT", [C, 2, E])
        ones_row = sb("ones_row", [1, P])[:, :]
        bo_bc = sb("bo_bc", [P, C])
        bv_bc = sb("bv_bc", [P, NK, C])
        rb_bc = sb("rb_bc", [P, E])
        lng = sb("lng", [C, 1])
        lnb = sb("lnb", [C, 1])
        bo_row = sb("bo_row", [1, C])
        bparts = sb("bparts", [1, 3, 3 * C], BF16)
        b3 = sb("b3", [3, 3 * C], BF16)
        wq1 = sb("wq1", [C, C])
        wk1 = sb("wk1", [C, C])
        wv1 = sb("wv1", [C, C])
        wgq = sb("wgq", [C, LAT])
        wgk = sb("wgk", [C, LAT])
        wgv = sb("wgv", [C, LAT])
        rout = sb("rout", [LAT, C])
        wout = sb("wout", [C, C])
        glr = sb("glr", [P, 2, C])
        wgate = sb("wgate", [C, 2, H, HD])
        wg16 = sb("wg16", [C, 2, H])
        lg = sb("lg", [P, NT, E])
        ex = sb("ex", [P, NT, E])
        ra = sb("ra", [P, NT, E])
        rc = sb("rc", [P, NT, E])
        rd = sb("rd", [P, NT, E])
        m1 = sb("m1", [P, NT, E])
        m2 = sb("m2", [P, NT, E])
        mb = sb("mb", [P, NT, E], BF16)
        top = sb("top", [P, NT])
        tie = sb("tie", [P, NT])
        den = sb("den", [P, NT])
        gate = sb("gate", [P, 2, NT])
        slotf = sb("slotf", [P, NT])
        slot = sb("slot", [P, 2, NT], I32)
        desc = sb("desc", [P, E])
        big_t = sb("big_t", [P, NT])
        kidx = sb("kidx", [P, NT1])
        cmp_ = sb("cmp_", [P, NT1 * E])
        cnt = sb("cnt", [P, E])
        ends = sb("ends", [P, E])
        endb = sb("endb", [P, E])
        kexp = sb("kexp", [P, NT1])
        expert = sb("expert", [P, 2, NT1], I32)
        st_all = sb("st_all", [P, NT, 6])
        mean = sb("mean", [P, NT])
        nq = sb("nq", [P, NT])
        st4 = sb("st4", [P, T, 6])
        mv4 = sb("mv4", [P, T, 2])
        rstd = sb("rstd", [P, NT])
        SPACE = 20620
        arena = sb("arena", [P, SPACE + E * F])
        w1 = arena[:, SPACE:SPACE + E * F].rearrange("p (e f) -> p e f", e=E)
        at, limit = [0], [SPACE]

        def start_views(n=0):
            at[0] = n

        def view(n, parts=P, dt=F32):
            a = arena[0:parts, at[0]:at[0] + n]
            at[0] += n
            assert at[0] <= limit[0], at[0]
            return a if dt == F32 else a.bitcast(dt)

        psum = ctx.enter_context(nc.psum_tensor("psum", [P, 8, 512], F32))

        s_x = sem("s_x")
        s_w = sem("s_w")
        s_w2 = sem("s_w2")
        s_w3 = sem("s_w3")
        s_b3 = sem("s_b3")
        s_const = sem("s_const")
        s_pool = sem("s_pool")
        s_pre = [sem(f"s_pre{n}") for n in range(2)]
        s_chain = sem("s_chain")
        s_achain = sem("s_achain")
        s_tr = sem("s_tr")
        s_trc = sem("s_trc")
        s_split = sem("s_split")
        s_phase = sem("s_phase")
        s_xn = sem("s_xn")
        s_tp = sem("s_tp")
        s_xT = sem("s_xT")
        s_lgu = sem("s_lgu")
        s_lg = sem("s_lg")
        s_cp = sem("s_cp")
        s_stat = sem("s_stat")
        s_root = sem("s_root")
        s_rt = sem("s_rt")
        s_rex = sem("s_rex")
        s_rps = sem("s_rps")
        s_slot = sem("s_slot")
        s_sc = sem("s_sc")
        s_bo = sem("s_bo")
        s_out = sem("s_out")

        s_alone = sem("s_alone")

        def alone(eng):
            eng.sem_inc(s_alone, 1)

        def phase_end(eng, n):
            eng.drain().then_inc(s_phase, 1)
            eng.wait_ge(s_phase, 3 * n)

        start_views()
        raw = view(6 * C).rearrange("p (n c) -> p n c", n=6)
        raw_e = view(E * C).rearrange("p (n c) -> p n c", n=E)
        raw_r = view(2 * C, parts=E).rearrange("p (n c) -> p n c", n=2)
        raw_b = view(P, parts=E * FC)
        brow = view(3 * C, parts=1)
        bres = view(3 * C, parts=1)
        N_W = 15

        def load_list(eng, sem_, pairs):
            for dst, src in pairs:
                eng.dma_start(dst, src).then_inc(sem_, 16)

        def setup_loads(sp):
            load_list(sp, s_w, [
                (raw[:, 0, :], d["L0_attn_Wq"]),
                (raw[:, 1:3, :], d["L0_attn_Wk"].rearrange("k o c -> o k c")),
                (raw[:, 3:5, :], d["L0_attn_Wv"].rearrange("k o c -> o k c")),
                (raw[:, 5, :], d["L0_attn_Wo"]),
                (raw_r[:, 0, :], d["L0_ffn_router_w"]),
                (raw_r[:, 1, :], d["L1_ffn_gate_w"]),
                (raw_e, d["L0_ffn_expert_w"].rearrange("e o c -> o e c")),
                (raw_b, d["L1_ffn_b1"].rearrange("e (j f) -> (e j) f", f=P)),
                (lng[:, :], d["L0_attn_ln_g"].rearrange("(c o) -> c o", o=1)),
                (lnb[:, :], d["L0_attn_ln_b"].rearrange("(c o) -> c o", o=1)),
                (bo_row[:, :], d["L0_attn_bo"].rearrange("(o c) -> o c", o=1)),
                (brow[:, 0:C], d["L0_attn_bq"].rearrange("(o c) -> o c", o=1)),
                (brow[:, C:3 * C], d["L0_attn_bk"].rearrange("(o k) c -> o (k c)", o=1)),
                (bv_bc[:, :, :], d["L0_attn_bv"].partition_broadcast(P)),
                (rb_bc[:, :], d["L0_ffn_router_b"].partition_broadcast(P))])
            for b in range(B):
                sp.dma_start(x_all[:, b * T:(b + 1) * T, :], x_v[:, b * T:(b + 1) * T, :]).then_inc(s_x, 16)

        N_W2 = 11

        def late_loads(sp):
            def prefill(dst, sem_):
                v = dst.rearrange("(n p) c -> p n c", p=P)
                sp.dma_start(v, pre_row.unsqueeze(1).to_broadcast([P, dst.shape[0] // P, ROW])).then_inc(sem_, 16)

            load_list(sp, s_w2, [
                (glr[:, 0, :], d["L1_attn_gate_local_w"].rearrange("h e -> (h e)").partition_broadcast(P)),
                (glr[:, 1, :], d["L1_attn_gate_remote_w"].rearrange("h e -> (h e)").partition_broadcast(P)),
                (wq1[:, :], d["L1_attn_wq"]),
                (wk1[:, :], d["L1_attn_wk"]),
                (wv1[:, :], d["L1_attn_wv"]),
                (wgq[:, :], d["L1_attn_wgq"]),
                (wgk[:, :], d["L1_attn_wgk"]),
                (wgv[:, :], d["L1_attn_wgv"]),
                (rout[:, :], d["L1_attn_r_out_w"]),
                (wout[:, :], d["L1_attn_w_out"]),
                (eb_bc, d["L0_ffn_expert_b"].partition_broadcast(P))])
            sp.wait_ge(s_const, 2)
            prefill(sorted0, s_pre[0])
            load_list(sp, s_w3, [
                (w2[:, :, :], d["L1_ffn_w2"].rearrange("e (j f) h -> f (e j) h", f=P)),
                (b2_bc[:, :, :], d["L1_ffn_b2"].partition_broadcast(P))])
            prefill(sorted1, s_pre[1])


        def setup_pool(g):
            ch = Chain(g, s_pool)
            ch.after(g.memset(ident[:, :], 0.0))
            ch.after(g.memset(onesb[:, :], 1.0))
            ch.after(g.memset(pre_row, 0.0))
            ch.after(g.memset(block1[:, :], 1.0))
            ch.after(g.memset(bmask[:, :, :], float(S) ** -2))
            ch.after(g.memset(row_m[:, :], 1.0))
            ch.after(g.memset(pick[:, :], 0.0))
            ch.after(g.memset(selq[:, :, :], 0.0))
            ch.after(g.memset(selr[:, :], 1.0))
            ch.after(g.memset(lmask[:, :, :, :], 0.0))
            ch.after(g.memset(gmask[:, :, :], 0.0))
            ch.after(g.memset(xr_all[:, :, C:C + 1], 1.0))
            ch.after(g.iota(xr_all[:, :, C + 1:C + 2].bitcast(I32), pattern=[[P, NT], [0, 1]], base=0,
                            channel_multiplier=1))
            ch.after(g.iota(desc[:, :], pattern=[[-1, E]], base=E, channel_multiplier=0,
                            allow_small_or_imprecise_dtypes=True))
            ch.after(g.iota(big_t[:, :], pattern=[[P, NT]], base=0, channel_multiplier=0,
                            allow_small_or_imprecise_dtypes=True))
            ch.after(g.iota(kidx[:, :], pattern=[[1, NT1]], base=0, channel_multiplier=0,
                            allow_small_or_imprecise_dtypes=True))
            ch.sync()

            def keep(view, pattern, base, mult, fill=0.0, op=ALU.is_ge):
                ch.link(g.affine_select(out=view, in_=view, compare_op=op, fill=fill, base=base, pattern=pattern,
                                        channel_multiplier=mult))

            keep(ident[:, :], [[-1, P]], 0, 1, 1.0, ALU.not_equal)
            ch.link(g.iota(pre_row[:, C + 1:C + 2].bitcast(I32), pattern=[[0, 1]], base=BAD_ROW,
                           channel_multiplier=1))
            g.memset(lower[:, :], 1.0).then_inc(s_const, 2)
            g.wait_ge(s_const, 2)
            keep(lower[:, :], [[1, P]], -1, -1)
            keep(block1[:, :], [[-HD, H]], 0, 1)
            keep(block1[:, :], [[HD, H]], HD - 1, -1)
            keep(bmask[:, :, :], [[-HD, H], [0, HD]], 0, 1)
            keep(bmask[:, :, :], [[HD, H], [0, HD]], HD - 1, -1)
            keep(row_m[:, :], [[-W, G]], 0, 1)
            keep(row_m[:, :], [[W, G]], W - 1, -1)
            for g4 in range(G):
                keep(pick[:, :], [[-1, W]], -W * g4, 1, 1.0, ALU.not_equal)
                keep(selq[:, :, :], [[0, G], [-1, W]], -W * g4, 1, 1.0, ALU.not_equal)
            keep(selr[:, :], [[1, P]], 0, -HD)
            keep(selr[:, :], [[-1, P]], HD - 1, HD)
            for g4 in range(G):
                q = lmask[W * g4:W * g4 + W, :, :, :]
                keep(q, [[0, 2], [0, 2], [1, 2 * W]], -1, -1, NEG)
                keep(q, [[0, 2], [0, 2], [-1, 2 * W]], W, 1, NEG)
                q0 = lmask[W * g4:W * g4 + W, 0, 0, :]
                keep(q0, [[1, 2 * W]], -W, 0, NEG)
            keep(gmask[:, :, :], [[P // HD, T], [-1, NL]], 0, 1, NEG)
            g.engine_nop().then_inc(s_const, 1)

        def setup_pe(pe):
            pe.wait_ge(s_const, 2)
            pe.wait_ge(s_w, 16 * N_W)
            for i in range(4):
                pe.transpose(psum[:, 0, i * C:(i + 1) * C], raw[:, i, :], ident[:, :])
            for i in range(2):
                mm = pe.transpose(psum[:, 1, i * C:(i + 1) * C], raw[:, 4 + i, :], ident[:, :])
            for i in range(2):
                pe.transpose(psum[:, 1, 2 * C + i * E:2 * C + (i + 1) * E], raw_r[:, i, :], ident[0:E, 0:E])
            mm = pe.transpose(psum[:, 1, 3 * C:3 * C + E * FC], raw_b, ident[0:E * FC, 0:E * FC])
            mm.then_inc(s_tr, 1)
            for e in range(E):
                mm = pe.transpose(psum[:, 2 + e // 4, (e % 4) * C:(e % 4 + 1) * C], raw_e[:, e, :], ident[:, :])
            mm.then_inc(s_tr, 1)
            pe.wait_ge(s_trc, 1)
            pe.matmul(psum[:, 4, 0:C], lnb[:, 0:1].to_broadcast([C, P]), woT[:, :], start=True, stop=False)
            pe.wait_ge(s_split, 1)
            pe.matmul(psum[:, 4, 0:C], ones_row, bo_row[:, :], start=False, stop=True).then_inc(s_tr, 1)


        def setup_dve(v):
            ch = Chain(v, s_chain)
            v.memset(ones_row, 1.0).then_inc(s_split, 1)
            v.wait_ge(s_w, 16 * N_W)
            v.wait_ge(s_tr, 1)
            ch.after(v.tensor_tensor(wqT[:, :], psum[:, 0, 0:C], ident[:, :], ALU.add))
            ch.after(v.tensor_tensor(wkT[:, :].rearrange("p (k c) -> p k c", k=NK),
                                     psum[:, 0, C:3 * C].rearrange("p (k c) -> p k c", k=NK),
                                     ident[:, :].unsqueeze(1).to_broadcast([P, NK, C]), ALU.add))
            ch.after(v.tensor_tensor(wvT[:, 0, :], psum[:, 0, 3 * C:4 * C], ident[:, :], ALU.add))
            ch.after(v.tensor_tensor(wvT[:, 1, :], psum[:, 1, 0:C], ident[:, :], ALU.add))
            ch.after(v.tensor_copy(rwT[:, :, :].rearrange("p a e -> p (a e)"), psum[:, 1, 2 * C:2 * C + 2 * E]))
            ch.after(v.tensor_scalar(wog[:, :], psum[:, 1, C:2 * C], lng[:, 0:1], None, ALU.mult))
            ch.after(v.tensor_copy(b1T[:, :], psum[:, 1, 3 * C:3 * C + E * FC]))
            v.tensor_copy(woT[:, :], psum[:, 1, C:2 * C]).then_inc(s_trc, 1)
            ch.sync()
            v.wait_ge(s_tr, 2)
            ch.after(v.tensor_copy(weT, psum[:, 2:4, :].rearrange("p a (b c) -> p (a b) c", c=C)))
            v.wait_ge(s_tr, 3)
            v.tensor_copy(bo_bc[:, :], psum[:, 4, 0:C]).then_inc(s_bo, 1)
            ch.restart()

        def layer1_dve(v):
            ch = Chain(v, s_chain)
            v.wait_ge(s_w2, 16 * N_W2)
            v.wait_ge(s_const, 3)
            ch.link(v.tensor_reduce(head_m[:, :], block1[:, :].rearrange("p (g h) -> p h g", g=G), AX, ALU.add))
            ch.after(v.tensor_scalar(head_m[:, :], head_m[:, :], SCORE, None, ALU.mult))
            ch.after(v.tensor_scalar(gk_m[:, :], block1[0:64, :], SCORE, None, ALU.mult))
            ch.after(v.tensor_scalar(wgk[:, :], wgk[:, :], NL / S, None, ALU.mult))
            ch.after(v.tensor_scalar(wgv[:, :], wgv[:, :], NL / S, None, ALU.mult))
            ch.after(v.tensor_scalar(wout[:, :], wout[:, :], 0.5, None, ALU.mult))
            ch.link(v.tensor_tensor(glr[:, :, :], glr[:, :, :], wq1[:, :].unsqueeze(1).to_broadcast([C, 2, C]),
                                    ALU.mult))
            ch.link(v.tensor_reduce(wg16[:, :, :], glr[:, :, :].rearrange("p a (h e) -> p a h e", e=HD), AX,
                                    ALU.add))
            ch.after(v.tensor_copy(wgate[:, :, :, :], wg16[:, :, :].unsqueeze(3).to_broadcast([C, 2, H, HD])))
            ch.restart()

        def batch(bt):
            return bt[0] + bt[1] * 2

        def two_deep(eng, stage):
            stage(eng, None, (0, 0))
            with eng.Fori(0, B // 2 - 1) as i:
                stage(eng, (0, i), (1, i))
                stage(eng, (1, i), (2, i))
            stage(eng, (B - 2, 0), (B - 1, 0))
            stage(eng, (B - 1, 0), None)

        def biases_dve(v):
            ch = Chain(v, s_chain)
            ch.link(v.tensor_copy(bparts[:, 0, :], brow[:, :]))
            ch.link(v.tensor_tensor(bres[:, :], brow[:, :], bparts[:, 0, :], ALU.subtract))
            ch.link(v.tensor_copy(bparts[:, 1, :], bres[:, :]))
            ch.link(v.tensor_tensor(bres[:, :], bres[:, :], bparts[:, 1, :], ALU.subtract))
            v.tensor_copy(bparts[:, 2, :], bres[:, :]).then_inc(s_split, 1)
            v.wait_ge(s_split, 2)
            ch.restart()

        start_views(8200)
        xns = [view(T * C).rearrange("p (t c) -> p t c", t=T) for _ in range(2)]
        xns_T = [view(T * P) for _ in range(2)]
        yl = [view(T * C).rearrange("p (t c) -> p t c", t=T) for _ in range(2)]
        s_yl = [sem(f"s_yl{r}") for r in range(2)]
        s_yu = sem("s_yu")

        s_xT2 = sem("s_xT2")
        s_rn = sem("s_rn")
        NP2 = B // 2

        def norm_dve(v, layer):
            def statistics(i):
                ch = Chain(v, s_chain)
                tiles = [i * 2 * T + t for t in range(2 * T)]
                if layer:
                    for t, n in enumerate(tiles):
                        if t % T == 0:
                            v.wait_ge(s_yl[t // T], 16 * (i + 1))
                        xt = x_all[:, bass.ds(n, 1), :].rearrange("p a c -> p (a c)")
                        ch.after(v.scalar_tensor_tensor(out=xt, in0=yl[t // T][:, t % T, :],
                                                        scalar=gate[:, 0, bass.ds(n, 1)], in1=xt,
                                                        op0=ALU.mult, op1=ALU.add))
                    ch.sync()
                    v.sem_inc(s_yu, 2)
                for n in tiles:
                    xt = x_all[:, bass.ds(n, 1), :].rearrange("p a c -> p (a c)")
                    ch.after(v.bn_stats(st_all[:, bass.ds(n, 1), :].rearrange("p a c -> p (a c)"), xt))
                ch.sync()
                me, qe, mo, qo = (st_all[:, bass.ds(i * 2 * T, 2 * T), k] for k in (1, 2, 4, 5))
                m, rs, q = (a[:, bass.ds(i * 2 * T, 2 * T)] for a in (mean, rstd, nq))
                ch.after(v.tensor_tensor(m, me, mo, ALU.add))
                ch.after(v.tensor_tensor(rs, me, mo, ALU.subtract))
                ch.link(v.tensor_tensor(q, qe, qo, ALU.add))
                ch.link(v.tensor_tensor(rs, rs, rs, ALU.mult))
                ch.link(v.scalar_tensor_tensor(out=rs, in0=rs, scalar=C / 4.0, in1=q, op0=ALU.mult, op1=ALU.add))
                v.tensor_scalar(rs, rs, 1.0 / C, EPS, ALU.mult, ALU.add).then_inc(s_stat, 1)
                ch.restart()

            def copies(i):
                for r in range(2):
                    b = i * 2 + r
                    v.wait_ge(s_xn, B * layer + b + 1)
                    v.tensor_copy(xr_all[:, bass.ds(b * T, T), 0:C], xns[r]).then_inc(s_cp, 1)

            def scales(i):
                ch = Chain(v, s_chain)
                m, rs = (a[:, bass.ds(i * 2 * T, 2 * T)] for a in (mean, rstd))
                v.wait_ge(s_root, NP2 * layer + i + 1)
                alone(v)
                ch.link(v.reciprocal(rs, rs))
                v.scalar_tensor_tensor(out=m, in0=m, scalar=-0.5, in1=rs, op0=ALU.mult,
                                       op1=ALU.mult).then_inc(s_rn, 1)
                ch.restart()

            statistics(0)
            scales(0)
            with v.Fori(1, NP2) as i:
                statistics(i)
                copies(i - 1)
                scales(i)
            copies(NP2 - 1)
            v.wait_ge(s_lg, B * (layer + 1) + 2)
            src = psum[:, 2, 0:NT * E].rearrange("p (t e) -> p t e", t=NT)
            if layer:
                v.tensor_copy(lg[:, :, :], src).then_inc(s_lgu, 1)
            else:
                v.tensor_tensor(lg[:, :, :], src, rb_bc[:, :].unsqueeze(1).to_broadcast([P, NT, E]),
                                ALU.add).then_inc(s_lgu, 1)

        def norm_pe(pe, layer):
            def stage(pe, prev, cur):
                if cur:
                    r = cur[0] % 2
                    k = batch(cur) + B * layer
                    pe.wait_ge(s_xn, k + 1)
                    pe.wait_ge(s_xT2, k + 1)
                    for t in range(T):
                        mm = pe.transpose(psum[:, r, t * P:(t + 1) * P], xns[r][:, t, :], ident[:, :])
                    mm.then_inc(s_tp, 1)
                if prev:
                    r = prev[0] % 2
                    b = batch(prev)
                    pe.wait_ge(s_xT, b + (B * layer + 1))
                    for t in range(T):
                        mm = pe.matmul(psum[:, 2, bass.ds(b * (T * E) + t * E, E)],
                                       xns_T[r][:, t * P:(t + 1) * P], rwT[:, layer, :], start=True, stop=True)
                    mm.then_inc(s_lg, 1)

            two_deep(pe, stage)

        def norm_act(act, layer):
            def roots(i):
                rs = rstd[:, bass.ds(i * 2 * T, 2 * T)]
                act.wait_ge(s_stat, i + (NP2 * layer + 1))
                act.activation(rs, rs, ACT.Sqrt).then_inc(s_root, 1)

            def rows(i):
                act.wait_ge(s_rn, i + (NP2 * layer + 1))
                for r in range(2):
                    b = i * 2 + r
                    k = b + B * layer
                    act.wait_ge(s_tp, k + 1)
                    act.wait_ge(s_cp, k + 1)
                    for t in range(T):
                        n = bass.ds(b * T + t, 1)
                        ins = act.activation(xns[r][:, t, :], x_all[:, n, :].rearrange("p a c -> p (a c)"),
                                             ACT.Identity, bias=mean[:, n], scale=rstd[:, n])
                    ins.then_inc(s_xn, 1)

            def channels(i):
                for r in range(2):
                    b = i * 2 + r
                    k = b + B * layer
                    act.wait_ge(s_tp, k + 3)
                    act.wait_ge(s_lg, k + 1)
                    act.activation(xns_T[r], psum[:, r, :], ACT.Copy).then_inc(s_xT, 1)
                    act.activation(xnT_all[:, bass.ds(b * S, S)], psum[:, r, :], ACT.Copy).then_inc(s_xT2, 1)

            roots(0)
            with act.Fori(0, NP2 - 1) as i:
                rows(i)
                roots(i + 1)
                channels(i)
            rows(NP2 - 1)
            channels(NP2 - 1)

        def bc_e(a):
            return a.unsqueeze(2).to_broadcast([P, NT, E])

        def routing_dve(v, layer):
            ch = Chain(v, s_chain)
            nt = NT1 if layer else NT0
            v.wait_ge(s_lgu, layer + 1)
            ch.link(v.tensor_reduce(top[:, :], lg[:, :, :], AX, ALU.max))
            ch.after(v.tensor_tensor(ra[:, :, :], lg[:, :, :], bc_e(top[:, :]), ALU.subtract))
            ch.sync()
            v.engine_nop().then_inc(s_rt, 1)

            def first_of(dst, src, peak):
                ch.link(v.tensor_tensor(rc[:, :, :], src, bc_e(peak), ALU.is_equal))
                ch.link(v.tensor_tensor(rc[:, :, :], rc[:, :, :],
                                        desc[:, :].unsqueeze(1).to_broadcast([P, NT, E]), ALU.mult))
                ch.link(v.tensor_reduce(tie[:, :], rc[:, :, :], AX, ALU.max))
                ch.link(v.tensor_tensor(dst, rc[:, :, :], bc_e(tie[:, :]), ALU.is_equal))

            first_of(m1[:, :, :], lg[:, :, :], top[:, :])
            mask = m1
            if layer:
                ch.link(v.tensor_scalar(rd[:, :, :], m1[:, :, :], NEG, None, ALU.mult))
                ch.link(v.tensor_tensor(rd[:, :, :], rd[:, :, :], lg[:, :, :], ALU.add))
                ch.link(v.tensor_reduce(top[:, :], rd[:, :, :], AX, ALU.max))
                first_of(m2[:, :, :], rd[:, :, :], top[:, :])
                ch.link(v.tensor_tensor(mb[:, :, :], m1[:, :, :], m2[:, :, :], ALU.add))
            else:
                ch.link(v.tensor_copy(mb[:, :, :], mask[:, :, :]))
            v.engine_nop().then_inc(s_rt, 1)
            v.wait_ge(s_rex, layer + 1)
            ch.link(v.tensor_reduce(den[:, :], ex[:, :, :], AX, ALU.add))
            ch.link(v.reciprocal(gate[:, 0, :], den[:, :]))
            if layer:
                ch.link(v.tensor_tensor(rc[:, :, :], ex[:, :, :], m2[:, :, :], ALU.mult))
                ch.link(v.tensor_reduce(tie[:, :], rc[:, :, :], AX, ALU.add))
                ch.link(v.tensor_tensor(gate[:, 1, :], tie[:, :], gate[:, 0, :], ALU.mult))
            v.wait_ge(s_rps, layer + 1)
            tot = psum[:, 5, 0:NT * E].rearrange("p (t e) -> p t e", t=NT)
            before = psum[:, 4, 0:NT * E].rearrange("p (t e) -> p t e", t=NT)
            ch.link(v.tensor_copy(ra[:, :, :], tot))
            src, dst = ra, rc
            step = 1
            while step < NT:
                ch.after(v.tensor_copy(dst[:, 0:step, :], src[:, 0:step, :]))
                ch.link(v.tensor_tensor(dst[:, step:NT, :], src[:, step:NT, :], src[:, 0:NT - step, :], ALU.add))
                src, dst = dst, src
                step *= 2
            ch.link(v.tensor_copy(cnt[:, :], src[:, NT - 1, :]))
            ch.link(v.tensor_tensor(rd[:, :, :], src[:, :, :], tot, ALU.subtract))
            ch.link(v.tensor_tensor(rd[:, :, :], rd[:, :, :], before, ALU.add))
            v.engine_nop().then_inc(s_rt, 1)
            c3 = cmp_[:, 0:E * NT].rearrange("p (e t) -> p e t", e=E)
            ch.link(v.tensor_tensor(c3, cnt[:, :].unsqueeze(2).to_broadcast([P, E, NT]),
                                    big_t[:, :].unsqueeze(1).to_broadcast([P, E, NT]), ALU.is_gt))
            ch.link(v.tensor_reduce(cnt[:, :], c3, AX, ALU.add))
            src2, dst2 = ends, endb
            ch.link(v.tensor_copy(src2[:, :], cnt[:, :]))
            step = 1
            while step < E:
                ch.after(v.tensor_copy(dst2[:, 0:step], src2[:, 0:step]))
                ch.link(v.tensor_tensor(dst2[:, step:E], src2[:, step:E], src2[:, 0:E - step], ALU.add))
                src2, dst2 = dst2, src2
                step *= 2
            ch.link(v.tensor_tensor(dst2[:, :], src2[:, :], cnt[:, :], ALU.subtract))
            ch.link(v.tensor_scalar(dst2[:, :], dst2[:, :], float(P), None, ALU.mult))
            ch.link(v.tensor_tensor(rd[:, :, :], rd[:, :, :], dst2[:, :].unsqueeze(1).to_broadcast([P, NT, E]),
                                    ALU.add))
            for c, m in ((0, m1), (1, m2))[:layer + 1]:
                ch.link(v.tensor_tensor(rc[:, :, :], rd[:, :, :], m[:, :, :], ALU.mult))
                ch.link(v.tensor_reduce(slotf[:, :], rc[:, :, :], AX, ALU.add))
                ch.link(v.tensor_copy(slot[:, c, :], slotf[:, :]))
            c4 = cmp_[:, 0:nt * E].rearrange("p (k e) -> p k e", e=E)
            ch.link(v.tensor_tensor(c4, kidx[:, 0:nt].unsqueeze(2).to_broadcast([P, nt, E]),
                                    src2[:, :].unsqueeze(1).to_broadcast([P, nt, E]), ALU.is_ge))
            ch.link(v.tensor_reduce(kexp[:, 0:nt], c4, AX, ALU.add))
            ch.link(v.tensor_scalar(expert[:, layer, 0:nt], kexp[:, 0:nt], float(E - 1), None, ALU.min))
            ch.restart()
            v.engine_nop().then_inc(s_slot, 1)

        def routing_act(act, layer):
            act.wait_ge(s_rt, 3 * layer + 1)
            act.activation(ex[:, :, :], ra[:, :, :], ACT.Exp).then_inc(s_rex, 1)

        def routing_pe(pe, layer):
            pe.wait_ge(s_rt, 3 * layer + 2)
            m = mb[:, :, :].rearrange("p t e -> p (t e)")
            pe.matmul(psum[:, 4, 0:NT * E], lower[:, :], m, start=True, stop=True)
            pe.matmul(psum[:, 5, 0:NT * E], onesb[:, 0:P], m, start=True, stop=True).then_inc(s_rps, 1)

        def scatter_pool(g, layer, choice, dst):
            g.wait_ge(s_slot, layer + 1)
            g.wait_ge(s_cp, B * (layer + 1) + 2)
            g.wait_ge(s_pre[layer], 16)
            for t in range(NT):
                g.indirect_dma_start(out=dst, out_offset=bass.IndirectOffsetOnAxis(ap=slot[:, choice, t:t + 1], axis=0),
                                     in_=xr_all[:, t, :], in_offset=None, bounds_check=dst.shape[0] - 1,
                                     oob_is_err=False).then_inc(s_sc, 16)

        NKN = T * NK * H
        NQN = T * H
        NN = NKN + NQN
        NG = C + 1
        limit[0] = SPACE + E * F
        start_views()
        a_uk = view(B * 2 * S)
        a_zqs = view(B * S)
        a_nn = view(B * NN)
        both = at[0]
        a_xT = [view(S) for _ in range(2)]
        a_uq = [view(S) for _ in range(2)]
        a_tk = [view(2 * S) for _ in range(2)]
        a_sq = [view(S) for _ in range(2)]
        a_k2 = view(2 * S)
        start_views(both)
        a_kh = [view(2 * S).rearrange("p (t k c) -> p t k c", t=T, k=NK) for _ in range(2)]
        a_zq = [view(S) for _ in range(2)]
        a_G = view(2 * NG).rearrange("p (k c) -> p k c", k=NK)
        a_GT = view(2 * C).rearrange("p (k c) -> p k c", k=NK)
        a_s = view(2 * C).rearrange("p (k c) -> p k c", k=NK)
        a_bd = view(C)
        a_on = view(S).rearrange("p (t c) -> p t c", t=T)
        a_oT = view(S)
        a_w = view(S)
        g_x = [view(4 * ROW).rearrange("p (j c) -> p j c", j=4) for _ in range(2)]
        g_y = view(4 * C).rearrange("p (j c) -> p j c", j=4)
        g_xT = view(4 * P)
        g_w = [view(8 * C).rearrange("p (j a c) -> p j a c", j=4, a=2) for _ in range(2)]
        a_o = [view(S).rearrange("p (t c) -> p t c", t=T) for _ in range(2)]
        limit[0] = SPACE
        small = [cmp_[:, k:k + n] for k, n in ((0, NKN), (NKN, NQN), (NKN + NQN, NQN), (NKN + 2 * NQN, T),
                                               (NKN + 2 * NQN + T, T), (NKN + 2 * NQN + 2 * T, T))]
        a_kn, a_rq, a_ve, a_rl, a_nb = small[0], small[1:3], small[3], small[4], small[5]
        a_ld = [sem(f"a_ld{r}") for r in range(2)]
        b_ld = [sem(f"b_ld{r}") for r in range(2)]
        (a_q, a_tqr, a_uqr, a_zqr, a_sqr, a_nsq, a_nsu, a_k, a_tkr, a_ukr, a_k2r, a_red, a_root, b_all) = (
            sem(n) for n in ("a_q a_tqr a_uqr a_zqr a_sqr a_nsq a_nsu a_k a_tkr a_ukr a_k2r a_red a_root "
                             "b_all").split())
        (b_kh, b_g, b_gs, b_gt, b_gts, b_st, b_bd, b_out, b_ve, b_sq, b_rl, b_on, b_oTp, b_oTs, b_wo, b_w, b_xu) = (
            sem(n) for n in ("b_kh b_g b_gs b_gt b_gts b_st b_bd b_out b_ve b_sq b_rl b_on b_oTp b_oTs b_wo "
                             "b_w b_xu").split())

        (g_xTp, g_xTr, g_yp, g_yr) = (sem(n) for n in "g_xTp g_xTr g_yp g_yr".split())
        g_ld = [sem(f"g_ld{r}") for r in range(2)]
        g_id = [sb(f"g_id{r}", [P, 4], I32) for r in range(2)]
        g_idr = sem("g_idr")
        g_wl = [sem(f"g_wl{r}") for r in range(2)]
        g_sc = [sem(f"g_sc{r}") for r in range(2)]
        NGR = NT0 // 4
        assert NGR == B + 2

        def attn0_loads(sp):
            sp.wait_ge(s_phase, 6)
            for b in range(B):
                if b >= 2:
                    sp.wait_ge(a_k, b - 1)
                sp.dma_start(a_xT[b % 2], xnT_all[:, b * S:(b + 1) * S]).then_inc(a_ld[b % 2], 16)
            sp.wait_ge(b_all, 1)
            for b in range(B):
                if b >= 2:
                    sp.wait_ge(b_out, b - 1)
                sp.dma_start(a_zq[b % 2], a_zqs[:, b * S:(b + 1) * S]).then_inc(b_ld[b % 2], 16)
                if b == 0:
                    sp.wait_ge(s_sc, 16 * NT)
                    group_load(sp, 0)
                    group_load(sp, 1)
                else:
                    group_load(sp, b + 1)
            group_load(sp, B + 1)

        def group_load(sp, g):
            if g >= 2:
                sp.wait_ge(g_xTp, g - 1)
                sp.wait_ge(g_idr, g - 1)
            sp.dma_start(g_x[g % 2], sorted0.rearrange("(n p) c -> p n c", p=P)[:, 4 * g:4 * g + 4, :]).then_inc(
                g_ld[g % 2], 16)
            if g >= 2:
                sp.wait_ge(g_yp, g - 1)
            for j in range(4):
                e = sp.value_load(expert[0:1, 0, 4 * g + j:4 * g + j + 1], min_val=0, max_val=E - 1)
                sp.dma_start(g_w[g % 2][:, j, :, :].rearrange("p a c -> p (a c)"),
                             mix0_e[:, bass.ds(e, 1), :, :].rearrange("p o a c -> p (o a c)")).then_inc(
                    g_wl[g % 2], 16)

        def before(grp):
            return (grp[0] - 1, grp[1]) if grp[0] else None

        def uses(bt):
            return bt[1] + bt[0] // 2

        def group_pe_transposes(pe, grp):
            r = grp[0] % 2
            pe.wait_ge(g_ld[r], (uses(grp) + 1) * 16)
            alone(pe)
            for j in range(4):
                mm = pe.transpose(psum[:, 1, j * P:(j + 1) * P], g_x[r][:, j, 0:C], ident[:, :])
            mm.then_inc(g_xTp, 1)

        def group_pe_products(pe, grp):
            r = grp[0] % 2
            pe.wait_ge(g_wl[r], (uses(grp) + 1) * 64)
            alone(pe)
            pe.wait_ge(g_xTr, batch(grp) + 1)
            alone(pe)
            pe.wait_ge(g_yr, batch(grp) + 1)
            alone(pe)
            for j in range(4):
                pe.matmul(psum[:, 3, j * C:(j + 1) * C], g_xT[:, j * P:(j + 1) * P], g_w[r][:, j, 0, :], start=True,
                          stop=False)
                mm = pe.matmul(psum[:, 3, j * C:(j + 1) * C], ones_row, g_w[r][0:1, j, 1, :],
                               start=False, stop=True)
            mm.then_inc(g_yp, 1)

        def group_act(act, grp):
            act.wait_ge(g_xTp, batch(grp) + 1)
            act.activation(g_xT, psum[:, 1, :], ACT.Copy).then_inc(g_xTr, 1)

        def group_numbers(v, grp):
            r = grp[0] % 2
            v.wait_ge(g_ld[r], (uses(grp) + 1) * 16)
            alone(v)
            if grp[0] >= 2:
                v.wait_ge(g_sc[r], uses(grp) * 64)
                alone(v)
            v.tensor_copy(g_id[r][:, :].unsqueeze(2), g_x[r][:, :, C + 1:C + 2].bitcast(I32)).then_inc(g_idr, 1)

        def group_results(act, grp):
            r = grp[0] % 2
            act.wait_ge(g_yp, batch(grp) + 1)
            last = (grp[0] - 1, grp[1])
            if grp[0] >= 1:
                act.wait_ge(g_sc[1 - r], (uses(last) + 1) * 64)
            act.activation(g_y.rearrange("p j c -> p (j c)"), psum[:, 3, :], ACT.Copy).then_inc(g_yr, 1)

        def group_pool(g, grp):
            r = grp[0] % 2
            g.wait_ge(g_idr, batch(grp) + 1)
            alone(g)
            g.wait_ge(g_yr, batch(grp) + 2)
            alone(g)
            for j in range(4):
                g.indirect_dma_start(out=ydram, out_offset=bass.IndirectOffsetOnAxis(
                    ap=g_id[r][:, j:j + 1], axis=0), in_=g_y[:, j, :], in_offset=None,
                    bounds_check=ydram.shape[0] - 1, oob_is_err=False).then_inc(g_sc[r], 16)

        def feat_pe(pe, prev, cur):
            if cur:
                b, r = batch(cur), cur[0] % 2
                pe.wait_ge(a_ld[r], (cur[1] + (cur[0] // 2 + 1)) * 16)
                pe.wait_ge(a_uqr, b + 1)
                pe.matmul(psum[:, r, :], b3[:, 0:C], onesb[0:3, :], start=True, stop=False)
                pe.matmul(psum[:, r, :], wqT[:, :], a_xT[r], start=False, stop=True).then_inc(a_q, 1)
                pe.wait_ge(a_ukr, b + 1)
                for t in range(T):
                    o = psum[:, 2 + 2 * r + t // 2, (t % 2) * 2 * C:(t % 2 + 1) * 2 * C]
                    pe.matmul(o, onesb[0:3, 0:P], b3[:, C:3 * C], start=True, stop=False)
                    mm = pe.matmul(o, a_xT[r][:, t * P:(t + 1) * P], wkT[:, :], start=False, stop=True)
                mm.then_inc(a_k, 1)
            if prev:
                b, r = batch(prev), prev[0] % 2
                pe.wait_ge(a_sqr, b + 1)
                pe.wait_ge(a_nsu, b + 1)
                for t in range(T):
                    mm = pe.matmul(psum[:, 6 + r, t * H:(t + 1) * H], a_sq[r][:, t * P:(t + 1) * P],
                                   block1[:, :], start=True, stop=True)
                mm.then_inc(a_nsq, 1)

        def keys_psum(r):
            return psum[:, 2 + 2 * r:4 + 2 * r, :].rearrange("p a c -> p (a c)")

        def feat_act(act, prev, cur):
            if cur:
                b, r = batch(cur), cur[0] % 2
                act.wait_ge(a_q, b + 1)
                act.wait_ge(a_zqr, b + 1)
                act.activation(a_uq[r], psum[:, r, :], ACT.Tanh, scale=0.5).then_inc(a_tqr, 1)
                act.wait_ge(a_k, b + 1)
                act.wait_ge(a_ukr, b + 1)
                act.activation(a_tk[r], keys_psum(r), ACT.Tanh, scale=0.5).then_inc(a_tkr, 1)
            if prev:
                b = batch(prev)
                act.wait_ge(a_ukr, b + 3)
                act.wait_ge(a_red, b + 1)
                act.activation(a_k2, a_uk[:, bass.ds(b * 2 * S, 2 * S)], ACT.Square, bias=1.0).then_inc(a_k2r, 1)
            if cur:
                b, r = batch(cur), cur[0] % 2
                act.wait_ge(a_uqr, b + 3)
                act.wait_ge(a_nsq, b)
                act.activation(a_sq[r], a_uq[r], ACT.Square, bias=1.0).then_inc(a_sqr, 1)

        def feat_dve(v, prev, cur):
            if cur:
                b, r = batch(cur), cur[0] % 2
                v.wait_ge(a_tqr, b + 1)
                v.scalar_tensor_tensor(out=a_uq[r], in0=a_uq[r], scalar=1.0, in1=psum[:, r, :], op0=ALU.add,
                                       op1=ALU.mult).then_inc(a_uqr, 1)
                v.wait_ge(a_uqr, b + 3)
                v.tensor_scalar(a_zqs[:, bass.ds(b * S, S)], a_uq[r], 1.0, None, ALU.add).then_inc(a_zqr, 1)
                v.wait_ge(a_tkr, b + 1)
                v.scalar_tensor_tensor(out=a_uk[:, bass.ds(b * 2 * S, 2 * S)], in0=a_tk[r], scalar=1.0,
                                       in1=keys_psum(r), op0=ALU.add, op1=ALU.mult).then_inc(a_ukr, 1)
            if prev:
                b, r = batch(prev), prev[0] % 2
                v.wait_ge(a_k2r, b + 1)
                v.tensor_reduce(a_nn[:, bass.ds(b * NN, NKN)], a_k2.rearrange("p (n e) -> p n e", e=HD), AX,
                                ALU.add).then_inc(a_red, 1)
                v.wait_ge(a_nsq, b + 2)
                v.tensor_copy(a_nn[:, bass.ds(b * NN + NKN, NQN)], psum[:, 6 + r, 0:NQN]).then_inc(a_nsu, 1)

        def roots_act(act):
            act.wait_ge(a_red, 1 + B)
            act.wait_ge(a_nsu, 2 + B)
            act.activation(a_nn, a_nn, ACT.Sqrt).then_inc(a_root, 1)

        def roots_dve(v):
            v.wait_ge(a_root, 1)
            v.tensor_scalar(a_nn, a_nn, 2e-6, None, ALU.add).then_inc(a_root, 1)
            v.wait_ge(a_root, 2)
            v.wait_ge(a_zqr, 2 + B)
            v.wait_ge(a_sqr, B)
            v.sem_inc(b_all, 1)

        def state_pe(pe, three, two, one, grp):
            if two:
                b, r = batch(two), two[0] % 2
                pe.wait_ge(b_gs, b + 1)
                for k in range(NK):
                    mm = pe.transpose(psum[:, 2, k * C:(k + 1) * C], a_G[:, k, 0:C], ident[:, :])
                mm.then_inc(b_gt, 1)
                pe.wait_ge(b_gts, b + 1)
                for k in range(NK):
                    mm = pe.matmul(psum[:, 2, 2 * C + k * C:2 * C + (k + 1) * C], a_GT[:, k, :], wvT[:, k, :],
                                   start=True, stop=True)
                mm.then_inc(b_st, 1)
            if before(grp):
                group_pe_products(pe, before(grp))
            if three:
                b = batch(three)
                pe.wait_ge(b_on, b + 1)
                for t in range(T):
                    mm = pe.transpose(psum[:, 6, t * P:(t + 1) * P], a_on[:, t, :], ident[:, :])
                mm.then_inc(b_oTp, 1)
            if two:
                b, r = batch(two), two[0] % 2
                pe.wait_ge(b_bd, b + 1)
                alone(pe)
                pe.wait_ge(b_ld[r], (two[1] + (two[0] // 2 + 1)) * 16)
                for t in range(T):
                    mm = pe.matmul(psum[:, 4, t * C:(t + 1) * C], a_zq[r][:, t * P:(t + 1) * P],
                                   a_bd, start=True, stop=True)
                mm.then_inc(b_out, 1)
            if three:
                group_pe_transposes(pe, grp)
                b = batch(three)
                pe.wait_ge(b_oTs, b + 1)
                pe.wait_ge(b_w, b + 1)
                for t in range(T):
                    mm = pe.matmul(psum[:, 7, t * C:(t + 1) * C], a_oT[:, t * P:(t + 1) * P], wog[:, :],
                                   start=True, stop=True)
                mm.then_inc(b_wo, 1)
            if one:
                b, r = batch(one), one[0] % 2
                pe.wait_ge(b_kh, b + 1)
                for k in range(NK):
                    for t in range(T):
                        mm = pe.matmul(psum[:, 0, k * NG:(k + 1) * NG], a_kh[r][:, t, k, :],
                                       xr_all[:, bass.ds(b * T + t, 1), 0:NG].rearrange("p a c -> p (a c)"),
                                       start=(t == 0), stop=(t == T - 1))
                mm.then_inc(b_g, 1)
            if not three:
                group_pe_transposes(pe, grp)

        def state_act(act, three, two, one, grp):
            if two:
                b, r = batch(two), two[0] % 2
                act.wait_ge(b_gt, b + 1)
                act.activation(a_GT.rearrange("p k c -> p (k c)"), psum[:, 2, 0:2 * C],
                               ACT.Copy).then_inc(b_gts, 1)
            if three:
                b, r = batch(three), three[0] % 2
                act.wait_ge(b_rl, b + 1)
                for t in range(T):
                    ins = act.activation(a_on[:, t, :], a_o[r][:, t, :], ACT.Identity, bias=a_nb[:, t:t + 1],
                                         scale=a_rl[:, t:t + 1])
                ins.then_inc(b_on, 1)
                act.wait_ge(b_oTp, b + 1)
                act.activation(a_oT, psum[:, 6, :], ACT.Copy).then_inc(b_oTs, 1)
                group_act(act, grp)
            if three:
                b = batch(three)
                act.wait_ge(b_wo, b + 1)
                act.wait_ge(b_xu, b + 1)
                act.activation(a_w, psum[:, 7, :], ACT.Copy).then_inc(b_w, 1)
            if one:
                b, r = batch(one), one[0] % 2
                act.wait_ge(b_g, b + 1)
                act.activation(a_G.rearrange("p k c -> p (k c)"), psum[:, 0, 0:2 * NG],
                               ACT.Copy).then_inc(b_gs, 1)
            if two:
                b = batch(two)
                act.wait_ge(b_ve, b + 1)
                act.activation(a_ve[:, :], a_ve[:, :], ACT.Sqrt).then_inc(b_sq, 1)
            if not three:
                group_act(act, grp)
            if before(grp):
                group_results(act, before(grp))

        def state_dve(v, three, two, one, grp):
            ch = Chain(v, s_chain)
            if three:
                v.wait_ge(b_sq, batch(three) + 1)
                ch.link(v.reciprocal(a_rl[:, :], a_ve[:, :]))
                v.scalar_tensor_tensor(out=a_nb[:, :], in0=mv4[:, :, 0], scalar=-1.0, in1=a_rl[:, :], op0=ALU.mult,
                                       op1=ALU.mult).then_inc(b_rl, 1)
                v.wait_ge(b_rl, batch(three) + 1)
            if one:
                b, r = batch(one), one[0] % 2
                ch.after(v.reciprocal(a_kn[:, :], a_nn[:, bass.ds(b * NN, NKN)]))
                ch.after(v.reciprocal(a_rq[r][:, :], a_nn[:, bass.ds(b * NN + NKN, NQN)]))
            if two:
                b, r = batch(two), two[0] % 2
                v.wait_ge(b_st, b + 1)
                for k in range(NK):
                    ch.after(v.scalar_tensor_tensor(out=a_s[:, k, :], in0=bv_bc[:, k, :],
                                                    scalar=a_G[:, k, C:C + 1],
                                                    in1=psum[:, 2, 2 * C + k * C:2 * C + (k + 1) * C],
                                                    op0=ALU.mult, op1=ALU.add))
                ch.sync()
                ch.link(v.tensor_tensor(a_s[:, 0, :], a_s[:, 0, :], a_s[:, 1, :], ALU.mult))
                v.tensor_tensor(a_bd, a_s[:, 0, :], bmask[:, :, :].rearrange("p h e -> p (h e)"),
                                ALU.mult).then_inc(b_bd, 1)
                v.wait_ge(b_bd, b + 1)
            alone(v)
            ch.sync()
            if one:
                b, r = batch(one), one[0] % 2
                v.scalar_tensor_tensor(out=a_kh[r].rearrange("p t k (h e) -> p (t k h) e", e=HD),
                                       in0=a_uk[:, bass.ds(b * 2 * S, 2 * S)].rearrange("p (n e) -> p n e", e=HD),
                                       scalar=1.0, in1=a_kn[:, :].unsqueeze(2).to_broadcast([P, NKN, HD]),
                                       op0=ALU.add, op1=ALU.mult).then_inc(b_kh, 1)
                v.wait_ge(b_kh, b + 1)
            if two:
                b, r = batch(two), two[0] % 2
                v.wait_ge(b_out, b + 1)
                ch.link(v.tensor_tensor(a_o[r].rearrange("p t (h e) -> p (t h) e", e=HD),
                                        psum[:, 4, :].rearrange("p (h e) -> p h e", e=HD),
                                        a_rq[r][:, :].unsqueeze(2).to_broadcast([P, T * H, HD]), ALU.mult))
                for t in range(T):
                    ch.after(v.bn_stats(st4[:, t, :], a_o[r][:, t, :]))
                ch.sync()
                for t in range(T):
                    ch.after(v.bn_aggr(mv4[:, t, :], st4[:, t, :]))
                ch.sync()
                v.tensor_scalar(a_ve[:, :], mv4[:, :, 1], EPS, None, ALU.add).then_inc(b_ve, 1)
            alone(v)
            ch.restart()
            group_numbers(v, grp)

        def state_pool(g, three, two, one, grp):
            if three:
                b = batch(three)
                g.wait_ge(b_w, b + 2)
                alone(g)
                xb = x_all[:, bass.ds(b * T, T), :]
                g.tensor_tensor(xb, xb, a_w.rearrange("p (t c) -> p t c", t=T), ALU.add).then_inc(b_xu, 1)
            if before(grp):
                group_pool(g, before(grp))

        def states(eng, stage):
            stage(eng, None, None, (0, 0), (0, 0))
            stage(eng, None, (0, 0), (1, 0), (1, 0))
            with eng.Fori(0, B // 2 - 1) as i:
                stage(eng, (0, i), (1, i), (2, i), (2, i))
                stage(eng, (1, i), (2, i), (3, i), (3, i))
            stage(eng, (B - 2, 0), (B - 1, 0), None, (B, 0))
            stage(eng, (B - 1, 0), None, None, (B + 1, 0))

        def bias_pool(g):
            g.wait_ge(s_bo, 1)
            g.wait_ge(s_phase, 6)
            with g.Fori(0, B) as b:
                xb = x_all[:, bass.ds(b * T, T), :]
                g.tensor_tensor(xb, xb, bo_bc[:, :].unsqueeze(1).to_broadcast([P, T, C]), ALU.add).then_inc(s_bo, 1)

        start_views()
        RING = 8
        f_x = [view(ROW) for _ in range(RING)]
        f_y = [view(C) for _ in range(RING)]
        f_xT = [view(P) for _ in range(2)]
        f_w1 = [view(F) for _ in range(4)]
        f_hT = [view(F) for _ in range(4)]
        f_xTp, f_xTr, f_hp, f_hTr, f_yp, f_yr = (sem(n) for n in "f_xTp f_xTr f_hp f_hTr f_yp f_yr".split())
        f_ld = [sem(f"f_ld{r}") for r in range(RING)]
        f_sc = [sem(f"f_sc{r}") for r in range(RING)]
        f_w = [sem(f"f_w{r}") for r in range(4)]

        def steps(eng, lead, lag, step):
            for k in range(-lead, RING):
                step(k, 0, k)
            with eng.Fori(1, NT1 // RING - 1) as i:
                for r in range(RING):
                    step(i * RING + r, i, r)
            for k in range(NT1 - RING, NT1 + lag):
                step(k, NT1 // RING - 1, k - (NT1 - RING))

        def tile(k, i, r, off):
            if isinstance(k, int) and not 0 <= k + off < NT1:
                return None
            r += off
            return k + off, i + r // RING, r % RING

        def expert_of(eng, k):
            return eng.value_load(expert[0:1, 1, bass.ds(k, 1)], min_val=0, max_val=E - 1)

        def ffn_sp(sp):
            sv = sorted1.rearrange("(n p) c -> p n c", p=P)

            def step(k, i, r):
                t = tile(k, i, r, -1)
                if t:
                    n, u, rr = t
                    e = expert_of(sp, n)
                    if not (isinstance(n, int) and n < 4):
                        sp.wait_ge(f_hp, n - 3)
                        alone(sp)
                    sp.dma_start(f_w1[rr % 4], w1[:, bass.ds(e, 1), :].rearrange("p a f -> p (a f)")).then_inc(
                        f_w[rr % 4], 16)
                t = tile(k, i, r, 0)
                if t:
                    n, u, rr = t
                    if not (isinstance(u, int) and u == 0):
                        sp.wait_ge(f_sc[rr], u * 16)
                        alone(sp)
                        sp.wait_ge(f_xTp, n - (RING - 1))
                        alone(sp)
                    sp.dma_start(f_x[rr], sv[:, bass.ds(n, 1), :].rearrange("p a c -> p (a c)")).then_inc(
                        f_ld[rr], 16)

            steps(sp, 0, 1, step)

        def ffn_pe(pe):
            def step(k, i, r):
                t = tile(k, i, r, 1)
                if t:
                    n, u, rr = t
                    pe.wait_ge(f_ld[rr], (u + 1) * 16)
                    pe.transpose(psum[:, rr % 2, 0:P], f_x[rr][:, 0:C], ident[:, :]).then_inc(f_xTp, 1)
                t = tile(k, i, r, 0)
                if t:
                    n, u, rr = t
                    pe.wait_ge(f_xTr, n + 1)
                    pe.wait_ge(f_w[rr % 4], (u * 2 + (rr // 4 + 1)) * 16)
                    for j in range(FC):
                        mm = pe.matmul(psum[:, 2 + rr % 2, j * P:(j + 1) * P], f_w1[rr % 4][:, j * P:(j + 1) * P],
                                       f_xT[rr % 2], start=True, stop=True)
                    mm.then_inc(f_hp, 1)
                t = tile(k, i, r, -2)
                if t:
                    n, u, rr = t
                    e = expert_of(pe, n)
                    pe.wait_ge(f_hTr, n + 1)
                    if not (isinstance(n, int) and n < 2):
                        pe.wait_ge(f_yr, n - 1)
                    for j in range(FC):
                        mm = pe.matmul(psum[:, 6 + rr % 2, 0:C], f_hT[rr % 4][:, j * P:(j + 1) * P],
                                       w2[:, bass.ds(e * FC + j, 1), :].rearrange("p a f -> p (a f)"),
                                       start=(j == 0), stop=(j == FC - 1))
                    mm.then_inc(f_yp, 1)

            steps(pe, 1, 2, step)

        def ffn_act(act):
            def step(k, i, r):
                t = tile(k, i, r, 1)
                if t:
                    n, u, rr = t
                    act.wait_ge(f_xTp, n + 1)
                    act.activation(f_xT[rr % 2], psum[:, rr % 2, 0:P], ACT.Copy).then_inc(f_xTr, 1)
                t = tile(k, i, r, 0)
                if t:
                    n, u, rr = t
                    e = expert_of(act, n)
                    act.wait_ge(f_hp, n + 1)
                    for j in range(FC):
                        ins = act.activation(f_hT[rr % 4][:, j * P:(j + 1) * P],
                                             psum[:, 2 + rr % 2, j * P:(j + 1) * P], ACT.Relu,
                                             bias=b1T[:, bass.ds(e * FC + j, 1)])
                    ins.then_inc(f_hTr, 1)

            steps(act, 1, 0, step)

        def ffn_dve(v):
            def step(k, i, r):
                t = tile(k, i, r, -2)
                if t:
                    n, u, rr = t
                    e = expert_of(v, n)
                    v.wait_ge(f_yp, n + 1)
                    if not (isinstance(u, int) and u == 0):
                        v.wait_ge(f_sc[rr], u * 16)
                    v.tensor_tensor(f_y[rr], psum[:, 6 + rr % 2, 0:C],
                                    b2_bc[:, bass.ds(e, 1), :].rearrange("p a f -> p (a f)"),
                                    ALU.add).then_inc(f_yr, 1)

            steps(v, 0, 2, step)

        def ffn_pool(g):
            def step(k, i, r):
                t = tile(k, i, r, 0)
                if t:
                    n, u, rr = t
                    g.wait_ge(f_yr, n + 1)
                    alone(g)
                    g.indirect_dma_start(out=ydram, out_offset=bass.IndirectOffsetOnAxis(
                        ap=f_x[rr][:, C + 1:C + 2].bitcast(I32), axis=0), in_=f_y[rr], in_offset=None,
                        bounds_check=ydram.shape[0] - 1, oob_is_err=False).then_inc(f_sc[rr], 16)

            steps(g, 0, 0, step)

        def y0_loads(sp):
            for r in range(2):
                sp.wait_ge(g_sc[r], 64 * (NGR // 2))
            for b in range(B):
                if b >= 2:
                    sp.wait_ge(s_yu, b - 1)
                sp.dma_start(yl[b % 2], y_v[:, 0, b * T:(b + 1) * T, :]).then_inc(s_yl[b % 2], 16)

        start_views()
        W2 = 2 * W
        XP = W + S
        NP_ = NB // 2
        c_xT = [view(XP) for _ in range(2)]
        c_kz = view(G * XP).rearrange("p (g n) -> p g n", g=G)
        c_q = mix0[:, 0:NB * P].rearrange("p (n h q) -> p n h q", n=NB, h=G)
        c_gq = view(S)
        c_gk = view(LH * NL).rearrange("p (h n) -> p h n", h=LH)
        c_v = view(NP_ * G * 2 * (W + 1)).rearrange("p (j g b e) -> p j g b e", j=NP_, g=G, b=2)
        c_gv = view(LH * (HD + 1)).rearrange("p (j b e) -> p j b e", j=LH // 2, b=2)
        c_tl = view(S)
        c_tr = view(S)
        c_lg = view(S)
        c_sx = [view(512) for _ in range(2)]
        c_p = [view(512) for _ in range(3)]
        c_pT = [view(512) for _ in range(2)]
        c_z = [view(HB * P).rearrange("p (n g c) -> p n g c", n=HB, g=G) for _ in range(2)]
        c_rem = view(T * LAT).rearrange("p (t c) -> p t c", t=T)
        c_rT = view(S, parts=LAT)
        c_cb = view(S)
        c_xp = view(2 * NL).rearrange("p (b n) -> p b n", b=2)
        c_mx = view(8)
        c_rs = view(8)
        c_rm = view(8 * G).rearrange("p (n h) -> p n h", n=8)
        order = [n // 4 * 4 + (0, 2, 1, 3)[n % 4] for n in range(HB)]
        U = 12

        def pair(u):
            return [u // 4 * HB + order[u % 4 * 2 + k] for k in range(2)]

        ACC = ["S0", "V1", "S1", "GQ", "S2", "S3", "GV", "S4", "S5", "remo", "S6", "out", "gl", "S7", "gr", "S8",
               "loc0", "Q", "S9", "K", "S10", "V0", "S11", "loc1"]
        PT = ["T10", "T11", "T0", "GK", "T1", "T2", "remT"] + [f"T{u}" for u in range(3, U - 2)]
        PROJ = ("Q", "K", "V0")
        TAIL = ("T10", "T11", "remT", "remo", "out")

        c_vr = [sem(f"c_vr{n}") for n in range(3)]

        def use_counts(period, banks):
            seq = [(n, 0) for n in period if n in PROJ]
            for b in range(B):
                for n in period:
                    owner = b + (1 if n in PROJ else -1 if n in TAIL else 0)
                    if 0 <= owner < B:
                        seq.append((n, owner))
            seq += [(n, B - 1) for n in period if n in TAIL]
            seen, table = [0] * banks, {}
            for n, owner in seq:
                k = period.index(n) % banks
                seen[k] += 1
                table[n, owner] = seen[k]
            return table

        acc_uses, pt_uses = use_counts(ACC, 4), use_counts(PT, 2)

        c_rdy = [sem(f"c_rdy{n}") for n in range(4)]
        c_free = [sem(f"c_free{n}") for n in range(4)]
        c_prdy = [sem(f"c_prdy{n}") for n in range(2)]
        c_pfree = [sem(f"c_pfree{n}") for n in range(2)]
        c_ordy = [sem(f"c_ordy{n}") for n in range(2)]
        c_ofree = [sem(f"c_ofree{n}") for n in range(2)]
        c_ld = [sem(f"c_ld{n}") for n in range(2)]
        (c_init, c_xpr, c_qr, c_gqr, c_gkr, c_tr_, c_sxr, c_pr, c_pTr, c_zr, c_remr, c_rTr, c_cbr) = (
            sem(n) for n in ("c_init c_xpr c_qr c_gqr c_gkr c_tanh c_sxr c_pr c_pTr c_zr c_remr c_rTr "
                             "c_cbr").split())

        def acc(name, bt):
            k = ACC.index(name) % 4
            return psum[:, k, :], c_rdy[k], c_free[k], acc_uses[name, bt[0]] + bt[1] * (2 * len(ACC) // 4)

        def pt_bank(name, bt):
            k = PT.index(name) % 2
            return psum[:, 4 + k, :], c_prdy[k], c_pfree[k], pt_uses[name, bt[0]] + bt[1] * len(PT)

        def o_bank(u, bt):
            return psum[:, 6 + u % 2, :], c_ordy[u % 2], c_ofree[u % 2], batch(bt) * 6 + (u // 2 + 1)

        def attn1_init(g):
            ch = Chain(g, s_pool)
            g.sem_clear(s_pool)
            g.wait_ge(s_phase, 12)
            for a in (c_xT[0], c_xT[1], c_kz[:, 0, :], c_kz[:, 1, :], c_kz[:, 2, :], c_kz[:, 3, :]):
                ch.link(g.memset(a[:, 0:W], 0.0))
            ch.link(g.memset(c_gq[LAT:P, :], 0.0))
            ch.link(g.memset(c_gk[LAT:P, :, :], 0.0))
            ch.link(g.memset(c_v, 0.0))
            ch.link(g.memset(c_v[0:64, :, :, 0, W:W + 1], 1.0))
            ch.link(g.memset(c_v[64:P, :, :, 1, W:W + 1], 1.0))
            ch.link(g.memset(c_gv, 0.0))
            ch.link(g.memset(c_gv[0:64, :, 0, HD:HD + 1], 1.0))
            ch.link(g.memset(c_gv[64:P, :, 1, HD:HD + 1], 1.0))
            g.engine_nop().then_inc(c_init, 1)

        def attn1_loads(sp):
            sp.wait_ge(c_init, 1)
            for b in range(B):
                if b >= 2:
                    _, rdy, _, n = acc("gr", (b - 2, 0))
                    sp.wait_ge(rdy, n)
                    sp.wait_ge(c_xpr, b - 1)
                sp.dma_start(c_xT[b % 2][:, W:XP], xnT_all[:, b * S:(b + 1) * S]).then_inc(c_ld[b % 2], 16)

        def unit_at(s, lag, prev, cur):
            return (s - lag, cur) if s >= lag else (U + s - lag, prev)

        def attn1_pe(pe, prev, cur, nxt):
            def begin(bank):
                o, rdy, free, n = bank
                pe.wait_ge(free, n)
                return o, rdy

            def project(name, bt):
                if not bt:
                    return
                r = bt[0] % 2
                xT = c_xT[r][:, W:XP]
                if name == "Q":
                    pe.wait_ge(c_ld[r], (bt[1] + (bt[0] // 2 + 1)) * 16)
                if name in ("GV", "GK"):
                    pe.wait_ge(c_xpr, batch(bt) + 1)
                o, rdy = begin(pt_bank(name, bt) if name == "GK" else acc(name, bt))
                if name[0] == "V":
                    for j in range(NP_ // 2):
                        first = W * (int(name[1]) * HB + order[2 * j])
                        mm = pe.matmul(o[:, j * C:(j + 1) * C], c_xT[r][:, first:first + 2 * W2], wv1[:, :],
                                       start=True, stop=True)
                elif name == "GV":
                    mm = pe.matmul(o[:, 0:LAT], c_xp.rearrange("p b n -> p (b n)"), wgv[:, :], start=True,
                                   stop=True)
                elif name == "GK":
                    mm = pe.matmul(o[0:LAT, 0:NL], wgk[:, :], c_xp[:, 0, :], start=True, stop=True)
                elif name == "GQ":
                    mm = pe.matmul(o[0:LAT, :], wgq[:, :], xT, start=True, stop=True)
                else:
                    w = dict(Q=wq1[:, :], K=wk1[:, :], gl=wgate[:, 0, :, :].rearrange("p h e -> p (h e)"),
                             gr=wgate[:, 1, :, :].rearrange("p h e -> p (h e)"))[name]
                    mm = pe.matmul(o, w, xT, start=True, stop=True)
                mm.then_inc(rdy, 1)

            def scores(u):
                o, rdy = begin(acc(f"S{u}", cur))
                if u < 8:
                    if u == 0:
                        pe.wait_ge(c_qr, batch(cur) + 1)
                    pe.matmul(o, selq[:, :, :].rearrange("p h q -> p (h q)"),
                              lmask[:, 0 if u == 0 else 1, :, :].rearrange("p k j -> p (k j)").unsqueeze(1)
                              .to_broadcast([P, G, 2 * W2]), start=True, stop=False, skip_group_check=True)
                    ov = o.rearrange("p (g k j) -> p g k j", g=G, k=2)
                    for k in range(2):
                        n = pair(u)[k]
                        mm = pe.matmul(ov[:, :, k, :], c_q[:, n, :, :].rearrange("p h q -> p (h q)"),
                                       c_kz[:, :, n * W:n * W + W2], start=False, stop=(k == 1),
                                       skip_group_check=True)
                else:
                    t = u - 8
                    if t == 0:
                        pe.wait_ge(c_gqr, batch(cur) + 1)
                        pe.wait_ge(c_gkr, batch(cur) + 1)
                    pe.matmul(o, selr[:, :], gmask[:, t, :].unsqueeze(1).to_broadcast([P, LH, NL]), start=True,
                              stop=False)
                    mm = pe.matmul(o, c_gq[:, t * P:(t + 1) * P], c_gk.rearrange("p h n -> p (h n)"), start=False,
                                   stop=True)
                mm.then_inc(rdy, 1)

            def transposes(u, bt):
                if not bt:
                    return
                pe.wait_ge(c_pr, batch(bt) * U + (u + 1))
                o, rdy = begin(pt_bank(f"T{u}", bt))
                for j in range(4):
                    mm = pe.transpose(o[:, j * P:(j + 1) * P], c_p[u % 3][:, j * P:(j + 1) * P], ident[:, :])
                mm.then_inc(rdy, 1)

            def values(u, bt):
                if not bt:
                    return
                pe.wait_ge(c_pTr, batch(bt) * U + (u + 1))
                if u in (0, 4, 8):
                    pe.wait_ge(c_vr[u // 4], batch(bt) + 1)
                o, rdy = begin(o_bank(u, bt))
                for j in range(4):
                    w = c_pT[u % 2][:, j * P:(j + 1) * P]
                    if u < 8:
                        dst = o[:, 0:8 * (W + 1)].rearrange("p (k g e) -> p k g e", k=2, g=G)[:, :, j, :]
                        rhs = c_v[:, u, j, :, :]
                    else:
                        n = 2 * (HD + 1)
                        dst = o[:, j * n:(j + 1) * n]
                        rhs = c_gv[:, j, :, :].rearrange("p b e -> p (b e)")
                    mm = pe.matmul(dst, w, rhs, start=True, stop=True)
                mm.then_inc(rdy, 1)

            def local_out(hf):
                pe.wait_ge(c_zr, batch(cur) * 8 + (4 * hf + 4))
                o, rdy = begin(acc(f"loc{hf}", cur))
                for j in range(HB):
                    mm = pe.matmul(o[:, order[j] * W:(order[j] + 1) * W], c_z[hf][:, j, :, :].rearrange("p g c -> p (g c)"),
                                   pick[:, :], start=True, stop=True)
                mm.then_inc(rdy, 1)

            def tail(name):
                if not prev:
                    return
                if name == "remT":
                    pe.wait_ge(c_remr, batch(prev) + 1)
                    o, rdy = begin(pt_bank("remT", prev))
                    alone(pe)
                    for t in range(T):
                        mm = pe.transpose(o[0:LAT, t * P:(t + 1) * P], c_rem[:, t, :], ident[:, :])
                elif name == "remo":
                    pe.wait_ge(c_rTr, batch(prev) + 1)
                    o, rdy = begin(acc("remo", prev))
                    mm = pe.matmul(o, rout[:, :], c_rT, start=True, stop=True)
                else:
                    pe.wait_ge(c_cbr, batch(prev) + 1)
                    o, rdy = begin(acc("out", prev))
                    for t in range(T):
                        mm = pe.matmul(o[:, t * C:(t + 1) * C], c_cb[:, t * P:(t + 1) * P], wout[:, :],
                                       start=True, stop=True)
                mm.then_inc(rdy, 1)

            if not cur and not prev:
                for name in PROJ:
                    project(name, nxt)
                return
            for s in range(U):
                if cur:
                    scores(s)
                transposes(*unit_at(s, 2, prev, cur))
                values(*unit_at(s, 3, prev, cur))
                if s in (4, 5, 6):
                    tail({4: "remT", 5: "remo", 6: "out"}[s])
                if s == 8 and cur:
                    local_out(0)
                if s == 11 and cur:
                    local_out(1)
                for at_step, name, bt in ((0, "V1", cur), (1, "GQ", cur), (2, "GK", cur), (3, "GV", cur),
                                          (6, "gl", cur), (7, "gr", cur), (8, "Q", nxt), (9, "K", nxt),
                                          (10, "V0", nxt)):
                    if s == at_step:
                        project(name, bt)

        def attn1_act(act, prev, cur, nxt):
            def bank(x):
                o, rdy, free, n = x
                act.wait_ge(rdy, n)
                return o, free

            def queries(heads):
                o, free = bank(acc("Q", nxt))
                for h in heads:
                    ins = act.activation(c_q[:, :, h, :], o.rearrange("p (n q) -> p n q", n=NB), ACT.Copy,
                                         scale=head_m[:, h:h + 1])
                if G - 1 in heads:
                    ins.then_inc(free, 1)

            def keys(groups):
                o, free = bank(acc("K", nxt))
                for g in groups:
                    ins = act.activation(c_kz[:, g, W:XP], o, ACT.Copy, scale=row_m[:, g:g + 1])
                if G - 1 in groups:
                    ins.then_inc(free, 1)
                    act.wait_ge(free, acc("K", nxt)[3] + 1)
                    act.sem_inc(c_qr, 1)

            def gates(name, dst):
                o, free = bank(acc(name, cur))
                act.activation(dst, o, ACT.Tanh, scale=0.5).then_inc(free, 1)
                if name == "gr":
                    act.wait_ge(free, acc("gr", cur)[3] + 1)
                    act.sem_inc(c_tr_, 1)

            def window_values(hf, bt):
                o, free = bank(acc(f"V{hf}", bt))
                ov = o.rearrange("p (j g e) -> p j g e", j=4, g=G)
                for bb in range(2):
                    row = slice(64 * bb, 64 * bb + 64)
                    ins = act.activation(c_v[row, 4 * hf:4 * hf + 4, :, bb, 0:W], ov[row, :, :, :], ACT.Copy)
                ins.then_inc(free, 1)
                act.wait_ge(free, acc(f"V{hf}", bt)[3] + 1)
                act.sem_inc(c_vr[hf], 1)

            def latent_queries():
                o, free = bank(acc("GQ", cur))
                act.activation(c_gq[0:LAT, :], o[0:LAT, :], ACT.Copy).then_inc(free, 1)
                act.wait_ge(free, acc("GQ", cur)[3] + 1)
                act.sem_inc(c_gqr, 1)

            def latent_values():
                o, free = bank(acc("GV", cur))
                ov = o[:, 0:LAT].rearrange("p (j b e) -> p j b e", j=LH // 2, b=2)
                for bb in range(2):
                    row = slice(64 * bb, 64 * bb + 64)
                    ins = act.activation(c_gv[row, :, bb, 0:HD], ov[row, :, bb, :], ACT.Copy)
                ins.then_inc(free, 1)
                act.wait_ge(free, acc("GV", cur)[3] + 1)
                act.sem_inc(c_vr[2], 1)

            def tail():
                o, free = bank(pt_bank("remT", prev))
                act.activation(c_rT, o[0:LAT, :], ACT.Copy).then_inc(free, 1)
                act.wait_ge(free, pt_bank("remT", prev)[3] + 1)
                act.sem_inc(c_rTr, 1)

            if not cur and not prev:
                queries(range(G))
                keys(range(G))
                window_values(0, nxt)
                return
            for s in range(U):
                if cur:
                    act.wait_ge(c_sxr, batch(cur) * U + (s + 1))
                    act.activation(c_p[s % 3], c_sx[s % 2], ACT.Exp).then_inc(c_pr, 1)
                u, bt = unit_at(s, 2, prev, cur)
                if bt:
                    o, free = bank(pt_bank(f"T{u}", bt))
                    act.activation(c_pT[u % 2], o, ACT.Copy).then_inc(free, 1)
                    act.wait_ge(free, pt_bank(f"T{u}", bt)[3] + 1)
                    act.sem_inc(c_pTr, 1)
                if s == 4 and prev:
                    tail()
                if cur:
                    if s == 0:
                        window_values(1, cur)
                    if s == 1:
                        latent_queries()
                    if s == 3:
                        latent_values()
                    if s == 6:
                        gates("gl", c_tl)
                    if s == 7:
                        gates("gr", c_tr)
                if nxt:
                    if s == 8:
                        queries((0, 1, 2))
                    if s == 9:
                        queries((3,))
                        keys((0, 1))
                    if s == 10:
                        keys((2, 3))
                    if s == 11:
                        window_values(0, nxt)

        def attn1_dve(v, prev, cur, nxt):
            ch = Chain(v, s_chain)

            def bank(x):
                o, rdy, free, n = x
                v.wait_ge(rdy, n)
                return o, free

            def pooled():
                r = cur[0] % 2
                v.wait_ge(c_ld[r], (cur[1] + (cur[0] // 2 + 1)) * 16)
                ch.link(v.tensor_reduce(c_xp[:, 0, :], c_xT[r][:, W:XP].rearrange("p (n e) -> p n e", n=NL), AX,
                                        ALU.add))
                v.tensor_copy(c_xp[:, 1, :], c_xp[:, 0, :]).then_inc(c_xpr, 1)

            def latent_keys():
                o, free = bank(pt_bank("GK", cur))
                v.tensor_tensor(c_gk[0:LAT, :, :], o[0:LAT, 0:NL].unsqueeze(1).to_broadcast([LAT, LH, NL]),
                                gk_m[:, 0:LH].unsqueeze(2).to_broadcast([LAT, LH, NL]), ALU.mult).then_inc(free, 1)
                v.wait_ge(free, pt_bank("GK", cur)[3] + 1)
                v.sem_inc(c_gkr, 1)

            def joined():
                o, free = bank(acc("remo", prev))
                v.scalar_tensor_tensor(out=c_cb, in0=c_tr, scalar=1.0, in1=o, op0=ALU.add,
                                       op1=ALU.mult).then_inc(free, 1)
                v.wait_ge(free, acc("remo", prev)[3] + 1)
                v.tensor_tensor(c_cb, c_cb, c_lg, ALU.add).then_inc(c_cbr, 1)

            def onto_stream():
                o, free = bank(acc("out", prev))
                xb = x_all[:, bass.ds(batch(prev) * T, T), :]
                v.tensor_tensor(xb, xb, o.rearrange("p (t c) -> p t c", t=T), ALU.add).then_inc(free, 1)

            def normalise(u, bt):
                if not bt:
                    return
                oo, ofree = bank(o_bank(u, bt))
                e = W if u < 8 else HD
                ov = oo[:, 0:8 * (e + 1)].rearrange("p (n e) -> p n e", n=8)
                ch.link(v.reciprocal(c_rs, ov[:, :, e]))
                if u < 8:
                    ch.link(v.tensor_tensor(c_rm, c_rs.unsqueeze(2).to_broadcast([P, 8, G]),
                                            row_m[:, :].unsqueeze(1).to_broadcast([P, 8, G]), ALU.mult))
                    v.tensor_tensor(c_z[u // 4][:, u % 4 * 2:u % 4 * 2 + 2, :, :]
                                    .rearrange("p k g (h e) -> p (k g) h e", h=G),
                                    ov[:, :, 0:W].rearrange("p n (h e) -> p n h e", h=G),
                                    c_rm.unsqueeze(3).to_broadcast([P, 8, G, HD]), ALU.mult).then_inc(c_zr, 1)
                    v.wait_ge(c_zr, batch(bt) * 8 + (u + 1))
                    v.sem_inc(ofree, 1)
                else:
                    v.tensor_tensor(c_rem[:, u - 8, :].rearrange("p (h e) -> p h e", h=LH), ov[:, :, 0:HD],
                                    c_rs.unsqueeze(2).to_broadcast([P, LH, HD]), ALU.mult).then_inc(ofree, 1)
                    v.wait_ge(ofree, o_bank(u, bt)[3] + 1)

            def gated(hf, bt):
                if hf == 0:
                    v.wait_ge(c_tr_, batch(bt) + 1)
                o, free = bank(acc(f"loc{hf}", bt))
                h2 = slice(hf * S // 2, (hf + 1) * S // 2)
                v.scalar_tensor_tensor(out=c_lg[:, h2], in0=c_tl[:, h2], scalar=1.0,
                                       in1=o[:, 0:S // 2], op0=ALU.add, op1=ALU.mult).then_inc(free, 1)
                v.wait_ge(free, acc(f"loc{hf}", bt)[3] + 1)

            if not cur and not prev:
                return
            for s in range(U):
                if cur:
                    o, free = bank(acc(f"S{s}", cur))
                    sv = o.rearrange("p (n j) -> p n j", n=8)
                    ch.link(v.tensor_reduce(c_mx, sv, AX, ALU.max))
                    if s >= 2:
                        v.wait_ge(c_pr, batch(cur) * U + (s - 1))
                    v.tensor_tensor(c_sx[s % 2].rearrange("p (n j) -> p n j", n=8), sv,
                                    c_mx.unsqueeze(2).to_broadcast([P, 8, W2]), ALU.subtract).then_inc(c_sxr, 1)
                    v.wait_ge(c_sxr, batch(cur) * U + (s + 1))
                    v.sem_inc(free, 1)
                if prev:
                    if s == 0:
                        gated(1, prev)
                    if s == 5:
                        joined()
                    if s == 7:
                        onto_stream()
                if s == 9 and cur:
                    gated(0, cur)
                normalise(*unit_at(s, 3, prev, cur))
                if s == 2 and prev:
                    v.sem_inc(c_remr, 1)
                if cur:
                    if s == 1:
                        pooled()
                    if s == 3:
                        latent_keys()
            alone(v)
            ch.restart()

        def attn1(eng, stage):
            stage(eng, None, None, (0, 0))
            stage(eng, None, (0, 0), (1, 0))
            with eng.Fori(0, B // 2 - 1) as i:
                stage(eng, (0, i), (1, i), (2, i))
                stage(eng, (1, i), (2, i), (3, i))
            stage(eng, (B - 2, 0), (B - 1, 0), None)
            stage(eng, (B - 1, 0), None, None)

        s_ids = sem("s_ids")

        def ids1(g):
            g.wait_ge(s_sc, 16 * NT * 2)
            g.iota(xr_all[:, :, C + 1:C + 2].bitcast(I32), pattern=[[P, NT], [0, 1]], base=NT * P,
                   channel_multiplier=1).then_inc(s_ids, 1)
            g.wait_ge(s_ids, 1)

        start_views()
        Z = 4
        z_y = [view(2 * S).rearrange("p (k t c) -> p k t c", k=2, t=T) for _ in range(Z)]
        z_ld = [sem(f"z_ld{r}") for r in range(Z)]
        z_s = sem("z_s")
        z_x = sem("z_x")

        def last_sp(sp):
            sp.wait_ge(s_phase, 15)
            for r in range(RING):
                sp.wait_ge(f_sc[r], 16 * (NT1 // RING))

            def load(b):
                for k in range(2):
                    sp.dma_start(z_y[b % Z][:, k, :, :], y_v[:, k, b * T:(b + 1) * T, :]).then_inc(z_ld[b % Z], 16)

            for b in range(Z):
                load(b)
            for b in range(B):
                sp.wait_ge(z_x, b + 1)
                if b + Z < B:
                    load(b + Z)
                sp.dma_start(out_v[:, b * T:(b + 1) * T, :], x_all[:, b * T:(b + 1) * T, :]).then_inc(s_out, 16)
            sp.wait_ge(s_out, 16 * B)

        def last_act(act):
            with act.Fori(0, B // Z) as i:
                for r in range(Z):
                    b = i * Z + r
                    act.wait_ge(z_ld[r], (i + 1) * 32)
                    for t in range(T):
                        ins = act.activation(z_y[r][:, 0, t, :], z_y[r][:, 0, t, :], ACT.Copy,
                                             scale=gate[:, 0, bass.ds(b * T + t, 1)])
                    ins.then_inc(z_s, 1)

        def last_dve(v):
            ch = Chain(v, s_chain)
            with v.Fori(0, B // Z) as i:
                for r in range(Z):
                    b = i * Z + r
                    v.wait_ge(z_ld[r], (i + 1) * 32)
                    for t in range(T):
                        n = b * T + t
                        xt = x_all[:, bass.ds(n, 1), :].rearrange("p a c -> p (a c)")
                        ch.after(v.scalar_tensor_tensor(out=xt, in0=z_y[r][:, 1, t, :],
                                                        scalar=gate[:, 1, bass.ds(n, 1)], in1=xt,
                                                        op0=ALU.mult, op1=ALU.add))
                    v.wait_ge(z_s, b + 1)
                    alone(v)
                    ch.sync()
                    xb = x_all[:, bass.ds(b * T, T), :]
                    v.tensor_tensor(xb, xb, z_y[r][:, 0, :, :], ALU.add).then_inc(z_x, 1)
                    ch.restart()

        block = ctx.enter_context(nc.Block())

        @block.sync
        def _(sp):
            setup_loads(sp)
            late_loads(sp)
            sp.wait_ge(s_split, 2)
            for k in range(3):
                sp.dma_start(b3[k:k + 1, :], bparts[:, k, :]).then_inc(s_b3, 16)
            attn0_loads(sp)
            sp.wait_ge(s_phase, 9)
            sp.wait_ge(b_xu, 1 + B)
            y0_loads(sp)
            sp.dma_start(w1, d["L1_ffn_w1"].rearrange("e h f -> h e f")).then_inc(s_w3, 16)
            attn1_loads(sp)
            sp.wait_ge(s_phase, 15)
            sp.wait_ge(s_sc, 16 * NT * 3)
            sp.wait_ge(s_w3, 48)
            ffn_sp(sp)
            last_sp(sp)

        @block.gpsimd
        def _(g):
            setup_pool(g)
            bias_pool(g)
            scatter_pool(g, 0, 0, sorted0)
            states(g, state_pool)
            group_pool(g, (B + 1, 0))
            attn1_init(g)
            scatter_pool(g, 1, 0, sorted1)
            ids1(g)
            scatter_pool(g, 1, 1, sorted1)
            ffn_pool(g)

        @block.scalar
        def _(act):
            phase_end(act, 1)
            norm_act(act, 0)
            phase_end(act, 2)
            routing_act(act, 0)
            two_deep(act, feat_act)
            roots_act(act)
            states(act, state_act)
            group_results(act, (B + 1, 0))
            phase_end(act, 3)
            norm_act(act, 1)
            phase_end(act, 4)
            routing_act(act, 1)
            act.wait_ge(c_init, 1)
            attn1(act, attn1_act)
            phase_end(act, 5)
            ffn_act(act)
            last_act(act)

        @block.vector
        def _(v):
            for s, n in [(s_tp, 2), (s_lg, 2), (s_xT2, 2), (s_cp, 2), (a_uqr, 2), (a_zqr, 2), (a_ukr, 2),
                         (a_nsu, 2), (a_nsq, 1), (a_red, 1), (b_w, 1), (b_xu, 1), (g_yr, 1)] + [
                    (q, 1) for q in c_free + c_pfree + c_ofree]:
                v.sem_inc(s, n)
            setup_dve(v)
            phase_end(v, 1)
            v.wait_ge(s_x, 16 * B)
            norm_dve(v, 0)
            phase_end(v, 2)
            biases_dve(v)
            routing_dve(v, 0)
            layer1_dve(v)
            v.wait_ge(s_bo, 1 + B)
            two_deep(v, feat_dve)
            roots_dve(v)
            states(v, state_dve)
            phase_end(v, 3)
            v.wait_ge(s_sc, 16 * NT)
            v.wait_ge(b_xu, 1 + B)
            norm_dve(v, 1)
            phase_end(v, 4)
            routing_dve(v, 1)
            v.wait_ge(c_init, 1)
            attn1(v, attn1_dve)
            phase_end(v, 5)
            v.wait_ge(s_w3, 48)
            ffn_dve(v)
            last_dve(v)

        @block.tensor
        def _(pe):
            setup_pe(pe)
            phase_end(pe, 1)
            norm_pe(pe, 0)
            phase_end(pe, 2)
            pe.wait_ge(s_const, 3)
            routing_pe(pe, 0)
            pe.wait_ge(s_b3, 48)
            pe.wait_ge(s_rt, 3)
            two_deep(pe, feat_pe)
            pe.wait_ge(s_w2, 16 * N_W2)
            states(pe, state_pe)
            group_pe_products(pe, (B + 1, 0))
            phase_end(pe, 3)
            norm_pe(pe, 1)
            phase_end(pe, 4)
            routing_pe(pe, 1)
            pe.wait_ge(c_init, 1)
            attn1(pe, attn1_pe)
            phase_end(pe, 5)
            pe.wait_ge(s_w3, 48)
            ffn_pe(pe)


_INS = ["L0_attn_x", "L0_attn_Wq", "L0_attn_bq", "L0_attn_Wk", "L0_attn_bk", "L0_attn_Wv", "L0_attn_bv",
        "L0_attn_Wo", "L0_attn_bo", "L0_attn_ln_g", "L0_attn_ln_b", "L0_ffn_router_w", "L0_ffn_router_b",
        "L0_ffn_expert_w", "L0_ffn_expert_b", "L1_attn_wq", "L1_attn_wk", "L1_attn_wv", "L1_attn_wgq",
        "L1_attn_wgk", "L1_attn_wgv", "L1_attn_r_out_w", "L1_attn_gate_local_w", "L1_attn_gate_remote_w",
        "L1_attn_w_out", "L1_ffn_gate_w", "L1_ffn_w1", "L1_ffn_b1", "L1_ffn_w2", "L1_ffn_b2"]


def kernel(**inputs):
    import numpy as np
    import concourse.bacc as bacc
    from concourse.bass_utils import run_bass_kernel_spmd

    nc = bacc.Bacc("TRN2", target_bir_lowering=False, num_devices=1)
    arrays, d = {}, {}
    for name in _INS:
        a = np.ascontiguousarray(inputs[name])
        arrays[f"in_{name}_dram"] = a
        d[name] = nc.dram_tensor(f"in_{name}_dram", a.shape, mybir.dt.from_np(a.dtype), kind="ExternalInput").ap()
    shape = inputs["L0_attn_x"].shape
    rows = shape[0] * shape[1]
    experts = inputs["L0_ffn_router_w"].shape[0]
    out = nc.dram_tensor("out_0_dram", shape, F32, kind="ExternalOutput").ap()
    sorted0 = nc.dram_tensor("sorted0", (rows + experts * P, shape[2] + 2), F32, kind="Internal").ap()
    sorted1 = nc.dram_tensor("sorted1", (2 * rows + experts * P, shape[2] + 2), F32, kind="Internal").ap()
    ydram = nc.dram_tensor("ydram", (2 * rows, shape[2]), F32, kind="Internal").ap()
    build(nc, d, out, sorted0, sorted1, ydram)
    r = run_bass_kernel_spmd(nc, [arrays], core_ids=[0])
    return r.results[0]["out_0_dram"]
```
